# Optimizing a Trainium2 kernel written in Bass

```python
import numpy as np
import jax
import jax.numpy as jnp

def _softmax(x, axis=-1):
    return jax.nn.softmax(x, axis=axis)

def _gelu(x):
    return jax.nn.gelu(x, approximate=True)

def _silu(x):
    return jax.nn.silu(x)

def _sigmoid(x):
    return jax.nn.sigmoid(x)

def _layernorm(x, axis=-1, eps=1e-05):
    m = jnp.mean(x, axis=axis, keepdims=True)
    v = jnp.var(x, axis=axis, keepdims=True)
    return (x - m) / jnp.sqrt(v + eps)

def _scatter_add(tgt, idx, src, axis=0):
    return tgt.at[idx].add(src)

def _segment_sum(src, seg, n):
    return jax.ops.segment_sum(src, seg, n)
kernel_name = 'mk_decoder_postln_d1_seqx_r4_cc5b64'

def setup_inputs(seed: int=0):
    np.random.seed(seed)
    _w = jnp.asarray

    def _rec_inputs():
        import jax
        import jax.numpy as jnp
        _rk = jax.random.key(seed)
        x = -0.0005207 + 1.001 * jax.random.normal(jax.random.fold_in(_rk, 1), (2, 1024, 256), jnp.float32)
        _lenS = 1024 - jax.random.randint(jax.random.fold_in(_rk, 7), (2,), 0, max(1, 1024 // 4) + 1, jnp.int32)
        _lenS2 = 64 - jax.random.randint(jax.random.fold_in(_rk, 8), (2,), 0, max(1, 64 // 4) + 1, jnp.int32)
        _ctx_1024P = jax.random.normal(jax.random.fold_in(_rk, 11), (2, 16, 256), jnp.float32)
        _ctx_1024c = jax.random.dirichlet(jax.random.fold_in(_rk, 511), 0.3 * jnp.ones((16,), jnp.float32), (2, 64))
        _ctx_1024t = jnp.einsum('bsk,bkd->bsd', _ctx_1024c, _ctx_1024P)
        _ctx_1024t = _ctx_1024t * jax.lax.rsqrt(jnp.mean(jnp.square(_ctx_1024t)) + 1e-12) * 0.953939
        ctx_1024 = -1.39393e-06 + 0.999914 * (_ctx_1024t + 0.3 * jax.random.normal(jax.random.fold_in(_rk, 611), (2, 64, 256), jnp.float32))
        itok_BxSx64_0_2047 = jax.random.randint(jax.random.fold_in(_rk, 12), (2, 1024, 64), 0, 512, jnp.int32)
        return (x, ctx_1024, itok_BxSx64_0_2047)
    x, ctx_1024, itok_BxSx64_0_2047 = _rec_inputs()

    def _L0_attn_setup():
        import jax, jax.numpy as jnp
        import numpy as np
        DIM = 256
        HEADS = 16
        KDIM = DIM // 2
        VDIM = DIM
        DK = KDIM // HEADS
        DV = VDIM // HEADS
        LOW = 16
        NORMALIZER = 16.0
        EPS = 1e-05
        B, T = (2, 1024)

        def _gla_scan(q, k, v, gk):
            scale = DK ** (-0.5)

            def step(h, inp):
                qt, kt, vt, gt = inp
                h = h * jnp.exp(gt)[..., None] + kt[..., None] * vt[..., None, :]
                ot = jnp.einsum('bhk,bhkv->bhv', qt * scale, h)
                return (h, ot)
            h0 = jnp.zeros((q.shape[0], HEADS, DK, DV), q.dtype)
            xs = tuple((jnp.moveaxis(a, 1, 0) for a in (q, k, v, gk)))
            _, o = jax.lax.scan(step, h0, xs)
            return jnp.moveaxis(o, 0, 1)
        key = jax.random.key(seed)
        ks = jax.random.split(key, 9)

        def lin(k, sh, fan_in):
            return jax.random.normal(k, sh, jnp.float32) * fan_in ** (-0.5)
        return {'x': jax.random.normal(ks[0], (B, T, DIM), jnp.float32), 'Wq': lin(ks[1], (DIM, KDIM), DIM), 'Wk': lin(ks[2], (DIM, KDIM), DIM), 'Wv': lin(ks[3], (DIM, VDIM), DIM), 'Wgk1': lin(ks[4], (DIM, LOW), DIM), 'Wgk2': lin(ks[5], (LOW, KDIM), LOW), 'bgk2': jnp.zeros((KDIM,), jnp.float32), 'Wg': lin(ks[6], (DIM, VDIM), DIM), 'gnw': jnp.ones((DV,), jnp.float32), 'Wo': lin(ks[7], (VDIM, DIM), VDIM)}
    _L0_attn_all = _L0_attn_setup()
    _L0_attn_in = {k: v for k, v in _L0_attn_all.items() if k in ('Wq', 'Wk', 'Wv', 'Wgk1', 'Wgk2', 'bgk2', 'Wg', 'gnw', 'Wo')}
    del _L0_attn_all

    def _L0_xattn_setup():
        import jax, jax.numpy as jnp
        import numpy as np
        B, NQ, NKV, K = (2, 256, 512, 64)
        D, H, LAT = (256, 16, 128)
        HD = D // H
        SCALE = 1.0 / np.sqrt(HD)
        key = jax.random.key(seed)
        ks = jax.random.split(key, 7)
        s = lambda fan_in: 1.0 / np.sqrt(fan_in)
        return {'x_q': jax.random.normal(ks[0], (B, NQ, D), jnp.float32), 'x_kv': jax.random.normal(ks[1], (B, NKV, D), jnp.float32), 'indices': jax.random.randint(ks[2], (B, NQ, K), 0, NKV), 'W_q': jax.random.normal(ks[3], (D, D), jnp.float32) * s(D), 'W_kv_down': jax.random.normal(ks[4], (LAT, D), jnp.float32) * s(D), 'W_kv_up': jax.random.normal(ks[5], (2 * D, LAT), jnp.float32) * s(LAT), 'W_out': jax.random.normal(ks[6], (D, D), jnp.float32) * s(D)}
    _L0_xattn_all = _L0_xattn_setup()
    _L0_xattn_in = {k: v for k, v in _L0_xattn_all.items() if k in ('W_q', 'W_kv_down', 'W_kv_up', 'W_out')}
    del _L0_xattn_all

    def _L0_ffn_setup():
        import jax, jax.numpy as jnp
        import numpy as np
        EPS = 1e-05
        N_HEADS = 16
        TOP_K = 2

        def _ln(x, g, b):
            m = x.mean(-1, keepdims=True)
            v = ((x - m) ** 2).mean(-1, keepdims=True)
            return (x - m) / jnp.sqrt(v + EPS) * g + b

        def _block_fwd(x, ln1_g, ln1_b, ln2_g, ln2_b, Wq, bq, Wk, bk, Wv, bv, Wo, bo, Wr, br, e_w1, e_b1, e_w2, e_b2):
            B, S, D = x.shape
            H = N_HEADS
            hd = D // H
            h = _ln(x, ln1_g, ln1_b)
            q = (h @ Wq + bq).reshape(B, S, H, hd).transpose(0, 2, 1, 3)
            k = (h @ Wk + bk).reshape(B, S, H, hd).transpose(0, 2, 1, 3)
            v = (h @ Wv + bv).reshape(B, S, H, hd).transpose(0, 2, 1, 3)
            scores = jnp.einsum('bhqd,bhkd->bhqk', q, k) / hd ** 0.5
            causal = jnp.tril(jnp.ones((S, S), dtype=bool))
            scores = jnp.where(causal, scores, -jnp.inf)
            attn = jax.nn.softmax(scores, axis=-1)
            o = jnp.einsum('bhqk,bhkd->bhqd', attn, v).transpose(0, 2, 1, 3).reshape(B, S, D)
            a = o @ Wo + bo + x
            h2 = _ln(a, ln2_g, ln2_b)
            logits = h2 @ Wr + br
            topv = jax.lax.top_k(logits, TOP_K)[0]
            kmask = logits >= topv[..., -1:]
            w = jax.nn.softmax(jnp.where(kmask, logits, -jnp.inf), axis=-1)
            mid = jax.nn.gelu(jnp.einsum('bsd,edf->bsef', h2, e_w1) + e_b1, approximate=False)
            eo = jnp.einsum('bsef,efd->bsed', mid, e_w2) + e_b2
            moe = jnp.einsum('bse,bsed->bsd', w, eo)
            return moe + a
        key = jax.random.key(seed)
        B, S, D, E = (1, 512, 256, 8)
        F = 4 * D
        ks = jax.random.split(key, 8)

        def n(k, shape):
            return jax.random.normal(k, shape, jnp.float32) * 0.02
        return dict(x=jax.random.normal(ks[0], (B, S, D), jnp.float32), ln1_g=jnp.ones((D,), jnp.float32), ln1_b=jnp.zeros((D,), jnp.float32), ln2_g=jnp.ones((D,), jnp.float32), ln2_b=jnp.zeros((D,), jnp.float32), Wq=n(ks[1], (D, D)), bq=jnp.zeros((D,), jnp.float32), Wk=n(ks[2], (D, D)), bk=jnp.zeros((D,), jnp.float32), Wv=n(ks[3], (D, D)), bv=jnp.zeros((D,), jnp.float32), Wo=n(ks[4], (D, D)), bo=jnp.zeros((D,), jnp.float32), Wr=n(ks[5], (D, E)), br=jnp.zeros((E,), jnp.float32), e_w1=n(ks[6], (E, D, F)), e_b1=jnp.zeros((E, F), jnp.float32), e_w2=n(ks[7], (E, F, D)), e_b2=jnp.zeros((E, D), jnp.float32))
    _L0_ffn_all = _L0_ffn_setup()
    _L0_ffn_in = {k: v for k, v in _L0_ffn_all.items() if k in ('ln1_g', 'ln1_b', 'ln2_g', 'ln2_b', 'Wq', 'bq', 'Wk', 'bk', 'Wv', 'bv', 'Wo', 'bo', 'Wr', 'br', 'e_w1', 'e_b1', 'e_w2', 'e_b2')}
    del _L0_ffn_all
    return {'x': x, 'ctx_1024': ctx_1024, 'itok_BxSx64_0_2047': itok_BxSx64_0_2047, 'L0_attn_Wq': _L0_attn_in['Wq'], 'L0_attn_Wk': _L0_attn_in['Wk'], 'L0_attn_Wv': _L0_attn_in['Wv'], 'L0_attn_Wgk1': _L0_attn_in['Wgk1'], 'L0_attn_Wgk2': _L0_attn_in['Wgk2'], 'L0_attn_bgk2': _L0_attn_in['bgk2'], 'L0_attn_Wg': _L0_attn_in['Wg'], 'L0_attn_gnw': _L0_attn_in['gnw'], 'L0_attn_Wo': _L0_attn_in['Wo'], 'L0_xattn_W_q': _L0_xattn_in['W_q'], 'L0_xattn_W_kv_down': _L0_xattn_in['W_kv_down'], 'L0_xattn_W_kv_up': _L0_xattn_in['W_kv_up'], 'L0_xattn_W_out': _L0_xattn_in['W_out'], 'L0_ffn_ln1_g': _L0_ffn_in['ln1_g'], 'L0_ffn_ln1_b': _L0_ffn_in['ln1_b'], 'L0_ffn_ln2_g': _L0_ffn_in['ln2_g'], 'L0_ffn_ln2_b': _L0_ffn_in['ln2_b'], 'L0_ffn_Wq': _L0_ffn_in['Wq'], 'L0_ffn_bq': _L0_ffn_in['bq'], 'L0_ffn_Wk': _L0_ffn_in['Wk'], 'L0_ffn_bk': _L0_ffn_in['bk'], 'L0_ffn_Wv': _L0_ffn_in['Wv'], 'L0_ffn_bv': _L0_ffn_in['bv'], 'L0_ffn_Wo': _L0_ffn_in['Wo'], 'L0_ffn_bo': _L0_ffn_in['bo'], 'L0_ffn_Wr': _L0_ffn_in['Wr'], 'L0_ffn_br': _L0_ffn_in['br'], 'L0_ffn_e_w1': _L0_ffn_in['e_w1'], 'L0_ffn_e_b1': _L0_ffn_in['e_b1'], 'L0_ffn_e_w2': _L0_ffn_in['e_w2'], 'L0_ffn_e_b2': _L0_ffn_in['e_b2']}

def reference(x, ctx_1024, itok_BxSx64_0_2047, L0_attn_Wq, L0_attn_Wk, L0_attn_Wv, L0_attn_Wgk1, L0_attn_Wgk2, L0_attn_bgk2, L0_attn_Wg, L0_attn_gnw, L0_attn_Wo, L0_xattn_W_q, L0_xattn_W_kv_down, L0_xattn_W_kv_up, L0_xattn_W_out, L0_ffn_ln1_g, L0_ffn_ln1_b, L0_ffn_ln2_g, L0_ffn_ln2_b, L0_ffn_Wq, L0_ffn_bq, L0_ffn_Wk, L0_ffn_bk, L0_ffn_Wv, L0_ffn_bv, L0_ffn_Wo, L0_ffn_bo, L0_ffn_Wr, L0_ffn_br, L0_ffn_e_w1, L0_ffn_e_b1, L0_ffn_e_w2, L0_ffn_e_b2):
    import jax
    import jax.numpy as jnp

    def _L0_attn_ref(x, Wq, Wk, Wv, Wgk1, Wgk2, bgk2, Wg, gnw, Wo):
        import jax, jax.numpy as jnp
        import numpy as np
        DIM = 256
        HEADS = 16
        KDIM = DIM // 2
        VDIM = DIM
        DK = KDIM // HEADS
        DV = VDIM // HEADS
        LOW = 16
        NORMALIZER = 16.0
        EPS = 1e-05
        B, T = (2, 1024)

        def _gla_scan(q, k, v, gk):
            scale = DK ** (-0.5)

            def step(h, inp):
                qt, kt, vt, gt = inp
                h = h * jnp.exp(gt)[..., None] + kt[..., None] * vt[..., None, :]
                ot = jnp.einsum('bhk,bhkv->bhv', qt * scale, h)
                return (h, ot)
            h0 = jnp.zeros((q.shape[0], HEADS, DK, DV), q.dtype)
            xs = tuple((jnp.moveaxis(a, 1, 0) for a in (q, k, v, gk)))
            _, o = jax.lax.scan(step, h0, xs)
            return jnp.moveaxis(o, 0, 1)
        Bx, Tx, _ = x.shape
        q = (x @ Wq).reshape(Bx, Tx, HEADS, DK)
        k = (x @ Wk).reshape(Bx, Tx, HEADS, DK)
        v = (x @ Wv).reshape(Bx, Tx, HEADS, DV)
        gk = jax.nn.log_sigmoid(x @ Wgk1 @ Wgk2 + bgk2)
        gk = gk.reshape(Bx, Tx, HEADS, DK) / NORMALIZER
        o = _gla_scan(q, k, v, gk)
        g = (x @ Wg).reshape(Bx, Tx, HEADS, DV)
        o = o * jax.lax.rsqrt(jnp.mean(o * o, axis=-1, keepdims=True) + EPS) * gnw
        o = o * (g * jax.nn.sigmoid(g))
        return o.reshape(Bx, Tx, VDIM) @ Wo

    def _L0_xattn_ref(x_q, x_kv, indices, W_q, W_kv_down, W_kv_up, W_out):
        import jax, jax.numpy as jnp
        import numpy as np
        B, NQ, NKV, K = (2, 256, 512, 64)
        D, H, LAT = (256, 16, 128)
        HD = D // H
        SCALE = 1.0 / np.sqrt(HD)
        b, nq, d = x_q.shape
        q = (x_q @ W_q.T).reshape(b, nq, H, HD)
        c_kv = x_kv @ W_kv_down.T
        c_sel = c_kv[jnp.arange(b)[:, None, None], indices]
        kv = (c_sel @ W_kv_up.T).reshape(b, nq, K, 2, H, HD)
        k = kv[:, :, :, 0]
        v = kv[:, :, :, 1]
        scores = jnp.einsum('bqhd,bqkhd->bqkh', q, k) * SCALE
        attn = jax.nn.softmax(scores, axis=2)
        out = jnp.einsum('bqkh,bqkhd->bqhd', attn, v).reshape(b, nq, d)
        return out @ W_out.T

    def _L0_ffn_ref(x, ln1_g, ln1_b, ln2_g, ln2_b, Wq, bq, Wk, bk, Wv, bv, Wo, bo, Wr, br, e_w1, e_b1, e_w2, e_b2):
        import jax, jax.numpy as jnp
        import numpy as np
        EPS = 1e-05
        N_HEADS = 16
        TOP_K = 2

        def _ln(x, g, b):
            m = x.mean(-1, keepdims=True)
            v = ((x - m) ** 2).mean(-1, keepdims=True)
            return (x - m) / jnp.sqrt(v + EPS) * g + b

        def _block_fwd(x, ln1_g, ln1_b, ln2_g, ln2_b, Wq, bq, Wk, bk, Wv, bv, Wo, bo, Wr, br, e_w1, e_b1, e_w2, e_b2):
            B, S, D = x.shape
            H = N_HEADS
            hd = D // H
            h = _ln(x, ln1_g, ln1_b)
            q = (h @ Wq + bq).reshape(B, S, H, hd).transpose(0, 2, 1, 3)
            k = (h @ Wk + bk).reshape(B, S, H, hd).transpose(0, 2, 1, 3)
            v = (h @ Wv + bv).reshape(B, S, H, hd).transpose(0, 2, 1, 3)
            scores = jnp.einsum('bhqd,bhkd->bhqk', q, k) / hd ** 0.5
            causal = jnp.tril(jnp.ones((S, S), dtype=bool))
            scores = jnp.where(causal, scores, -jnp.inf)
            attn = jax.nn.softmax(scores, axis=-1)
            o = jnp.einsum('bhqk,bhkd->bhqd', attn, v).transpose(0, 2, 1, 3).reshape(B, S, D)
            a = o @ Wo + bo + x
            h2 = _ln(a, ln2_g, ln2_b)
            logits = h2 @ Wr + br
            topv = jax.lax.top_k(logits, TOP_K)[0]
            kmask = logits >= topv[..., -1:]
            w = jax.nn.softmax(jnp.where(kmask, logits, -jnp.inf), axis=-1)
            mid = jax.nn.gelu(jnp.einsum('bsd,edf->bsef', h2, e_w1) + e_b1, approximate=False)
            eo = jnp.einsum('bsef,efd->bsed', mid, e_w2) + e_b2
            moe = jnp.einsum('bse,bsed->bsd', w, eo)
            return moe + a
        return _block_fwd(x, ln1_g, ln1_b, ln2_g, ln2_b, Wq, bq, Wk, bk, Wv, bv, Wo, bo, Wr, br, e_w1, e_b1, e_w2, e_b2)
    x = _layernorm(x + _L0_attn_ref(x, L0_attn_Wq, L0_attn_Wk, L0_attn_Wv, L0_attn_Wgk1, L0_attn_Wgk2, L0_attn_bgk2, L0_attn_Wg, L0_attn_gnw, L0_attn_Wo), axis=-1)
    x = _layernorm(x + _L0_xattn_ref(x, ctx_1024, itok_BxSx64_0_2047, L0_xattn_W_q, L0_xattn_W_kv_down, L0_xattn_W_kv_up, L0_xattn_W_out), axis=-1)
    x = _layernorm(x + _L0_ffn_ref(x, L0_ffn_ln1_g, L0_ffn_ln1_b, L0_ffn_ln2_g, L0_ffn_ln2_b, L0_ffn_Wq, L0_ffn_bq, L0_ffn_Wk, L0_ffn_bk, L0_ffn_Wv, L0_ffn_bv, L0_ffn_Wo, L0_ffn_bo, L0_ffn_Wr, L0_ffn_br, L0_ffn_e_w1, L0_ffn_e_b1, L0_ffn_e_w2, L0_ffn_e_b2), axis=-1)
    return x

_drawn_inputs = setup_inputs


def setup_inputs(seed=0):
    import zlib

    import numpy as np

    out = dict(_drawn_inputs(seed))
    spreads = {'L0_attn_bgk2': (0.0, 0.443),
     'L0_attn_gnw': (1.0, 0.2),
     'L0_ffn_ln1_g': (1.0, 0.6),
     'L0_ffn_ln1_b': (0.0, 0.8),
     'L0_ffn_ln2_g': (1.0, 0.593),
     'L0_ffn_ln2_b': (0.0, 0.47),
     'L0_ffn_bq': (0.0, 0.8),
     'L0_ffn_bk': (0.0, 0.8),
     'L0_ffn_bv': (0.0, 0.494),
     'L0_ffn_bo': (0.0, 0.1),
     'L0_ffn_br': (0.0, 0.1),
     'L0_ffn_e_b1': (0.0, 0.618),
     'L0_ffn_e_b2': (0.0, 0.1)}
    factors = {'L0_ffn_Wq': 8.0, 'L0_ffn_Wk': 8.0}
    for name, (base, spread) in spreads.items():
        noise = np.random.default_rng([zlib.crc32(name.encode()), seed]).standard_normal(out[name].shape)
        drawn = base * np.exp(spread * noise) if base else spread * noise
        out[name] = jnp.asarray(drawn.astype(out[name].dtype))
    for name, factor in factors.items():
        out[name] = (out[name] * factor).astype(out[name].dtype)
    return out
```

```python
from contextlib import ExitStack

import concourse.bass as bass
from concourse import mybir

F32 = mybir.dt.float32
F32R = mybir.dt.float32r
BF16 = mybir.dt.bfloat16
I32 = mybir.dt.int32
ALU = mybir.AluOpType
ACT = mybir.ActivationFunctionType
AX = mybir.AxisListType

P = 128
B = 2
T = 1024
N = B * T
D = 256
KD = D // P
H = 16
HD = D // H
DK = 8
LOW = 16
NT = N // P
BLK = 512
NB = N // BLK
TB = BLK // P
NCTX = 64
NSEL = 64
LAT = 128
E = 8
FF = 4 * D
NF = FF // P
EPS = 1e-5
MASKED = -1e30
HG = P // HD


class Steps:

    def __init__(self, sem, names, before=()):
        self.sem, self.names, self.before = sem, list(names), ["start", *before]
        assert len(set(self.names)) == len(self.names)

    def value(self, name, i=0):
        if name in self.before:
            return self.before.index(name) + 1
        return len(self.before) + i * len(self.names) + self.names.index(name) + 1

    def start(self, eng):
        eng.sem_inc(self.sem, 1)

    def done(self, instruction, name):
        instruction.then_inc(self.sem, 1)

    def wait_apart(self, eng, name, i, apart):
        self.wait(eng, name, i)
        eng.sem_inc(apart, 1)

    def wait(self, eng, name, i=0):
        eng.wait_ge(self.sem, self.value(name, i))

    def wait_before(self, eng, i):
        eng.wait_ge(self.sem, len(self.before) + i * len(self.names))


class Kernel:
    def __init__(self, nc, a, out):
        self.nc, self.a, self.out = nc, a, out
        self.top = ExitStack()
        self.n_sem = 0

    def sb(self, ctx, name, shape, dt=F32):
        return ctx.enter_context(self.nc.sbuf_tensor(name, shape, dt))

    def sem(self, name):
        return self.top.enter_context(self.nc.semaphore(name))

    def steps(self, name, names, before=()):
        return Steps(self.sem(name), names, before)

    def build(self, upto=99):
        nc = self.nc
        with self.top:
            nc.scalar.preload_act_table_set('natural_log_exp_and_others') if 0 else None
            self.PS = self.top.enter_context(nc.psum_tensor("PS", [P, 8, BLK], F32))
            self.X = self.sb(self.top, "X", [P, NT, D])
            self.ident = self.sb(self.top, "ident", [P, P])
            self.apart = self.sem("apart")
            with ExitStack() as c:
                self.gla_setup(c)
                self.gla_gates(c)
                self.gla_scan(c)
                self.gla_out(c)
            if upto >= 2:
                with ExitStack() as c:
                    self.cross_setup(c)
                    self.cross_blocks(c)
            if upto >= 3:
                self.self_attention()
            if upto >= 4:
                with ExitStack() as c:
                    self.experts(c)
            self.store()

    def store(self):
        s_out = self.sem("s_out")
        with self.nc.Block() as block:
            @block.sync
            def _(e):
                e.dma_start(self.out.rearrange("b (t p) d -> p (b t) d", p=P), self.X[:, :, :]).then_inc(s_out, 16)
                e.wait_ge(s_out, 16)


    def transposes(self, pe, src, blk, banks):
        for kt in range(KD):
            for t in range(TB):
                last = pe.transpose(self.PS[:, banks[kt], t * P:(t + 1) * P],
                                    src[:, TB * blk + t, kt * P:(kt + 1) * P], self.ident[:, :])
        return last

    def token_major(self, pe, srcT, w, banks, start=True, stop=True):
        for t in range(TB):
            for kt in range(KD):
                last = pe.matmul(self.PS[:, banks[t // 2], (t % 2) * D:(t % 2 + 1) * D],
                                 srcT[:, kt, t * P:(t + 1) * P], w[:, kt, :], start=kt == 0, stop=kt == KD - 1)
        return last

    def pair_banks(self, b0):
        return self.PS[:, b0:b0 + 2, :].rearrange("p b (t d) -> p (b t) d", t=2)

    def norm_stats(self, dve, V, i, y, st, mv, tag="stats"):
        for t in range(TB):
            last = dve.bn_stats(st[:, t, :], y[:, t, :])
        V.done(last, tag)
        V.wait_apart(dve, tag, i, self.apart)
        for t in range(TB):
            last = dve.bn_aggr(mv[:, t, :], st[:, t, :])
        V.done(last, tag + "_mv")

    def norm_rstd(self, act, A, V, i, mv, lv, rstd, tag="stats", out="rstd"):
        V.wait(act, tag + "_mv", i)
        A.done(act.activation(lv[:, :], mv[:, :, 1], ACT.Ln, bias=self.eps[:, 0:1]), out + "_ln")
        A.wait(act, out + "_ln", i)
        A.done(act.activation(rstd[:, :], lv[:, :], ACT.Exp, scale=-0.5), out)


    def gla_setup(self, c):
        nc, a, PS, X, ident = self.nc, self.a, self.PS, self.X, self.ident
        sb = lambda n, s, dt=F32: self.sb(c, n, s, dt)
        self.eps = self.sb(self.top, "eps", [P, 1])
        self.XT = XT = sb("XT", [P, KD, N])
        self.Wq, self.Wk = sb("Wq", [P, KD, P]), sb("Wk", [P, KD, P])
        self.Wgk1, self.Wgk2 = sb("Wgk1", [P, KD, LOW]), sb("Wgk2", [LOW, P])
        self.bgk2 = sb("bgk2", [P, 1])
        Wv, Wg, self.Wo = sb("Wv", [P, KD, D]), sb("Wg", [P, KD, D]), sb("Wo", [P, KD, D])
        gnw = sb("gnw", [P, HD])
        self.G = G = sb("G", [P, NT, D])
        self.WvB = WvB = sb("WvB", [P, KD, HD, H, DK])
        self.headsum = R = sb("headsum", [P, 32])
        s_x, s_w = self.sem("g_x"), self.sem("g_w")
        loads = [(self.Wq, "L0_attn_Wq"), (self.Wk, "L0_attn_Wk"), (self.Wgk1, "L0_attn_Wgk1"), (Wv, "L0_attn_Wv"),
                 (Wg, "L0_attn_Wg"), (self.Wo, "L0_attn_Wo")]
        n_w = 16 * (len(loads) + 3)
        C = self.steps("g_c", ["zero", "zeror", "eps", "ident", "r1", "r2"])
        S = self.steps("g_pe", [n for k in range(NB) for n in (f"t{k}", f"g{k}")])
        V = self.steps("g_dve", [n for k in range(NB) for n in (f"x0{k}",)] + ["wv0", "wv1"] + [f"gn{k}" for k in range(NB)])
        A = self.steps("g_act", [n for k in range(NB) for n in (f"x1{k}", f"silu{k}")])
        with nc.Block() as block:
            @block.sync
            def _(e):
                for k in range(NB):
                    e.dma_start(X[:, k * TB:(k + 1) * TB, :],
                                a["x"].rearrange("b (t p) d -> p (b t) d", p=P)[:, k * TB:(k + 1) * TB, :]).then_inc(s_x, 16)
                    e.wait_ge(s_x, 16 * (k + 1))
            @block.gpsimd
            def _(e):
                for t, w in loads:
                    e.dma_start(t[:, :, :], a[w].rearrange("(k p) n -> p k n", p=P)).then_inc(s_w, 16)
                e.dma_start(self.Wgk2[:, :], a["L0_attn_Wgk2"]).then_inc(s_w, 16)
                e.dma_start(self.bgk2[:, :], a["L0_attn_bgk2"].rearrange("(p o) -> p o", o=1)).then_inc(s_w, 16)
                e.dma_start(gnw[:, :], a["L0_attn_gnw"].partition_broadcast(P)).then_inc(s_w, 16)
                C.start(e)
                C.done(e.memset(ident[:, :], 0.0), "zero")
                C.done(e.memset(R[:, :], 1.0), "zeror")
                C.done(e.memset(self.eps[:, :], EPS), "eps")
                C.wait(e, "zeror")
                C.done(e.affine_select(out=ident[:, :], in_=ident[:, :], compare_op=ALU.not_equal, fill=1.0, base=0,
                                       pattern=[[-1, P]], channel_multiplier=1), "ident")
                C.done(e.affine_select(out=R[:, :], in_=R[:, :], compare_op=ALU.is_ge, fill=0.0, base=0,
                                       pattern=[[-DK, 32]], channel_multiplier=1), "r1")
                C.wait(e, "r1")
                C.done(e.affine_select(out=R[:, :], in_=R[:, :], compare_op=ALU.is_ge, fill=0.0, base=DK - 1,
                                       pattern=[[DK, 32]], channel_multiplier=-1), "r2")
            @block.tensor
            def _(e):
                S.start(e)
                C.wait(e, "ident")
                for k in range(NB):
                    e.wait_ge(s_x, 16 * (k + 1))
                    if k >= 2:
                        V.wait(e, f"x0{k - 2}")
                        A.wait(e, f"x1{k - 2}")
                    S.done(self.transposes(e, X, k, (2 * (k % 2), 2 * (k % 2) + 1)), f"t{k}")
                    e.wait_ge(s_w, n_w)
                    V.wait(e, f"x0{k}")
                    A.wait(e, f"x1{k}")
                    if k >= 2:
                        A.wait(e, f"silu{k - 2}")
                    S.done(self.token_major(e, XT[:, :, k * BLK:(k + 1) * BLK], Wg, (4 + 2 * (k % 2), 5 + 2 * (k % 2))), f"g{k}")
            @block.vector
            def _(e):
                V.start(e)
                for k in range(NB):
                    S.wait(e, f"t{k}")
                    V.done(e.tensor_copy(XT[:, 0, k * BLK:(k + 1) * BLK], PS[:, 2 * (k % 2), :]), f"x0{k}")
                for kt in range(KD):
                    e.wait_ge(s_w, n_w)
                    V.done(e.tensor_copy(WvB[:, kt, :, :, :],
                                         Wv[:, kt, :].rearrange("p (h j) -> p j h", j=HD).unsqueeze(3).broadcast_to((P, HD, H, DK))),
                           f"wv{kt}")
                for k in range(NB):
                    A.wait(e, f"silu{k}")
                    g = G[:, k * TB:(k + 1) * TB, :].rearrange("p t (h j) -> p (t h) j", j=HD)
                    V.done(e.tensor_tensor(g, g, gnw[:, :].unsqueeze(1).broadcast_to((P, TB * H, HD)), ALU.mult), f"gn{k}")
            @block.scalar
            def _(e):
                A.start(e)
                for k in range(NB):
                    S.wait(e, f"t{k}")
                    A.done(e.activation(XT[:, 1, k * BLK:(k + 1) * BLK], PS[:, 2 * (k % 2) + 1, :], ACT.Copy), f"x1{k}")
                    S.wait(e, f"g{k}")
                    A.done(e.activation(G[:, k * TB:(k + 1) * TB, :], self.pair_banks(4 + 2 * (k % 2)), ACT.Silu), f"silu{k}")

    def gla_gates(self, c):
        nc, PS, XT = self.nc, self.PS, self.XT
        sb = lambda n, s, dt=F32: self.sb(c, n, s, dt)
        self.QT, self.KT, self.decay = sb("QT", [P, N]), sb("KT", [P, N]), sb("decay", [P, N])
        lowT, z, az, lz, u = sb("lowT", [LOW, BLK]), sb("z", [P, BLK]), sb("az", [P, BLK]), sb("lz", [P, BLK]), sb("u", [P, BLK])
        S = self.steps("gg_pe", ["low", "q", "k", "z"])
        A = self.steps("gg_act", ["low", "z", "abs", "q", "exp", "ln", "decay"])
        V = self.steps("gg_dve", ["k", "u"])
        with nc.Block() as block:
            @block.tensor
            def _(e):
                S.start(e)
                with e.Fori(0, NB) as i:
                    x = lambda kt: XT[:, kt, bass.ds(i * BLK, BLK)]
                    A.wait_before(e, i)
                    V.wait_before(e, i)
                    for name, w, bank, m in (("low", self.Wgk1, 0, LOW), ("q", self.Wq, 1, P), ("k", self.Wk, 2, P)):
                        for kt in range(KD):
                            last = e.matmul(PS[0:m, bank, :], w[:, kt, :], x(kt), start=kt == 0, stop=kt == KD - 1)
                        S.done(last, name)
                    A.wait(e, "low", i)
                    S.done(e.matmul(PS[:, 3, :], self.Wgk2[:, :], lowT[:, :], start=True, stop=True), "z")
            @block.scalar
            def _(e):
                A.start(e)
                with e.Fori(0, NB) as i:
                    cols = bass.ds(i * BLK, BLK)
                    S.wait(e, "low", i)
                    A.done(e.activation(lowT[:, :], PS[0:LOW, 0, :], ACT.Copy), "low")
                    S.wait(e, "z", i)
                    A.done(e.activation(z[:, :], PS[:, 3, :], ACT.Identity, bias=self.bgk2[:, 0:1]), "z")
                    A.wait(e, "z", i)
                    A.done(e.activation(az[:, :], z[:, :], ACT.Abs), "abs")
                    A.done(e.activation(self.QT[:, cols], PS[:, 1, :], ACT.Copy, scale=DK ** -0.5), "q")
                    A.wait(e, "abs", i)
                    A.done(e.activation(az[:, :], az[:, :], ACT.Exp, scale=-1.0), "exp")
                    A.wait(e, "exp", i)
                    A.done(e.activation(lz[:, :], az[:, :], ACT.Ln, bias=1.0), "ln")
                    V.wait(e, "u", i)
                    A.done(e.activation(self.decay[:, cols], u[:, :], ACT.Exp, scale=1.0 / 16.0), "decay")
            @block.vector
            def _(e):
                V.start(e)
                with e.Fori(0, NB) as i:
                    S.wait(e, "k", i)
                    V.done(e.tensor_copy(self.KT[:, bass.ds(i * BLK, BLK)], PS[:, 2, :]), "k")
                    A.wait(e, "ln", i)
                    V.done(e.scalar_tensor_tensor(out=u[:, :], in0=z[:, :], scalar=0.0, in1=lz[:, :], op0=ALU.min,
                                                  op1=ALU.subtract), "u")

    def gla_scan(self, c):
        nc, PS, XT = self.nc, self.PS, self.XT
        sb = lambda n, s, dt=F32: self.sb(c, n, s, dt)
        self.O = O = sb("O", [P, NT, D])
        with ExitStack() as c2:
            sb2 = lambda n, s, dt=F32: self.sb(c2, n, s, dt)
            kv, hs = sb2("kv", [P, 2, T]), sb2("hs", [P, 2, T])
            qh = sb2("qh", [P, 8, T])
            OT = sb2("OT", [P, 4, T])
            TBt = T // P
            S = self.steps("gs_pe", self.scan_pe_order())
            V = self.steps("gs_dve", [n for j in range(HD) for n in (f"kv{j}", f"h{j}", f"qh{j}")])
            A = self.steps("gs_act", [f"o{g}" for g in range(4)] + [f"tok{t}" for t in range(TBt)])
            with nc.Block() as block:
                @block.tensor
                def _(e):
                    S.start(e)
                    with e.Fori(0, B) as i:
                        def values(j):
                            if j >= 2:
                                V.wait(e, f"kv{j - 2}", i)
                            for half in range(2):
                                for kt in range(KD):
                                    last = e.matmul(PS[:, 2 * (j % 2) + half, :],
                                                    self.WvB[:, kt, j, :, :].rearrange("p h k -> p (h k)"),
                                                    XT[:, kt, bass.ds(i * T + half * BLK, BLK)], start=kt == 0, stop=kt == KD - 1)
                            S.done(last, f"v{j}")
                        def sums(g):
                            V.wait(e, f"qh{4 * g + 3}", i)
                            if g:
                                A.wait(e, f"o{g - 1}", i)
                            for half in range(2):
                                for r in range(4):
                                    last = e.matmul(PS[32 * r:32 * r + 32, 4 + half, :], self.headsum[:, :],
                                                    qh[:, 4 * (g % 2) + r, half * BLK:(half + 1) * BLK], start=True, stop=True)
                            S.done(last, f"s{g}")
                        def turn(t):
                            A.wait(e, "o3", i)
                            if t >= 2:
                                A.wait(e, f"tok{t - 2}", i)
                            for g in range(4):
                                last = e.transpose(PS[:, 6 + t % 2, g * P:(g + 1) * P], OT[:, g, t * P:(t + 1) * P], self.ident[:, :])
                            S.done(last, f"t{t}")
                        for name in self.scan_pe_order():
                            {"v": values, "s": sums, "t": turn}[name[0]](int(name[1:]))
                @block.vector
                def _(e):
                    V.start(e)
                    with e.Fori(0, B) as i:
                        cols = bass.ds(i * T, T)
                        for j in range(HD):
                            S.wait(e, f"v{j}", i)
                            if j >= 2:
                                V.wait(e, f"h{j - 2}", i)
                            V.done(e.tensor_tensor(kv[:, j % 2, :], PS[:, 2 * (j % 2):2 * (j % 2) + 2, :].rearrange("p b n -> p (b n)"),
                                                   self.KT[:, cols], ALU.mult), f"kv{j}")
                            V.wait(e, f"kv{j}", i)
                            V.done(e.tensor_tensor_scan(hs[:, j % 2, :], self.decay[:, cols], kv[:, j % 2, :], 0.0,
                                                        ALU.mult, ALU.add), f"h{j}")
                            V.wait(e, f"h{j}", i)
                            if j >= 8:
                                S.wait(e, f"s{j // 4 - 2}", i)
                            V.done(e.tensor_tensor(qh[:, j % 8, :], hs[:, j % 2, :], self.QT[:, cols], ALU.mult), f"qh{j}")
                @block.scalar
                def _(e):
                    A.start(e)
                    with e.Fori(0, B) as i:
                        for g in range(4):
                            S.wait(e, f"s{g}", i)
                            A.done(e.activation(OT[:, g, :], PS[:, 4:6, :].rearrange("p b n -> p (b n)"), ACT.Copy), f"o{g}")
                        for t in range(TBt):
                            S.wait(e, f"t{t}", i)
                            A.done(e.activation(O[:, i * TBt + t, :].rearrange("p (h j) -> p h j", j=HD),
                                                PS[:, 6 + t % 2, :].rearrange("p (j h) -> p h j", h=32)[:, 0:H, :], ACT.Copy), f"tok{t}")

    def scan_pe_order(self):
        order = ["v0", "v1"]
        for j in range(HD):
            if j % 4 == 3:
                order.append(f"s{j // 4}")
            if j + 2 < HD:
                order.append(f"v{j + 2}")
        return order + [f"t{t}" for t in range(T // P)]

    def gla_out(self, c):
        nc, PS, X, O, G = self.nc, self.PS, self.X, self.O, self.G
        sb = lambda n, s, dt=F32: self.sb(c, n, s, dt)
        og, ogT, y = sb("og", [P, TB, D]), sb("ogT", [P, KD, BLK]), sb("y", [P, TB, D])
        ms, lm, rs = sb("ms", [P, TB * H]), sb("lm", [P, TB * H]), sb("rs", [P, TB * H])
        st, mv, lv, rstd = sb("st", [P, TB, 6]), sb("mv", [P, TB, 2]), sb("lv", [P, TB]), sb("rstd", [P, TB])
        S = self.steps("go_pe", ["turn", "wo"])
        A = self.steps("go_act", ["sq", "lnms", "rs", "ogT1", "rstd_ln", "rstd"])
        V = self.steps("go_dve", ["ms", "norm", "gate", "ogT0", "y", "stats", "stats_mv", "out"])
        with nc.Block() as block:
            @block.tensor
            def _(e):
                S.start(e)
                with e.Fori(0, NB) as i:
                    V.wait(e, "gate", i)
                    S.done(self.transposes(e, og, 0, (0, 1)), "turn")
                    V.wait(e, "ogT0", i)
                    A.wait(e, "ogT1", i)
                    S.done(self.token_major(e, ogT, self.Wo, (2, 3)), "wo")
            @block.scalar
            def _(e):
                A.start(e)
                with e.Fori(0, NB) as i:
                    S.wait_before(e, i)
                    A.done(e.activation(og[:, :, :], O[:, bass.ds(i * TB, TB), :], ACT.Square), "sq")
                    V.wait(e, "ms", i)
                    A.done(e.activation(lm[:, :], ms[:, :], ACT.Ln, scale=1.0 / HD, bias=self.eps[:, 0:1]), "lnms")
                    A.wait(e, "lnms", i)
                    A.done(e.activation(rs[:, :], lm[:, :], ACT.Exp, scale=-0.5), "rs")
                    S.wait(e, "turn", i)
                    A.done(e.activation(ogT[:, 1, :], PS[:, 1, :], ACT.Copy), "ogT1")
                    self.norm_rstd(e, A, V, i, mv, lv, rstd)
            @block.vector
            def _(e):
                V.start(e)
                with e.Fori(0, NB) as i:
                    tiles = bass.ds(i * TB, TB)
                    byhead = lambda x: x.rearrange("p t (h j) -> p (t h) j", j=HD)
                    A.wait(e, "sq", i)
                    V.done(e.tensor_reduce(ms[:, :], byhead(og[:, :, :]), AX.X, ALU.add), "ms")
                    A.wait(e, "rs", i)
                    V.done(e.tensor_tensor(byhead(og[:, :, :]), byhead(O[:, tiles, :]),
                                           rs[:, :].unsqueeze(2).broadcast_to((P, TB * H, HD)), ALU.mult), "norm")
                    V.wait(e, "norm", i)
                    V.done(e.tensor_tensor(og[:, :, :], og[:, :, :], G[:, tiles, :], ALU.mult), "gate")
                    S.wait(e, "turn", i)
                    V.done(e.tensor_copy(ogT[:, 0, :], PS[:, 0, :]), "ogT0")
                    S.wait(e, "wo", i)
                    V.done(e.tensor_tensor(y[:, :, :], self.pair_banks(2), X[:, tiles, :], ALU.add), "y")
                    V.wait(e, "y", i)
                    self.norm_stats(e, V, i, y, st, mv)
                    A.wait(e, "rstd", i)
                    for t in range(TB):
                        last = e.tensor_scalar(X[:, i * TB + t, :], y[:, t, :], mv[:, t, 0:1], rstd[:, t:t + 1],
                                               ALU.subtract, ALU.mult)
                    V.done(last, "out")


    def cross_setup(self, c):
        nc, a, PS = self.nc, self.a, self.PS
        sb = lambda n, s, dt=F32: self.sb(c, n, s, dt)
        self.WqT, self.WoutT = WqT, WoutT = sb("c_WqT", [P, KD, D]), sb("c_WoutT", [P, KD, D])
        self.Kblk = Kblk = sb("c_Kblk", [P, B, KD, HG, NCTX])
        self.Vblk = Vblk = sb("c_Vblk", [P, B, H // 2, 2, HD])
        self.half = half = sb("c_half", [P, 2, HD])
        self.selaug = selaug = sb("c_selaug", [P, H // 2, 2, NCTX])
        self.L = L = sb("c_L", [P, B, T // P, NCTX])
        with ExitStack() as c2:
            sb2 = lambda n, s, dt=F32: self.sb(c2, n, s, dt)
            wq, wout, up, down = sb2("c_wq", [P, KD, D]), sb2("c_wout", [P, KD, D]), sb2("c_up", [P, 4, LAT]), sb2("c_down", [P, 1, D])
            ctx, upT, downT, ctxT = sb2("c_ctx", [P, 1, D]), sb2("c_upT", [P, 1, 4 * P]), sb2("c_downT", [P, KD, P]), sb2("c_ctxT", [P, KD, P])
            ckv, ckv2 = sb2("c_ckv", [P, P]), sb2("c_ckv2", [P, B, 2, NCTX])
            m16 = sb2("c_m16", [P, HG])
            idx = sb2("c_idx", [P, T // P, B, NSEL], I32)
            f, f2 = sb2("c_f", [P, T // P, B * NSEL]), sb2("c_f2", [P, T // P, B * NSEL])
            idxT = sb2("c_idxT", [P, T], BF16)
            cid = sb2("c_cid", [P, NCTX])
            win = sb2("c_win", [P, 3 * P], BF16)
            hot = sb2("c_hot", [P, 4, T], BF16)
            cntT = sb2("c_cntT", [P, T])
            s_i, s_w = self.sem("c_i"), self.sem("c_w")
            pools = ["z1", "z2", "z3", "z4", "z5", "cid", "m16a", "half_a", "w1", "sa1", "m16b", "half_b", "w2", "sa2"]
            C = self.steps("cs_pool", pools)
            turned = [("wq", wq, WqT, 2, 2), ("wout", wout, WoutT, 2, 2), ("up", up, upT, 4, 1), ("down", down, downT, 1, 2), ("ctx", ctx, ctxT, 1, 2)]
            S = self.steps("cs_pe", [n for n, *_ in turned] + ["ckv", "k", "v0", "v1", "idx"])
            A = self.steps("cs_act", [n for n, *_ in turned] + ["v0", "v1"])
            V = self.steps("cs_dve", ["neg", "wrap", "clamp", "ckv", "ckv2", "k", "idxT", "vb0", "vb1"])
            with nc.Block() as block:
                @block.sync
                def _(e):
                    for b in range(B):
                        e.dma_start(idx[:, :, b, :], a["itok_BxSx64_0_2047"][b].rearrange("(t p) k -> p t k", p=P)).then_inc(s_i, 16)
                        e.wait_ge(s_i, 16 * (b + 1))
                @block.gpsimd
                def _(e):
                    C.start(e)
                    for t, w in ((wq, "L0_xattn_W_q"), (wout, "L0_xattn_W_out"), (up, "L0_xattn_W_kv_up"), (down, "L0_xattn_W_kv_down")):
                        e.dma_start(t[:, :, :], a[w].rearrange("(k p) n -> p k n", p=P)).then_inc(s_w, 16)
                    e.dma_start(ctx[:, 0, :], a["ctx_1024"].rearrange("b c d -> (b c) d")).then_inc(s_w, 16)
                    C.done(e.memset(m16[:, :], 1.0), "z1")
                    C.done(e.memset(half[:, :, :], 1.0), "z2")
                    C.done(e.memset(win[:, :], 0.0), "z3")
                    C.done(e.memset(selaug[:, :, :, :], 0.0), "z4")
                    C.done(e.memset(cid[:, :], 0.0), "z5")
                    C.wait(e, "z5")
                    C.done(e.iota(cid[:, :], pattern=[[-1, NCTX]], base=NCTX - 1, channel_multiplier=0, allow_small_or_imprecise_dtypes=True), "cid")
                    sel = lambda t, op, fill, base, pattern, cm: e.affine_select(out=t, in_=t, compare_op=op, fill=fill, base=base,
                                                                                 pattern=pattern, channel_multiplier=cm)
                    C.done(sel(m16[:, :], ALU.is_ge, 0.0, 0, [[-HD, HG]], 1), "m16a")
                    C.done(sel(half[:, :, :], ALU.is_ge, 0.0, 0, [[-NCTX, 2], [0, HD]], 1), "half_a")
                    C.wait(e, "half_a")
                    C.done(sel(win[0:NCTX, :], ALU.not_equal, 1.0, -(P - 1), [[1, 3 * P]], 0), "w1")
                    C.wait(e, "w1")
                    C.done(sel(selaug[:, :, :, :], ALU.not_equal, 1.0, 0, [[0, H // 2], [0, 2], [-1, NCTX]], 1), "sa1")
                    C.wait(e, "sa1")
                    C.done(sel(m16[:, :], ALU.is_ge, 0.0, HD - 1, [[HD, HG]], -1), "m16b")
                    C.done(sel(half[:, :, :], ALU.is_ge, 0.0, NCTX - 1, [[NCTX, 2], [0, HD]], -1), "half_b")
                    C.wait(e, "half_b")
                    C.done(sel(win[NCTX:P, :], ALU.not_equal, 1.0, -(P - 1 + NCTX), [[1, 3 * P]], 0), "w2")
                    C.wait(e, "w2")
                    C.done(sel(selaug[:, :, :, :], ALU.not_equal, 1.0, -NCTX, [[-2, H // 2], [-1, 2], [0, NCTX]], 1), "sa2")
                @block.tensor
                def _(e):
                    S.start(e)
                    e.wait_ge(s_w, 16 * 5)
                    for n, (name, src, dst, rows, cols) in enumerate(turned):
                        if n >= 2:
                            A.wait(e, turned[n - 2][0])
                        for k in range(cols):
                            for r in range(rows):
                                last = e.transpose(PS[:, 2 * (n % 2) + (k * rows + r) // 4, ((k * rows + r) % 4) * P:((k * rows + r) % 4 + 1) * P],
                                                   src[:, r, k * P:(k + 1) * P], self.ident[:, :])
                        S.done(last, name)
                    A.wait(e, "ctx")
                    for kt in range(KD):
                        last = e.matmul(PS[:, 4, 0:P], downT[:, kt, :], ctxT[:, kt, :], start=kt == 0, stop=kt == KD - 1)
                    S.done(last, "ckv")
                    V.wait(e, "ckv")
                    for g in range(KD):
                        last = e.matmul(PS[:, 5, g * P:(g + 1) * P], upT[:, 0, g * P:(g + 1) * P], ckv[:, :], start=True, stop=True)
                    S.done(last, "k")
                    V.wait(e, "ckv2")
                    for b in range(B):
                        S.done(e.matmul(PS[:, 6 + b, 0:D], ckv2[:, b, :, :].rearrange("p a c -> p (a c)"), upT[:, 0, D:2 * D],
                                        start=True, stop=True), f"v{b}")
                    V.wait(e, "clamp")
                    for t in range(T // P):
                        last = e.transpose(PS[:, t // 4, (t % 4) * P:(t % 4 + 1) * P], f[:, t, :], self.ident[:, :])
                    S.done(last, "idx")
                @block.scalar
                def _(e):
                    A.start(e)
                    for n, (name, src, dst, rows, cols) in enumerate(turned):
                        S.wait(e, name)
                        A.done(e.activation(dst[:, :, :].rearrange("p k n -> p (k n)"), PS[:, 2 * (n % 2), 0:rows * cols * P], ACT.Copy), name)
                    for b in range(B):
                        S.wait(e, f"v{b}")
                        C.wait(e, "half_b")
                        A.done(e.activation(Vblk[:, b, :, :, :].rearrange("p a c d -> p (a c d)"), PS[:, 6 + b, 0:D], ACT.Copy), f"v{b}")
                @block.vector
                def _(e):
                    V.start(e)
                    e.wait_ge(s_i, 16 * B)
                    idx_ = idx[:, :, :, :].rearrange("p t b k -> p t (b k)")
                    V.done(e.tensor_scalar(f2[:, :, :], idx_, 0.0, float(NCTX), ALU.is_lt, ALU.mult), "neg")
                    V.wait(e, "neg")
                    V.done(e.tensor_tensor(f[:, :, :], f2[:, :, :], idx_, ALU.add), "wrap")
                    V.wait(e, "wrap")
                    V.done(e.tensor_scalar(f[:, :, :], f[:, :, :], 0.0, float(NCTX - 1), ALU.max, ALU.min), "clamp")
                    C.wait(e, "sa2")
                    S.wait(e, "ckv")
                    V.done(e.tensor_copy(ckv[:, :], PS[:, 4, 0:P]), "ckv")
                    V.wait(e, "ckv")
                    V.done(e.tensor_copy(ckv2[:, :, :, :], ckv[:, :].rearrange("p (b c) -> p b c", b=B).unsqueeze(2).broadcast_to((P, B, 2, NCTX))), "ckv2")
                    S.wait(e, "k")
                    for b in range(B):
                        for g in range(KD):
                            last = e.tensor_tensor(Kblk[:, b, g, :, :],
                                                   PS[:, 5, g * P + b * NCTX:g * P + (b + 1) * NCTX].unsqueeze(1).broadcast_to((P, HG, NCTX)),
                                                   m16[:, :].unsqueeze(2).broadcast_to((P, HG, NCTX)), ALU.mult)
                    V.done(last, "k")
                    S.wait(e, "idx")
                    V.done(e.tensor_copy(idxT[:, :], PS[:, 0:2, :].rearrange("p b n -> p (b n)")), "idxT")
                    for b in range(B):
                        A.wait(e, f"v{b}")
                        V.done(e.tensor_tensor(Vblk[:, b, :, :, :].rearrange("p a c d -> p a (c d)"), Vblk[:, b, :, :, :].rearrange("p a c d -> p a (c d)"),
                                               half[:, :, :].rearrange("p c d -> p (c d)").unsqueeze(1).broadcast_to((P, H // 2, 2 * HD)), ALU.mult), f"vb{b}")
            self.cross_counts(cid, idxT, hot, win, cntT)

    def cross_counts(self, cid, idxT, hot, win, cntT):
        nc, PS, L = self.nc, self.PS, self.L
        R = 4
        S = self.steps("cc_pe", [f"c{r}" for r in range(R)], before=["zero"])
        S2 = self.steps("cc_pe2", ["turn"])
        V = self.steps("cc_dve", [f"hot{r}" for r in range(R)])
        V2 = self.steps("cc_dve2", ["cnt", "least", "none", "L"])
        A2 = self.steps("cc_act2", ["ln"])
        with ExitStack() as c3:
            lc, none = self.sb(c3, "c_lc", [P, T // P, P]), self.sb(c3, "c_none", [P, T // P, P])
            with nc.Block() as block:
                @block.vector
                def _(e):
                    V.start(e)
                    V2.start(e)
                    with e.Fori(0, NCTX // R) as i:
                        for r in range(R):
                            S.wait_before(e, i)
                            V.done(e.tensor_scalar(hot[:, r, :], idxT[:, :], cid[:, bass.ds(i * R + r, 1)], None, ALU.is_equal), f"hot{r}")
                    S.wait(e, f"c{R - 1}", NCTX // R - 1)
                    V2.done(e.tensor_copy(cntT[:, :], PS[:, 0:2, :].rearrange("p b n -> p (b n)")), "cnt")
                    S2.wait(e, "turn")
                    cnt = PS[:, 2:4, :].rearrange("p b (t n) -> p (b t) n", n=P)
                    V2.done(e.tensor_scalar(lc[:, :, :], cnt, 1.0, None, ALU.max), "least")
                    V2.done(e.tensor_scalar(none[:, :, :], cnt, 1.0, 1.0, ALU.min, ALU.subtract), "none")
                    A2.wait(e, "ln")
                    V2.wait(e, "none")
                    for b in range(B):
                        last = e.scalar_tensor_tensor(out=L[:, b, :, :], in0=none[:, :, b * NCTX:(b + 1) * NCTX], scalar=-MASKED,
                                                      in1=lc[:, :, b * NCTX:(b + 1) * NCTX], op0=ALU.mult, op1=ALU.add)
                    V2.done(last, "L")
                @block.scalar
                def _(e):
                    A2.start(e)
                    V2.wait(e, "least")
                    V2.wait(e, "none")
                    A2.done(e.activation(lc[:, :, :], lc[:, :, :], ACT.Ln), "ln")
                @block.tensor
                def _(e):
                    S.start(e)
                    S2.start(e)
                    for b in range(2):
                        last = e.matmul(PS[:, b, :], win[:, 2 * P:3 * P], idxT[:, b * BLK:(b + 1) * BLK], start=True, stop=False, skip_group_check=True)
                    S.done(last, "zero")
                    with e.Fori(0, NCTX // R) as i:
                        for r in range(R):
                            V.wait(e, f"hot{r}", i)
                            for b in range(2):
                                last = e.matmul(PS[:, b, :], win[:, bass.ds(i * R + r + P - NCTX, P)], hot[:, r, b * BLK:(b + 1) * BLK],
                                                start=False, stop=False, skip_group_check=True)
                            S.done(last, f"c{r}")
                    V2.wait(e, "cnt")
                    for t in range(T // P):
                        last = e.transpose(PS[:, 2 + t // 4, (t % 4) * P:(t % 4 + 1) * P], cntT[:, t * P:(t + 1) * P], self.ident[:, :])
                    S2.done(last, "turn")

    def cross_blocks(self, c):
        nc, PS, X, L = self.nc, self.PS, self.X, self.L
        sb = lambda n, s, dt=F32: self.sb(c, n, s, dt)
        xs, xT, qT = sb("xs", [P, TB, D]), sb("xT", [P, KD, BLK]), sb("qT", [P, KD, BLK])
        aug, augT = sb("aug", [P, TB, P]), sb("augT", [P, BLK])
        pr = sb("pr", [P, H // 2, BLK])
        rs, oT, y = sb("c_rs", [P, KD, BLK]), sb("c_oT", [P, KD, BLK]), sb("c_y", [P, TB, D])
        st, mv, lv, rstd = sb("c_st", [P, TB, 6]), sb("c_mv", [P, TB, 2]), sb("c_lv", [P, TB]), sb("c_rstd", [P, TB])
        NP_ = H // 2
        for b in range(B):
            s_z = self.sem(f"cb_z{b}")
            S = self.steps(f"cb_pe{b}", ["turn", "q"] + [f"s{t}" for t in range(TB)] + ["aug"] + [f"e{k}" for k in range(4)] + ["pv0"]
                           + [f"e{k}" for k in range(4, 8)] + ["pv1", "wo"])
            A = self.steps(f"cb_act{b}", ["xs", "xT1", "q1", "augT"] + [f"p{k}" for k in range(4)] + ["ls0", "rs0"]
                           + [f"p{k}" for k in range(4, 8)] + ["ls1", "rs1", "rstd_ln", "rstd"])
            V = self.steps(f"cb_dve{b}", ["L", "xT0", "q0"] + [f"m{t}" for t in range(TB)] + ["o0", "o1", "y", "stats", "stats_mv", "out"])
            with nc.Block() as block:
                @block.gpsimd
                def _(e):
                    e.memset(aug[:, :, NCTX + H:P], 0.0).then_inc(s_z, 1)
                @block.tensor
                def _(e):
                    S.start(e)
                    with e.Fori(0, T // BLK) as i:
                        A.wait(e, "xs", i)
                        V.wait_before(e, i)
                        S.done(self.transposes(e, xs, 0, (0, 1)), "turn")
                        V.wait(e, "xT0", i)
                        A.wait(e, "xT1", i)
                        for g in range(KD):
                            for kt in range(KD):
                                last = e.matmul(PS[:, 2 + g, :], self.WqT[:, kt, g * P:(g + 1) * P], xT[:, kt, :], start=kt == 0, stop=kt == KD - 1)
                        S.done(last, "q")
                        V.wait(e, "q0", i)
                        A.wait(e, "q1", i)
                        for t in range(TB):
                            if t >= 2:
                                V.wait(e, f"m{t - 2}", i)
                            for g in range(KD):
                                bank = PS[:, 4 + 2 * (t % 2) + g, :]
                                e.matmul(bank, qT[:, g, t * P:(t + 1) * P], self.Kblk[:, b, g, :, :].rearrange("p h c -> p (h c)"), start=True, stop=False)
                                last = e.matmul(bank, self.ident[:, :], aug[:, t, 0:NCTX].unsqueeze(1).broadcast_to((P, HG, NCTX)), start=False, stop=True)
                            S.done(last, f"s{t}")
                        V.wait(e, f"m{TB - 1}", i)
                        e.wait_ge(s_z, 1)
                        for t in range(TB):
                            last = e.transpose(PS[:, 0, t * P:(t + 1) * P], aug[:, t, :], self.ident[:, :])
                        S.done(last, "aug")
                        A.wait(e, "augT", i)
                        for k in range(NP_):
                            if k >= 4:
                                A.wait(e, f"p{k - 4}", i)
                            g = k // 4
                            e.matmul(PS[:, 4 + k % 4, :], self.Kblk[:, b, g, 2 * (k % 4):2 * (k % 4) + 2, :].rearrange("p h c -> p (h c)"),
                                     qT[:, g, :], start=True, stop=False)
                            S.done(e.matmul(PS[:, 4 + k % 4, :], self.selaug[:, k, :, :].rearrange("p h c -> p (h c)"), augT[:, :],
                                            start=False, stop=True), f"e{k}")
                            if k % 4 == 3:
                                A.wait(e, f"p{k}", i)
                                for r in range(4):
                                    e.matmul(PS[32 * r:32 * r + 32, g, :], self.Vblk[:, b, 4 * g + r, :, :].rearrange("p h d -> p (h d)"),
                                             pr[:, 4 * g + r, :], start=True, stop=True)
                                for r in range(4):
                                    last = e.matmul(PS[32 * r:32 * r + 32, 2 + g, :], self.half[:, :, :].rearrange("p h d -> p (h d)"),
                                                    pr[:, 4 * g + r, :], start=True, stop=True)
                                S.done(last, f"pv{g}")
                        V.wait(e, "o1", i)
                        S.done(self.token_major(e, oT, self.WoutT, (4, 5)), "wo")
                @block.scalar
                def _(e):
                    A.start(e)
                    with e.Fori(0, T // BLK) as i:
                        S.wait_before(e, i)
                        A.done(e.activation(xs[:, :, :], X[:, bass.ds(b * (T // P) + i * TB, TB), :], ACT.Copy), "xs")
                        S.wait(e, "turn", i)
                        A.done(e.activation(xT[:, 1, :], PS[:, 1, :], ACT.Copy), "xT1")
                        S.wait(e, "q", i)
                        A.done(e.activation(qT[:, 1, :], PS[:, 3, :], ACT.Copy, scale=HD ** -0.5), "q1")
                        S.wait(e, "aug", i)
                        A.done(e.activation(augT[:, :], PS[:, 0, :], ACT.Copy), "augT")
                        for k in range(NP_):
                            S.wait(e, f"e{k}", i)
                            A.done(e.activation(pr[:, k, :], PS[:, 4 + k % 4, :], ACT.Exp), f"p{k}")
                            if k % 4 == 3:
                                g = k // 4
                                S.wait(e, f"pv{g}", i)
                                A.done(e.activation(rs[:, g, :], PS[:, 2 + g, :], ACT.Ln), f"ls{g}")
                                A.wait(e, f"ls{g}", i)
                                A.done(e.activation(rs[:, g, :], rs[:, g, :], ACT.Exp, scale=-1.0), f"rs{g}")
                        self.norm_rstd(e, A, V, i, mv, lv, rstd)
                @block.vector
                def _(e):
                    V.start(e)
                    with e.Fori(0, T // BLK) as i:
                        S.wait_before(e, i)
                        V.done(e.tensor_copy(aug[:, :, 0:NCTX], L[:, b, bass.ds(i * TB, TB), :]), "L")
                        S.wait(e, "turn", i)
                        V.done(e.tensor_copy(xT[:, 0, :], PS[:, 0, :]), "xT0")
                        S.wait(e, "q", i)
                        V.done(e.tensor_scalar(qT[:, 0, :], PS[:, 2, :], HD ** -0.5, None, ALU.mult), "q0")
                        for t in range(TB):
                            S.wait(e, f"s{t}", i)
                            V.done(e.tensor_reduce(aug[:, t, NCTX:NCTX + H], PS[:, 4 + 2 * (t % 2):6 + 2 * (t % 2), :].rearrange("p b (h c) -> p (b h) c", c=NCTX),
                                                   AX.X, ALU.max, negate=True), f"m{t}")
                        for g in range(KD):
                            A.wait(e, f"rs{g}", i)
                            V.done(e.tensor_tensor(oT[:, g, :], PS[:, g, :], rs[:, g, :], ALU.mult), f"o{g}")
                        S.wait(e, "wo", i)
                        tile0 = b * (T // P) + i * TB
                        V.done(e.tensor_tensor(y[:, :, :], self.pair_banks(4), X[:, bass.ds(tile0, TB), :], ALU.add), "y")
                        V.wait(e, "y", i)
                        self.norm_stats(e, V, i, y, st, mv)
                        A.wait(e, "rstd", i)
                        for t in range(TB):
                            last = e.tensor_scalar(X[:, tile0 + t, :], y[:, t, :], mv[:, t, 0:1], rstd[:, t:t + 1], ALU.subtract, ALU.mult)
                        V.done(last, "out")


    def row_norm_affine(self, e, V, A, i, src, dst, st, mv, rstd, gain, bias, tag):
        A.wait(e, "rstd", i)
        for t in range(TB):
            last = e.tensor_scalar(dst[:, t, :], src[:, t, :], mv[:, t, 0:1], rstd[:, t:t + 1], ALU.subtract, ALU.mult)
        V.done(last, tag + "_n")
        V.wait(e, tag + "_n", i)
        V.done(e.tensor_tensor(dst[:, :, :], dst[:, :, :], gain[:, :].unsqueeze(1).broadcast_to((P, TB, D)), ALU.mult), tag + "_g")
        V.wait(e, tag + "_g", i)
        V.done(e.tensor_tensor(dst[:, :, :], dst[:, :, :], bias[:, :].unsqueeze(1).broadcast_to((P, TB, D)), ALU.add), tag)

    def self_attention(self):
        nc = self.nc
        self.parts = nc.dram_tensor("qk_parts", (4, B * D, T), F32).ap()
        self.zero_rows = nc.dram_tensor("zero_rows", (HD, 2, T), F32).ap()
        self.w_all = self.sb(self.top, "w_all", [P, NT, E])
        with ExitStack() as c2:
            sb = lambda n, s, dt=F32: self.sb(c2, n, s, dt)
            self.V = sb("V", [P, NT, H, 2 * HD])
            with ExitStack() as c3:
                self.qkv(c3)
            self.OT = sb("OT_all", [P, B * H // 4, T])
            with ExitStack() as c3:
                self.attend(c3)
            with ExitStack() as c3:
                self.route(c3)

    def qkv(self, c):
        nc, a, PS, X, V_ = self.nc, self.a, self.PS, self.X, self.V
        sb = lambda n, s, dt=F32: self.sb(c, n, s, dt)
        Wq, Wk, Wv = sb("f_Wq", [P, KD, D]), sb("f_Wk", [P, KD, D]), sb("f_Wv", [P, KD, D])
        g1, b1, bv = sb("f_g1", [P, D]), sb("f_b1", [P, D]), sb("f_bv", [P, D])
        bq, bk, bqs = sb("f_bq", [P, KD]), sb("f_bk", [P, KD]), sb("f_bqs", [P, KD])
        h, hT = sb("f_h", [P, TB, D]), sb("f_hT", [P, KD, BLK])
        qf, kf = sb("f_q", [P, KD, BLK]), sb("f_k", [P, KD, BLK])
        part = [sb(n, [P, KD, BLK], F32R) for n in ("f_qhi", "f_qlo", "f_khi", "f_klo")]
        st, mv, lv, rstd = sb("f_st", [P, TB, 6]), sb("f_mv", [P, TB, 2]), sb("f_lv", [P, TB]), sb("f_rstd", [P, TB])
        zr = sb("f_zr", [HD, 2, T], F32R)
        s_w, s_st, s_z, s_zd, s_b = self.sem("f_w"), self.sem("f_store"), self.sem("f_z"), self.sem("f_zd"), self.sem("f_b")
        S = self.steps("f_pe", ["turn", "q", "k", "v"])
        A = self.steps("f_act", ["rstd_ln", "rstd", "hT1", "q", "k"])
        V = self.steps("f_dve", ["stats", "stats_mv", "h_n", "h_g", "h", "hT0", "qhi", "qlo", "khi", "klo", "v"])
        n_w = 16 * 8
        with nc.Block() as block:
            @block.gpsimd
            def _(e):
                for t, w in ((Wq, "Wq"), (Wk, "Wk"), (Wv, "Wv")):
                    e.dma_start(t[:, :, :], a["L0_ffn_" + w].rearrange("(k p) n -> p k n", p=P)).then_inc(s_w, 16)
                for t, w in ((g1, "ln1_g"), (b1, "ln1_b"), (bv, "bv")):
                    e.dma_start(t[:, :], a["L0_ffn_" + w].partition_broadcast(P)).then_inc(s_w, 16)
                for t, w in ((bq, "bq"), (bk, "bk")):
                    e.dma_start(t[:, :], a["L0_ffn_" + w].rearrange("(k p) -> p k", p=P), allow_slow_non_contiguous=True).then_inc(s_w, 16)
                e.memset(V_[:, :, :, HD:2 * HD], 1.0).then_inc(s_z, 1)
                e.memset(zr[:, :, :].bitcast(F32), 0.0).then_inc(s_z, 1)
                e.wait_ge(s_z, 2)
                e.dma_start(self.zero_rows, zr[:, :, :].bitcast(F32)).then_inc(s_zd, 16)
                e.wait_ge(s_zd, 16)
            @block.tensor
            def _(e):
                S.start(e)
                e.wait_ge(s_w, n_w)
                with e.Fori(0, NB) as i:
                    V.wait(e, "h", i)
                    S.done(self.transposes(e, h, 0, (0, 1)), "turn")
                    V.wait(e, "hT0", i)
                    A.wait(e, "hT1", i)
                    for name, w, bank in (("q", Wq, 2), ("k", Wk, 4)):
                        for g in range(KD):
                            for kt in range(KD):
                                last = e.matmul(PS[:, bank + g, :], w[:, kt, g * P:(g + 1) * P], hT[:, kt, :], start=kt == 0, stop=kt == KD - 1)
                        S.done(last, name)
                    S.done(self.token_major(e, hT, Wv, (6, 7)), "v")
            @block.scalar
            def _(e):
                A.start(e)
                e.wait_ge(s_w, n_w)
                e.activation(bqs[:, :], bq[:, :], ACT.Copy, scale=HD ** -0.5).then_inc(s_b, 1)
                e.wait_ge(s_b, 1)
                with e.Fori(0, NB) as i:
                    self.norm_rstd(e, A, V, i, mv, lv, rstd)
                    S.wait(e, "turn", i)
                    A.done(e.activation(hT[:, 1, :], PS[:, 1, :], ACT.Copy), "hT1")
                    for name, dst, bias, bank, scale in (("q", qf, bqs, 2, HD ** -0.5), ("k", kf, bk, 4, 1.0)):
                        S.wait(e, name, i)
                        for g in range(KD):
                            last = e.activation(dst[:, g, :], PS[:, bank + g, :], ACT.Identity, bias=bias[:, g:g + 1], scale=scale)
                        A.done(last, name)
            @block.vector
            def _(e):
                V.start(e)
                e.wait_ge(s_w, n_w)
                with e.Fori(0, NB) as i:
                    x = X[:, bass.ds(i * TB, TB), :]
                    for t in range(TB):
                        last = e.bn_stats(st[:, t, :], X[:, i * TB + t, :])
                    V.done(last, "stats")
                    V.wait_apart(e, "stats", i, self.apart)
                    for t in range(TB):
                        last = e.bn_aggr(mv[:, t, :], st[:, t, :])
                    V.done(last, "stats_mv")
                    self.row_norm_affine(e, V, A, i, x, h, st, mv, rstd, g1, b1, "h")
                    S.wait(e, "turn", i)
                    V.done(e.tensor_copy(hT[:, 0, :], PS[:, 0, :]), "hT0")
                    for n, (name, src) in enumerate((("q", qf), ("k", kf))):
                        hi, lo = part[2 * n], part[2 * n + 1]
                        A.wait(e, name, i)
                        e.wait_ge(s_st, 16 + 16 * 4 * i)
                        V.done(e.tensor_copy(hi[:, :, :], src[:, :, :]), name + "hi")
                        V.wait(e, name + "hi", i)
                        V.done(e.tensor_tensor(lo[:, :, :], src[:, :, :], hi[:, :, :].bitcast(F32), ALU.subtract), name + "lo")
                    S.wait(e, "v", i)
                    e.wait_ge(s_z, 1)
                    V.done(e.tensor_tensor(V_[:, bass.ds(i * TB, TB), :, 0:HD], self.pair_banks(6).rearrange("p t (h d) -> p t h d", h=H),
                                           bv[:, :].rearrange("p (h d) -> p h d", h=H).unsqueeze(1).broadcast_to((P, TB, H, HD)), ALU.add), "v")
            @block.sync
            def _(e):
                e.sem_inc(s_st, 16)
                dst = self.parts.rearrange("q (b g p) t -> q b p g t", b=B, g=KD)
                with e.Fori(0, B) as b:
                    with e.Fori(0, T // BLK) as cc:
                        for n, name in enumerate(("qhi", "qlo", "khi", "klo")):
                            V.wait(e, name, b * 2 + cc)
                            e.dma_start(dst[n, b, :, :, bass.ds(cc * BLK, BLK)], part[n][:, :, :].bitcast(F32)).then_inc(s_st, 16)
                e.wait_ge(s_st, 16 + 16 * 4 * NB)

    def attend(self, c):
        nc, PS, V_, OT = self.nc, self.PS, self.V, self.OT
        sb = lambda n, s, dt=F32: self.sb(c, n, s, dt)
        NG, NK, G4 = B * H // 4, T // P, 4
        Q = [sb(f"aQ{p}", [P, 2, T], F32R) for p in range(2)]
        K = [sb(f"aK{p}", [P, 2, 2, T], F32R) for p in range(2)]
        Vs = [sb(f"aV{p}", [P, NK, G4, 2 * HD]) for p in range(2)]
        R = 2
        Pb = [sb(f"aP{r}", [P, G4, BLK]) for r in range(R)]
        nm, nmhi, nmlo = sb("a_nm", [P, NK, G4]), sb("a_nmhi", [G4, T], F32R), sb("a_nmlo", [G4, T], F32R)
        identr, maskq, maskk = sb("a_idr", [P, P], F32R), sb("a_mq", [P, P], F32R), sb("a_mk", [P, P], F32R)
        parts = self.parts.rearrange("q (n s r2 r) t -> q n r2 r s t", s=2, r2=2, r=HD)
        zero_rows = self.zero_rows
        steps = [(qb, kt) for qb in range(2) for kt in range(4 * (qb + 1))]
        units = [(j, qt) for j in range(G4) for qt in (7, 0, 6, 1, 5, 2, 4, 3)]
        sched = {s: [] for s in range(len(steps))}
        for n, u in enumerate(units):
            sched[3 + n // 4 if n < 28 else 10].append(u)
        TURN = 10
        pe_names = []
        for s in range(len(steps)):
            pe_names += [f"e{s}a", f"e{s}b"] + [f"u{j}_{qt}" for j, qt in sched[s]]
            if s == TURN:
                pe_names.append("nmT")
            if s:
                pe_names.append(f"pv{s - 1}")
        pe_names.append(f"pv{len(steps) - 1}")
        first = [f"u{j}_{qt}" for j, qt in units] + ["nmT"]
        def two(names):
            return [f"{n}.{p}" for p in range(2) for n in names]
        S = self.steps("a_pe", two(pe_names), [f"{n}.-" for n in first])
        A = self.steps("a_act", two([f"p{s}{x}" for s in range(len(steps)) for x in "ab"]))
        dv = []
        for s in range(len(steps)):
            dv += [f"u{j}_{qt}" for j, qt in sched[s]]
            if s == TURN:
                dv += ["nmhi", "nmlo"]
            if s in (4, 11):
                dv.append(f"o{s // 11}")
        V = self.steps("a_dve", two(dv), [f"{n}.-" for n in [f"u{j}_{qt}" for j, qt in units] + ["nmhi", "nmlo"]])
        C = self.steps("a_pool", two(["vs"]), ["z", "zq", "id", "mq", "mk", "k0", "k1", "ones"] + ["vs.-"])
        s_ld = [self.sem(f"a_ld{p}") for p in range(2)]
        s_aug = [self.sem(f"a_aug{p}") for p in range(2)]
        n_ld, n_aug = 16 * 14, 16 * 2 * G4

        def at(steps_, eng, name, p, i):
            steps_.wait(eng, f"{name}.{p}", i)

        with nc.Block() as block:
            @block.gpsimd
            def _(e):
                C.start(e)
                sel = lambda t, op, fill, base, pattern, cm: e.affine_select(out=t, in_=t, compare_op=op, fill=fill, base=base,
                                                                             pattern=pattern, channel_multiplier=cm)
                e.memset(identr[:, :].bitcast(F32), 0.0)
                e.memset(maskq[:, :].bitcast(F32), 0.0)
                C.done(e.memset(maskk[:, :].bitcast(F32), 0.0), "z")
                e.memset(K[0][:, :, :, :].bitcast(F32), 0.0)
                C.done(e.memset(K[1][:, :, :, :].bitcast(F32), 0.0), "zq")
                C.wait(e, "zq")
                C.done(sel(identr[:, :], ALU.not_equal, 1.0, 0, [[-1, P]], 1), "id")
                C.done(sel(maskq[:, :], ALU.is_ge, MASKED, 0, [[-1, P]], 1), "mq")
                C.done(sel(maskk[:, :], ALU.is_ge, MASKED, 0, [[1, P]], -1), "mk")
                for p in range(2):
                    kk = K[p][:, :, :, :].rearrange("q s r t -> q s r t")
                    sel(kk, ALU.not_equal, 1.0, -3 * HD, [[0, 2], [-4 * HD, 2], [0, T]], 1).then_inc(C.sem, 1)
                C.wait(e, "k1")
                for p in range(2):
                    last = sel(K[p][:, :, :, :], ALU.not_equal, 1.0, -3 * HD - 1, [[0, 2], [-4 * HD, 2], [0, T]], 1)
                C.done(last, "ones")
                C.done(e.tensor_copy(Vs[0][:, :, :, :], V_[:, 0:NK, 0:G4, :]), "vs.-")
                with e.Fori(0, NG // 2) as i:
                    for p in range(2):
                        n = (i * 2 + p + 1) % NG
                        S.wait_before(e, i) if p == 0 else at(S, e, f"pv{len(steps) - 1}", 0, i)
                        C.done(e.tensor_copy(Vs[1 - p][:, :, :, :], V_[:, bass.ds((n // 4) * NK, NK), bass.ds((n % 4) * G4, G4), :]), f"vs.{p}")
            def loads(e, p, n):
                for par in range(2):
                    r0 = 4 * HD * par
                    for slot, part in enumerate((0, 0, 1)):
                        e.dma_start(Q[p][r0 + HD * slot:r0 + HD * slot + HD, :, :].bitcast(F32), parts[part, n, par, :, :, :]).then_inc(s_ld[p], 16)
                    e.dma_start(Q[p][r0 + 3 * HD:r0 + 4 * HD, :, :].bitcast(F32), zero_rows).then_inc(s_ld[p], 16)
                    for slot, part in enumerate((2, 3, 2)):
                        e.dma_start(K[p][r0 + HD * slot:r0 + HD * slot + HD, :, par, :].bitcast(F32), parts[part, n, par, :, :, :]).then_inc(s_ld[p], 16)
            def augs(e, p):
                for j in range(G4):
                    row = 4 * HD * (j % 2) + 3 * HD
                    e.dma_start(Q[p][row:row + 1, j // 2, :].bitcast(F32), nmhi[j:j + 1, :].bitcast(F32)).then_inc(s_aug[p], 16)
                    e.dma_start(Q[p][row + 1:row + 2, j // 2, :].bitcast(F32), nmlo[j:j + 1, :].bitcast(F32)).then_inc(s_aug[p], 16)
            @block.sync
            def _(e):
                C.wait(e, "ones")
                loads(e, 0, 0)
                V.wait(e, "nmhi.-")
                V.wait(e, "nmlo.-")
                augs(e, 0)
                with e.Fori(0, NG // 2) as i:
                    for p in range(2):
                        S.wait_before(e, i) if p == 0 else at(S, e, f"pv{len(steps) - 1}", 0, i)
                        loads(e, 1 - p, (i * 2 + p + 1) % NG)
                        at(V, e, "nmlo", p, i)
                        augs(e, 1 - p)
                for p in range(2):
                    e.wait_ge(s_aug[p], n_aug * (NG // 2 + (p == 0)))

            @block.tensor
            def _(e):
                S.start(e)
                def maxima(j, qt, q, tag, i, prev):
                    bank = 5 if qt >= 4 else 7
                    if prev:
                        V.wait(e, prev + tag, i)
                    cols = (qt + 1) * P
                    for b0 in range(0, cols, BLK):
                        w = min(BLK, cols - b0)
                        e.matmul(PS[:, bank + b0 // BLK, 0:w], Q[q][:, j // 2, qt * P:(qt + 1) * P], K[q][:, j // 2, j % 2, b0:b0 + w],
                                 start=True, stop=b0 + w < cols)
                    S.done(e.matmul(PS[:, bank + (cols - P) // BLK, (cols - P) % BLK:(cols - P) % BLK + P], identr[:, :], maskq[:, :],
                                    start=False, stop=True), f"u{j}_{qt}" + tag)
                def turn_maxima(tag, i):
                    V.wait(e, f"u{G4 - 1}_3" + tag, i)
                    for qt in range(NK):
                        last = e.transpose(PS[0:G4, 5 + qt // 4, (qt % 4) * P:(qt % 4 + 1) * P], nm[:, qt, :], self.ident[:, :])
                    S.done(last, "nmT" + tag)
                def before(n):
                    return f"u{units[n - 2][0]}_{units[n - 2][1]}" if n >= 2 else None
                e.wait_ge(s_ld[0], n_ld)
                for n, (j, qt) in enumerate(units):
                    maxima(j, qt, 0, ".-", 0, before(n))
                turn_maxima(".-", 0)
                with e.Fori(0, NG // 2) as i:
                    for p in range(2):
                        tag = f".{p}"
                        e.wait_ge(s_aug[p], n_aug * (i + 1))
                        at(C, e, "vs", 1, i - 1) if p == 0 else at(C, e, "vs", 0, i)
                        def pv(s):
                            qb, kt = steps[s]
                            c0 = max(0, kt - 4 * qb) * P
                            A.wait(e, f"p{s}b" + tag, i)
                            if kt == 0:
                                if qb:
                                    V.wait(e, "o0" + tag, i)
                                elif p:
                                    V.wait(e, "o1.0", i)
                                else:
                                    V.wait_before(e, i)
                            for j in range(G4):
                                last = e.matmul(PS[32 * j:32 * j + 32, 4, c0:BLK], Vs[p][:, kt, j, :], Pb[s % R][:, j, c0:BLK],
                                                start=kt == 0, stop=kt == 4 * qb + 3, skip_group_check=True)
                            S.done(last, f"pv{s}" + tag)
                        n = 0
                        for s, (qb, kt) in enumerate(steps):
                            c0 = max(0, kt - 4 * qb) * P
                            for x, js in (("a", (0, 1)), ("b", (2, 3))):
                                if s:
                                    A.wait(e, f"p{s - 1}{x}" + tag, i)
                                elif p:
                                    A.wait(e, f"p{len(steps) - 1}{x}.0", i)
                                else:
                                    A.wait_before(e, i)
                                for j in js:
                                    diag = kt >= 4 * qb
                                    last = e.matmul(PS[:, j, c0:BLK], K[p][:, j // 2, j % 2, kt * P:(kt + 1) * P],
                                                    Q[p][:, j // 2, qb * BLK + c0:(qb + 1) * BLK], start=True, stop=not diag)
                                    if diag:
                                        last = e.matmul(PS[:, j, c0:c0 + P], identr[:, :], maskk[:, :], start=False, stop=True)
                                S.done(last, f"e{s}{x}" + tag)
                            for j, qt in sched[s]:
                                if n == 0:
                                    e.wait_ge(s_ld[1 - p], n_ld * (i + 1 + (p == 1)))
                                    V.wait(e, "nmlo.0", i) if p else V.wait_before(e, i)
                                maxima(j, qt, 1 - p, tag, i, before(n))
                                n += 1
                            if s == TURN:
                                turn_maxima(tag, i)
                            if s:
                                pv(s - 1)
                        pv(len(steps) - 1)

            @block.scalar
            def _(e):
                A.start(e)
                with e.Fori(0, NG // 2) as i:
                    for p in range(2):
                        tag = f".{p}"
                        for s, (qb, kt) in enumerate(steps):
                            c0 = max(0, kt - 4 * qb) * P
                            for x, j0 in (("a", 0), ("b", 2)):
                                if s >= R:
                                    S.wait(e, f"pv{s - R}" + tag, i)
                                elif p:
                                    S.wait(e, f"pv{len(steps) - R + s}.0", i)
                                elif s == R - 1:
                                    S.wait_before(e, i)
                                else:
                                    S.wait_before(e, i)
                                S.wait(e, f"e{s}{x}" + tag, i)
                                A.done(e.activation(Pb[s % R][:, j0:j0 + 2, c0:BLK], PS[:, j0:j0 + 2, c0:BLK], ACT.Exp), f"p{s}{x}" + tag)

            @block.vector
            def _(e):
                V.start(e)
                def unit(j, qt, tag, i):
                    S.wait(e, f"u{j}_{qt}" + tag, i)
                    bank, cols = (5, (qt + 1) * P) if qt >= 4 else (7, (qt + 1) * P)
                    src = PS[:, bank:bank + 2, :].rearrange("p b n -> p (b n)")[:, 0:cols] if qt >= 4 else PS[:, bank, 0:cols]
                    V.done(e.tensor_reduce(nm[:, qt, j:j + 1], src, AX.X, ALU.max, negate=True), f"u{j}_{qt}" + tag)
                def negmax(tag, i):
                    S.wait(e, "nmT" + tag, i)
                    src = PS[0:G4, 5:7, :].rearrange("p b n -> p (b n)")
                    V.done(e.tensor_copy(nmhi[:, :], src), "nmhi" + tag)
                    V.wait(e, "nmhi" + tag, i)
                    V.done(e.tensor_tensor(nmlo[:, :], src, nmhi[:, :].bitcast(F32), ALU.subtract), "nmlo" + tag)
                for j, qt in units:
                    unit(j, qt, ".-", 0)
                negmax(".-", 0)
                with e.Fori(0, NG // 2) as i:
                    for p in range(2):
                        tag = f".{p}"
                        for s in range(len(steps)):
                            for j, qt in sched[s]:
                                unit(j, qt, tag, i)
                            if s == TURN:
                                if p == 0:
                                    e.wait_ge(s_aug[0], n_aug * (i + 1))
                                else:
                                    e.wait_ge(s_aug[1], n_aug * (i + 1))
                                negmax(tag, i)
                            if s in (4, 11):
                                qb = s // 11
                                S.wait(e, f"pv{3 if qb == 0 else 11}" + tag, i)
                                V.done(e.tensor_copy(OT[:, i * 2 + p, qb * BLK:(qb + 1) * BLK], PS[:, 4, :]), f"o{qb}" + tag)


    def route(self, c):
        nc, a, PS, X, OT = self.nc, self.a, self.PS, self.X, self.OT
        sb = lambda n, s, dt=F32: self.sb(c, n, s, dt)
        NG4 = H // 4
        Wo, bo, g2, b2 = sb("r_Wo", [P, KD, D]), sb("r_bo", [P, D]), sb("r_g2", [P, D]), sb("r_b2", [P, D])
        Wr, br, eb2 = sb("r_Wr", [P, KD, E]), sb("r_br", [P, E]), sb("r_eb2", [E, D])
        os_, rec, on, onT = sb("r_os", [P, NG4, BLK]), sb("r_rec", [P, TB, H]), sb("r_on", [P, TB, D]), sb("r_onT", [P, KD, BLK])
        ya, h2, h2T = sb("r_a", [P, TB, D]), sb("r_h2", [P, TB, D]), sb("r_h2T", [P, KD, BLK])
        hi, lo = sb("r_hi", [P, KD, BLK], F32R), sb("r_lo", [P, KD, BLK], F32R)
        lg, best, keep, ex, ws, wT = (sb("r_lg", [P, TB, E]), sb("r_best", [P, TB, 8]), sb("r_keep", [P, TB, E]), sb("r_ex", [P, TB, E]),
                                      sb("r_ws", [P, TB]), sb("r_wT", [E, BLK]))
        st, mv, lv, rstd = sb("r_st", [P, TB, 6]), sb("r_mv", [P, TB, 2]), sb("r_lv", [P, TB]), sb("r_rstd", [P, TB])
        self.h2_parts = nc.dram_tensor("h2_parts", (2, P, KD, N), F32).ap()
        s_w, s_st = self.sem("r_w"), self.sem("r_store")
        n_w = 16 * 7
        S = self.steps("r_pe", [f"ot{t}" for t in range(TB)] + ["onT", "wo", "h2T", "lg", "wT", "b2"])
        A = self.steps("r_act", ["os", "onT1", "rstd_ln", "rstd", "h2T1", "ex", "wT"])
        V = self.steps("r_dve", [n for t in range(TB) for n in (f"rec{t}", f"on{t}")] + ["onT0", "xb", "a", "stats", "stats_mv", "h2_n", "h2_g", "h2",
                                 "h2T0", "hi", "lo", "lg", "best", "keep", "sh", "w_", "ws", "wr", "w", "xa", "x"])
        with nc.Block() as block:
            @block.gpsimd
            def _(e):
                e.dma_start(Wo[:, :, :], a["L0_ffn_Wo"].rearrange("(k p) n -> p k n", p=P)).then_inc(s_w, 16)
                e.dma_start(Wr[:, :, :], a["L0_ffn_Wr"].rearrange("(k p) n -> p k n", p=P)).then_inc(s_w, 16)
                for t, w in ((bo, "bo"), (g2, "ln2_g"), (b2, "ln2_b"), (br, "br")):
                    e.dma_start(t[:, :], a["L0_ffn_" + w].partition_broadcast(P)).then_inc(s_w, 16)
                e.dma_start(eb2[:, :], a["L0_ffn_e_b2"]).then_inc(s_w, 16)
            @block.sync
            def _(e):
                e.sem_inc(s_st, 16)
                with e.Fori(0, NB) as i:
                    for n, (name, t) in enumerate((("hi", hi), ("lo", lo))):
                        V.wait(e, name, i)
                        e.dma_start(self.h2_parts[n, :, :, bass.ds(i * BLK, BLK)], t[:, :, :].bitcast(F32)).then_inc(s_st, 16)
                e.wait_ge(s_st, 16 + 16 * 2 * NB)
            @block.tensor
            def _(e):
                S.start(e)
                e.wait_ge(s_w, n_w)
                with e.Fori(0, NB) as i:
                    A.wait(e, "os", i)
                    for t in range(TB):
                        if t >= 2:
                            V.wait(e, f"on{t - 2}", i)
                        for g in range(NG4):
                            last = e.transpose(PS[:, t % 2, g * P:(g + 1) * P], os_[:, g, t * P:(t + 1) * P], self.ident[:, :])
                        S.done(last, f"ot{t}")
                    V.wait(e, f"on{TB - 1}", i)
                    S.done(self.transposes(e, on, 0, (2, 3)), "onT")
                    V.wait(e, "onT0", i)
                    A.wait(e, "onT1", i)
                    S.done(self.token_major(e, onT, Wo, (4, 5)), "wo")
                    V.wait(e, "h2", i)
                    S.done(self.transposes(e, h2, 0, (6, 7)), "h2T")
                    V.wait(e, "h2T0", i)
                    A.wait(e, "h2T1", i)
                    for t in range(TB):
                        for kt in range(KD):
                            last = e.matmul(PS[:, 0, t * E:(t + 1) * E], h2T[:, kt, t * P:(t + 1) * P], Wr[:, kt, :], start=kt == 0, stop=kt == KD - 1)
                    S.done(last, "lg")
                    V.wait(e, "w", i)
                    for t in range(TB):
                        last = e.transpose(PS[0:E, 1, t * P:(t + 1) * P], ex[:, t, :], self.ident[:, :])
                    S.done(last, "wT")
                    A.wait(e, "wT", i)
                    for t in range(TB):
                        last = e.matmul(PS[:, 2 + t // 2, (t % 2) * D:(t % 2 + 1) * D], wT[:, t * P:(t + 1) * P], eb2[:, :], start=True, stop=True)
                    S.done(last, "b2")
            @block.scalar
            def _(e):
                A.start(e)
                with e.Fori(0, B) as b:
                    with e.Fori(0, T // BLK) as cc:
                        i = b * 2 + cc
                        S.wait_before(e, i)
                        A.done(e.activation(os_[:, :, :], OT[:, bass.ds(b * NG4, NG4), bass.ds(cc * BLK, BLK)], ACT.Copy), "os")
                        S.wait(e, "onT", i)
                        A.done(e.activation(onT[:, 1, :], PS[:, 3, :], ACT.Copy), "onT1")
                        self.norm_rstd(e, A, V, i, mv, lv, rstd)
                        S.wait(e, "h2T", i)
                        A.done(e.activation(h2T[:, 1, :], PS[:, 7, :], ACT.Copy), "h2T1")
                        V.wait(e, "sh", i)
                        A.done(e.activation(ex[:, :, :], lg[:, :, :], ACT.Exp), "ex")
                        S.wait(e, "wT", i)
                        A.done(e.activation(wT[:, :], PS[0:E, 1, :], ACT.Copy), "wT")
            @block.vector
            def _(e):
                V.start(e)
                e.wait_ge(s_w, n_w)
                with e.Fori(0, NB) as i:
                    xt = X[:, bass.ds(i * TB, TB), :]
                    bc = lambda v, n: v.unsqueeze(2).broadcast_to((P, TB, n))
                    for t in range(TB):
                        S.wait(e, f"ot{t}", i)
                        o = PS[:, t % 2, :].rearrange("p (h c) -> p h c", c=2 * HD)
                        V.done(e.reciprocal(rec[:, t, :], o[:, :, HD]), f"rec{t}")
                        V.wait(e, f"rec{t}", i)
                        V.done(e.tensor_tensor(on[:, t, :].rearrange("p (h d) -> p h d", h=H), o[:, :, 0:HD],
                                               rec[:, t, :].unsqueeze(2).broadcast_to((P, H, HD)), ALU.mult), f"on{t}")
                    S.wait(e, "onT", i)
                    V.done(e.tensor_copy(onT[:, 0, :], PS[:, 2, :]), "onT0")
                    V.done(e.tensor_tensor(ya[:, :, :], xt, bo[:, :].unsqueeze(1).broadcast_to((P, TB, D)), ALU.add), "xb")
                    V.wait(e, "xb", i)
                    S.wait(e, "wo", i)
                    V.done(e.tensor_tensor(ya[:, :, :], self.pair_banks(4), ya[:, :, :], ALU.add), "a")
                    V.wait(e, "a", i)
                    self.norm_stats(e, V, i, ya, st, mv)
                    self.row_norm_affine(e, V, A, i, ya, h2, st, mv, rstd, g2, b2, "h2")
                    S.wait(e, "h2T", i)
                    V.done(e.tensor_copy(h2T[:, 0, :], PS[:, 6, :]), "h2T0")
                    e.wait_ge(s_st, 16 + 16 * 2 * i)
                    A.wait(e, "h2T1", i)
                    V.wait(e, "h2T0", i)
                    V.done(e.tensor_copy(hi[:, :, :], h2T[:, :, :]), "hi")
                    V.wait(e, "hi", i)
                    V.done(e.tensor_tensor(lo[:, :, :], h2T[:, :, :], hi[:, :, :].bitcast(F32), ALU.subtract), "lo")
                    S.wait(e, "lg", i)
                    V.done(e.tensor_tensor(lg[:, :, :], PS[:, 0, 0:TB * E].rearrange("p (t n) -> p t n", n=E),
                                           br[:, :].unsqueeze(1).broadcast_to((P, TB, E)), ALU.add), "lg")
                    V.wait_apart(e, "lg", i, self.apart)
                    for t in range(TB):
                        last = e.max(best[:, t, :], lg[:, t, :])
                    V.done(last, "best")
                    V.wait(e, "best", i)
                    V.done(e.tensor_tensor(keep[:, :, :], lg[:, :, :], bc(best[:, :, 1], E), ALU.is_ge), "keep")
                    V.wait(e, "keep", i)
                    V.done(e.tensor_tensor(lg[:, :, :], lg[:, :, :], bc(best[:, :, 0], E), ALU.subtract), "sh")
                    A.wait(e, "ex", i)
                    V.done(e.tensor_tensor(ex[:, :, :], ex[:, :, :], keep[:, :, :], ALU.mult), "w_")
                    V.wait(e, "w_", i)
                    V.done(e.tensor_reduce(ws[:, :], ex[:, :, :], AX.X, ALU.add), "ws")
                    V.wait(e, "ws", i)
                    V.done(e.reciprocal(ws[:, :], ws[:, :]), "wr")
                    V.wait(e, "wr", i)
                    w_blk = self.w_all[:, bass.ds(i * TB, TB), :]
                    e.tensor_tensor(w_blk, ex[:, :, :], bc(ws[:, :], E), ALU.mult)
                    V.done(e.tensor_tensor(ex[:, :, :], ex[:, :, :], bc(ws[:, :], E), ALU.mult), "w")
                    V.done(e.tensor_tensor(xt, xt, ya[:, :, :], ALU.add), "xa")
                    V.wait(e, "xa", i)
                    S.wait(e, "b2", i)
                    V.done(e.tensor_tensor(xt, self.pair_banks(2), xt, ALU.add), "x")

    def experts(self, c):
        nc, a, PS, X = self.nc, self.a, self.PS, self.X
        sb = lambda n, s, dt=F32: self.sb(c, n, s, dt)
        h2 = [sb(f"x_h2{n}", [P, KD, N], F32R) for n in range(2)]
        w1 = [[sb(f"x_w1{p}{n}", [P, KD, FF], F32R) for n in range(2)] for p in range(2)]
        w2 = [[sb(f"x_w2{p}{n}", [P, NF, D], F32R) for n in range(2)] for p in range(2)]
        raw1, raw2 = sb("x_raw1", [P, KD, FF]), sb("x_raw2", [P, NF, D])
        b1r, b1 = sb("x_b1r", [E * NF, P]), sb("x_b1", [P, E, NF])
        g = [sb(f"x_g{r}", [P, BLK]) for r in range(2)]
        mid = [sb(f"x_mid{n}", [P, NF, BLK], F32R) for n in range(2)]
        st, mv, lv, rstd = sb("x_st", [P, NT, 6]), sb("x_mv", [P, NT, 2]), sb("x_lv", [P, NT]), sb("x_rstd", [P, NT])
        PASSES = ((0, 0), (0, 1), (1, 0))
        s_h, s_b, s_w1, s_w2 = self.sem("x_h"), self.sem("x_b"), self.sem("x_w1"), self.sem("x_w2")
        fs = range(NF)
        S = self.steps("x_pe", [f"m{f}" for f in fs] + ["out"], ["b1"])
        A = self.steps("x_act", [f"g{f}" for f in fs], ["b1"])
        A2 = self.steps("x_act2", ["ln", "rstd"])
        V = self.steps("x_dve", [n for f in fs for n in (f"hi{f}", f"lo{f}")] + [f"x{t}" for t in range(TB)])
        V2 = self.steps("x_dve2", ["stats", "mv"])
        def free_pool(e, i, p):
            e.wait_ge(s_free[p], i + 1)
        s_free = [self.sem(f"x_free{p}") for p in range(2)]
        C = self.steps("x_pool", [n for p in range(2) for n in (f"w1hi{p}", f"w1lo{p}", f"w2hi{p}", f"w2lo{p}")])
        with nc.Block() as block:
            @block.sync
            def _(e):
                e.dma_start(b1r[:, :], a["L0_ffn_e_b1"].rearrange("e (f p) -> (e f) p", p=P)).then_inc(s_b, 16)
                e.dma_start(raw1[:, :, :], a["L0_ffn_e_w1"][0].rearrange("(k p) n -> p k n", p=P)).then_inc(s_w1, 16)
                e.dma_start(raw2[:, :, :], a["L0_ffn_e_w2"][0].rearrange("(k p) n -> p k n", p=P)).then_inc(s_w2, 16)
                for n in range(2):
                    e.dma_start(h2[n][:, :, :].bitcast(F32), self.h2_parts[n]).then_inc(s_h, 16)
                v1 = a["L0_ffn_e_w1"].rearrange("e (k p) n -> e p k n", p=P)
                v2 = a["L0_ffn_e_w2"].rearrange("e (k p) n -> e p k n", p=P)
                with e.Fori(0, E // 2) as i:
                    for p in range(2):
                        n = (i * 2 + p + 1) % E
                        C.wait(e, f"w1lo{p}", i)
                        e.dma_start(raw1[:, :, :], v1[n]).then_inc(s_w1, 16)
                        C.wait(e, f"w2lo{p}", i)
                        e.dma_start(raw2[:, :, :], v2[n]).then_inc(s_w2, 16)
                e.wait_ge(s_w1, 16 * (E + 1))
                e.wait_ge(s_w2, 16 * (E + 1))
            @block.gpsimd
            def _(e):
                C.start(e)
                with e.Fori(0, E // 2) as i:
                    for p in range(2):
                        free_pool(e, i, p)
                        for raw, w, name, s in ((raw1, w1, "w1", s_w1), (raw2, w2, "w2", s_w2)):
                            e.wait_ge(s, 16 * (i * 2 + p + 1))
                            e.sem_inc(self.apart, 1)
                            C.done(e.tensor_copy(w[p][0][:, :, :], raw[:, :, :]), f"{name}hi{p}")
                            C.wait(e, f"{name}hi{p}", i)
                            C.done(e.tensor_tensor(w[p][1][:, :, :], raw[:, :, :], w[p][0][:, :, :].bitcast(F32), ALU.subtract), f"{name}lo{p}")
            @block.tensor
            def _(e):
                S.start(e)
                e.sem_inc(s_free[0], 1)
                e.sem_inc(s_free[1], 1)
                e.wait_ge(s_b, 16)
                S.done(e.transpose(PS[:, 0, 0:E * NF], b1r[:, :], self.ident[0:E * NF, 0:E * NF]), "b1")
                A.wait(e, "b1")
                e.wait_ge(s_h, 32)
                with e.Fori(0, E // 2) as i:
                    for p in range(2):
                        with e.Fori(0, NB) as k:
                            it = (i * 2 + p) * NB + k
                            C.wait(e, f"w1lo{p}", i)
                            for f in fs:
                                if f >= 4:
                                    A.wait(e, f"g{f - 4}", it)
                                else:
                                    A.wait_before(e, it)
                                for n, (u, v) in enumerate(PASSES):
                                    for kt in range(KD):
                                        last = e.matmul(PS[:, f % 4, :], w1[p][u][:, kt, f * P:(f + 1) * P], h2[v][:, kt, bass.ds(k * BLK, BLK)],
                                                        start=n == 0 and kt == 0, stop=n == 2 and kt == KD - 1)
                                S.done(last, f"m{f}")
                            C.wait(e, f"w2lo{p}", i)
                            V.wait_before(e, it)
                            for f in fs:
                                V.wait(e, f"lo{f}", it)
                                for t in range(TB):
                                    for n, (u, v) in enumerate(PASSES):
                                        last = e.matmul(PS[:, 4 + t, 0:D], mid[u][:, f, t * P:(t + 1) * P], w2[p][v][:, f, :],
                                                        start=f == 0 and n == 0, stop=f == NF - 1 and n == 2)
                            S.done(last, "out")
                        S.wait_before(e, (i * 2 + p + 1) * NB)
                        e.sem_inc(s_free[p], 1)
            @block.scalar
            def _(e):
                A.start(e)
                A2.start(e)
                S.wait(e, "b1")
                A.done(e.activation(b1[:, :, :].rearrange("p e f -> p (e f)"), PS[:, 0, 0:E * NF], ACT.Copy), "b1")
                A.wait(e, "b1")
                with e.Fori(0, E) as n:
                    with e.Fori(0, NB) as k:
                        it = n * NB + k
                        for f in fs:
                            S.wait(e, f"m{f}", it)
                            if f >= 2:
                                V.wait(e, f"lo{f - 2}", it)
                            else:
                                V.wait_before(e, it)
                            A.done(e.activation(g[f % 2][:, :], PS[:, f % 4, :], ACT.Gelu, bias=b1[:, n, f:f + 1]), f"g{f}")
                V2.wait(e, "mv")
                A2.done(e.activation(lv[:, :], mv[:, :, 1], ACT.Ln, bias=self.eps[:, 0:1]), "ln")
                A2.wait(e, "ln")
                A2.done(e.activation(rstd[:, :], lv[:, :], ACT.Exp, scale=-0.5), "rstd")
            @block.vector
            def _(e):
                V.start(e)
                V2.start(e)
                with e.Fori(0, E) as n:
                    with e.Fori(0, NB) as k:
                        it = n * NB + k
                        for f in fs:
                            A.wait(e, f"g{f}", it)
                            if f == 0:
                                S.wait_before(e, it)
                            V.done(e.tensor_copy(mid[0][:, f, :], g[f % 2][:, :]), f"hi{f}")
                            V.wait(e, f"hi{f}", it)
                            V.done(e.tensor_tensor(mid[1][:, f, :], g[f % 2][:, :], mid[0][:, f, :].bitcast(F32), ALU.subtract), f"lo{f}")
                        S.wait(e, "out", it)
                        for t in range(TB):
                            xt = X[:, k * TB + t, :]
                            V.done(e.scalar_tensor_tensor(out=xt, in0=PS[:, 4 + t, 0:D], scalar=self.w_all[:, k * TB + t, bass.ds(n, 1)],
                                                          in1=xt, op0=ALU.mult, op1=ALU.add), f"x{t}")
                V.wait_before(e, E * NB)
                for t in range(NT):
                    last = e.bn_stats(st[:, t, :], X[:, t, :])
                V2.done(last, "stats")
                V2.wait(e, "stats")
                for t in range(NT):
                    last = e.bn_aggr(mv[:, t, :], st[:, t, :])
                V2.done(last, "mv")
                A2.wait(e, "rstd")
                for t in range(NT):
                    last = e.tensor_scalar(X[:, t, :], X[:, t, :], mv[:, t, 0:1], rstd[:, t:t + 1], ALU.subtract, ALU.mult)


def kernel(**inputs):
    import concourse.bacc as bacc
    import numpy as np
    from concourse.bass_utils import run_bass_kernel_spmd

    nc = bacc.Bacc("TRN2", target_bir_lowering=False, num_devices=1)
    arrays, aps = {}, {}
    for name, value in inputs.items():
        array = np.ascontiguousarray(value)
        arrays[name] = array
        aps[name] = nc.dram_tensor(name, array.shape, mybir.dt.from_np(array.dtype), kind="ExternalInput").ap()
    out = nc.dram_tensor("out", (B, T, D), F32, kind="ExternalOutput").ap()
    Kernel(nc, aps, out).build()
    results = run_bass_kernel_spmd(nc, [arrays], core_ids=[0])
    return results.results[0]["out"]
```

```python
from contextlib import ExitStack

import concourse.bass as bass
from concourse import mybir

F32 = mybir.dt.float32
F32R = mybir.dt.float32r
BF16 = mybir.dt.bfloat16
I32 = mybir.dt.int32
ALU = mybir.AluOpType
ACT = mybir.ActivationFunctionType
AX = mybir.AxisListType

P = 128
B = 2
T = 1024
N = B * T
D = 256
KD = D // P
H = 16
HD = D // H
DK = 8
LOW = 16
NT = N // P
BLK = 512
NB = N // BLK
TB = BLK // P
NCTX = 64
NSEL = 64
LAT = 128
E = 8
FF = 4 * D
NF = FF // P
EPS = 1e-5
MASKED = -1e30
LN_EXP = "natural_log_exp_and_others"
HG = P // HD


class Steps:

    def __init__(self, sem, names, before=()):
        self.sem, self.names, self.before = sem, list(names), ["start", *before]
        assert len(set(self.names)) == len(self.names)

    def value(self, name, i=0):
        if name in self.before:
            return self.before.index(name) + 1
        return len(self.before) + i * len(self.names) + self.names.index(name) + 1

    def start(self, eng):
        eng.sem_inc(self.sem, 1)

    def done(self, instruction, name):
        instruction.then_inc(self.sem, 1)

    def wait_apart(self, eng, name, i, apart):
        self.wait(eng, name, i)
        eng.sem_inc(apart, 1)

    def wait(self, eng, name, i=0):
        eng.wait_ge(self.sem, self.value(name, i))

    def wait_before(self, eng, i):
        eng.wait_ge(self.sem, len(self.before) + i * len(self.names))


class Kernel:
    def __init__(self, nc, a, out):
        self.nc, self.a, self.out = nc, a, out
        self.top = ExitStack()
        self.n_sem = 0

    def sb(self, ctx, name, shape, dt=F32):
        return ctx.enter_context(self.nc.sbuf_tensor(name, shape, dt))

    def sem(self, name):
        return self.top.enter_context(self.nc.semaphore(name))

    def steps(self, name, names, before=()):
        return Steps(self.sem(name), names, before)

    def build(self, upto=99):
        nc = self.nc
        with self.top:
            self.PS = self.top.enter_context(nc.psum_tensor("PS", [P, 8, BLK], F32))
            self.X = self.sb(self.top, "X", [P, NT, D])
            self.ident = self.sb(self.top, "ident", [P, P])
            self.eps = self.sb(self.top, "eps", [P, 1])
            self.w_all = self.sb(self.top, "w_all", [P, NT, E])
            self.apart = self.sem("apart")
            with ExitStack() as c:
                with ExitStack() as c2:
                    self.cross_buffers(c, c2)
                    with ExitStack() as c3:
                        self.gla_setup(c2, c3)
                    with ExitStack() as c3:
                        self.gla_gates(c2, c3)
                    self.gla_scan(c2)
                    self.cross_setup()
                    self.gla_out(c2)
                if upto >= 2:
                    self.cross_blocks(c)
            if upto >= 3:
                self.self_attention(upto >= 4)
            if upto < 4:
                self.store()

    def store(self):
        s_out = self.sem("s_out")
        with self.nc.Block() as block:
            @block.sync
            def _(e):
                e.dma_start(self.out.rearrange("b (t p) d -> p (b t) d", p=P), self.X[:, :, :]).then_inc(s_out, 16)
                e.wait_ge(s_out, 16)


    def transposes(self, pe, src, blk, banks):
        for kt in range(KD):
            for t in range(TB):
                last = pe.transpose(self.PS[:, banks[kt], t * P:(t + 1) * P],
                                    src[:, TB * blk + t, kt * P:(kt + 1) * P], self.ident[:, :])
        return last

    def token_major(self, pe, srcT, w, banks, start=True, stop=True):
        for t in range(TB):
            for kt in range(KD):
                last = pe.matmul(self.PS[:, banks[t // 2], (t % 2) * D:(t % 2 + 1) * D],
                                 srcT[:, kt, t * P:(t + 1) * P], w[:, kt, :], start=kt == 0, stop=kt == KD - 1)
        return last

    def pair_banks(self, b0):
        return self.PS[:, b0:b0 + 2, :].rearrange("p b (t d) -> p (b t) d", t=2)

    def norm_stats(self, dve, V, i, y, st, mv, tag="stats"):
        for t in range(TB):
            last = dve.bn_stats(st[:, t, :], y[:, t, :])
        V.done(last, tag)
        V.wait_apart(dve, tag, i, self.apart)
        for t in range(TB):
            last = dve.bn_aggr(mv[:, t, :], st[:, t, :])
        V.done(last, tag + "_mv")

    def norm_rstd(self, act, A, V, i, mv, lv, rstd, tag="stats", out="rstd"):
        V.wait(act, tag + "_mv", i)
        A.done(act.activation(lv[:, :], mv[:, :, 1], ACT.Ln, bias=self.eps[:, 0:1]), out + "_ln")
        A.wait(act, out + "_ln", i)
        A.done(act.activation(rstd[:, :], lv[:, :], ACT.Exp, scale=-0.5), out)


    def gla_setup(self, c, c3):
        nc, a, PS, X, ident = self.nc, self.a, self.PS, self.X, self.ident
        sb = lambda n, s, dt=F32: self.sb(c, n, s, dt)
        self.XT = XT = sb("XT", [P, KD, N])
        self.Wq, self.Wk = sb("Wq", [P, KD, P]), sb("Wk", [P, KD, P])
        self.Wgk1, self.Wgk2 = sb("Wgk1", [P, KD, LOW]), sb("Wgk2", [LOW, P])
        self.bgk2 = sb("bgk2", [P, 1])
        self.Wo = sb("Wo", [P, KD, D])
        self.G = G = sb("G", [P, NT, D])
        self.WvB = WvB = sb("WvB", [P, KD, HD, H, DK])
        self.headsum = R = sb("headsum", [P, 32])
        Wv, Wg, gnw = self.sb(c3, "Wv", [P, KD, D]), self.sb(c3, "Wg", [P, KD, D]), self.sb(c3, "gnw", [P, HD])
        s_x, s_w = self.sem("g_x"), self.sem("g_w")
        loads = [(self.Wq, "L0_attn_Wq"), (self.Wk, "L0_attn_Wk"), (self.Wgk1, "L0_attn_Wgk1"), (Wv, "L0_attn_Wv"),
                 (Wg, "L0_attn_Wg"), (self.Wo, "L0_attn_Wo")]
        n_w = 16 * (len(loads) + 3)
        C = self.steps("g_c", ["zero", "zeror", "eps", "ident", "r1", "r2"])
        S = self.steps("g_pe", [n for k in range(NB) for n in (f"t{k}", f"g{k}")])
        V = self.steps("g_dve", [n for k in range(NB) for n in (f"x0{k}",)] + ["wv0", "wv1"] + [f"gn{k}" for k in range(NB)])
        A = self.steps("g_act", [n for k in range(NB) for n in (f"x1{k}", f"silu{k}")])
        with nc.Block() as block:
            @block.sync
            def _(e):
                for k in range(NB):
                    e.dma_start(X[:, k * TB:(k + 1) * TB, :],
                                a["x"].rearrange("b (t p) d -> p (b t) d", p=P)[:, k * TB:(k + 1) * TB, :]).then_inc(s_x, 16)
                    e.wait_ge(s_x, 16 * (k + 1))
            @block.gpsimd
            def _(e):
                for t, w in loads:
                    e.dma_start(t[:, :, :], a[w].rearrange("(k p) n -> p k n", p=P)).then_inc(s_w, 16)
                e.dma_start(self.Wgk2[:, :], a["L0_attn_Wgk2"]).then_inc(s_w, 16)
                e.dma_start(self.bgk2[:, :], a["L0_attn_bgk2"].rearrange("(p o) -> p o", o=1)).then_inc(s_w, 16)
                e.dma_start(gnw[:, :], a["L0_attn_gnw"].partition_broadcast(P)).then_inc(s_w, 16)
                C.start(e)
                C.done(e.memset(ident[:, :], 0.0), "zero")
                C.done(e.memset(R[:, :], 1.0), "zeror")
                C.done(e.memset(self.eps[:, :], EPS), "eps")
                C.wait(e, "zeror")
                C.done(e.affine_select(out=ident[:, :], in_=ident[:, :], compare_op=ALU.not_equal, fill=1.0, base=0,
                                       pattern=[[-1, P]], channel_multiplier=1), "ident")
                C.done(e.affine_select(out=R[:, :], in_=R[:, :], compare_op=ALU.is_ge, fill=0.0, base=0,
                                       pattern=[[-DK, 32]], channel_multiplier=1), "r1")
                C.wait(e, "r1")
                C.done(e.affine_select(out=R[:, :], in_=R[:, :], compare_op=ALU.is_ge, fill=0.0, base=DK - 1,
                                       pattern=[[DK, 32]], channel_multiplier=-1), "r2")
            @block.tensor
            def _(e):
                S.start(e)
                C.wait(e, "ident")
                for k in range(NB):
                    e.wait_ge(s_x, 16 * (k + 1))
                    if k >= 2:
                        V.wait(e, f"x0{k - 2}")
                        A.wait(e, f"x1{k - 2}")
                    S.done(self.transposes(e, X, k, (2 * (k % 2), 2 * (k % 2) + 1)), f"t{k}")
                    e.wait_ge(s_w, n_w)
                    V.wait(e, f"x0{k}")
                    A.wait(e, f"x1{k}")
                    if k >= 2:
                        A.wait(e, f"silu{k - 2}")
                    S.done(self.token_major(e, XT[:, :, k * BLK:(k + 1) * BLK], Wg, (4 + 2 * (k % 2), 5 + 2 * (k % 2))), f"g{k}")
            @block.vector
            def _(e):
                V.start(e)
                for k in range(NB):
                    S.wait(e, f"t{k}")
                    V.done(e.tensor_copy(XT[:, 0, k * BLK:(k + 1) * BLK], PS[:, 2 * (k % 2), :]), f"x0{k}")
                for kt in range(KD):
                    e.wait_ge(s_w, n_w)
                    V.done(e.tensor_copy(WvB[:, kt, :, :, :],
                                         Wv[:, kt, :].rearrange("p (h j) -> p j h", j=HD).unsqueeze(3).broadcast_to((P, HD, H, DK))),
                           f"wv{kt}")
                for k in range(NB):
                    A.wait(e, f"silu{k}")
                    g = G[:, k * TB:(k + 1) * TB, :].rearrange("p t (h j) -> p (t h) j", j=HD)
                    V.done(e.tensor_tensor(g, g, gnw[:, :].unsqueeze(1).broadcast_to((P, TB * H, HD)), ALU.mult), f"gn{k}")
            @block.scalar
            def _(e):
                A.start(e)
                for k in range(NB):
                    S.wait(e, f"t{k}")
                    A.done(e.activation(XT[:, 1, k * BLK:(k + 1) * BLK], PS[:, 2 * (k % 2) + 1, :], ACT.Copy), f"x1{k}")
                    S.wait(e, f"g{k}")
                    A.done(e.activation(G[:, k * TB:(k + 1) * TB, :], self.pair_banks(4 + 2 * (k % 2)), ACT.Silu), f"silu{k}")

    def gla_gates(self, c, c3):
        nc, PS, XT = self.nc, self.PS, self.XT
        sb = lambda n, s, dt=F32: self.sb(c, n, s, dt)
        self.QT, self.KT, self.decay = sb("QT", [P, N]), sb("KT", [P, N]), sb("decay", [P, N])
        sb = lambda n, s, dt=F32: self.sb(c3, n, s, dt)
        lowT, z, az, lz, u = sb("lowT", [LOW, BLK]), sb("z", [P, BLK]), sb("az", [P, BLK]), sb("lz", [P, BLK]), sb("u", [P, BLK])
        S = self.steps("gg_pe", ["low", "q", "k", "z"])
        A = self.steps("gg_act", ["low", "z", "abs", "q", "exp", "ln", "decay"])
        V = self.steps("gg_dve", ["k", "u"])
        with nc.Block() as block:
            @block.sync
            def _(e):
                self.load_indices(e)
            @block.gpsimd
            def _(e):
                self.cross_constants(e)
            @block.tensor
            def _(e):
                S.start(e)
                with e.Fori(0, NB) as i:
                    x = lambda kt: XT[:, kt, bass.ds(i * BLK, BLK)]
                    A.wait_before(e, i)
                    V.wait_before(e, i)
                    for name, w, bank, m in (("low", self.Wgk1, 0, LOW), ("q", self.Wq, 1, P), ("k", self.Wk, 2, P)):
                        for kt in range(KD):
                            last = e.matmul(PS[0:m, bank, :], w[:, kt, :], x(kt), start=kt == 0, stop=kt == KD - 1)
                        S.done(last, name)
                    A.wait(e, "low", i)
                    S.done(e.matmul(PS[:, 3, :], self.Wgk2[:, :], lowT[:, :], start=True, stop=True), "z")
            @block.scalar
            def _(e):
                A.start(e)
                with e.Fori(0, NB) as i:
                    cols = bass.ds(i * BLK, BLK)
                    S.wait(e, "low", i)
                    A.done(e.activation(lowT[:, :], PS[0:LOW, 0, :], ACT.Copy), "low")
                    S.wait(e, "z", i)
                    A.done(e.activation(z[:, :], PS[:, 3, :], ACT.Identity, bias=self.bgk2[:, 0:1]), "z")
                    A.wait(e, "z", i)
                    A.done(e.activation(az[:, :], z[:, :], ACT.Abs), "abs")
                    A.done(e.activation(self.QT[:, cols], PS[:, 1, :], ACT.Copy, scale=DK ** -0.5), "q")
                    A.wait(e, "abs", i)
                    A.done(e.activation(az[:, :], az[:, :], ACT.Exp, scale=-1.0), "exp")
                    A.wait(e, "exp", i)
                    A.done(e.activation(lz[:, :], az[:, :], ACT.Ln, bias=1.0), "ln")
                    V.wait(e, "u", i)
                    A.done(e.activation(self.decay[:, cols], u[:, :], ACT.Exp, scale=1.0 / 16.0), "decay")
            @block.vector
            def _(e):
                V.start(e)
                with e.Fori(0, NB) as i:
                    S.wait(e, "k", i)
                    V.done(e.tensor_copy(self.KT[:, bass.ds(i * BLK, BLK)], PS[:, 2, :]), "k")
                    A.wait(e, "ln", i)
                    V.done(e.scalar_tensor_tensor(out=u[:, :], in0=z[:, :], scalar=0.0, in1=lz[:, :], op0=ALU.min,
                                                  op1=ALU.subtract), "u")

    def gla_scan(self, c):
        nc, PS, XT = self.nc, self.PS, self.XT
        sb = lambda n, s, dt=F32: self.sb(c, n, s, dt)
        self.O = O = sb("O", [P, NT, D])
        with ExitStack() as c2:
            sb2 = lambda n, s, dt=F32: self.sb(c2, n, s, dt)
            kv, hs = sb2("kv", [P, 2, T]), sb2("hs", [P, 2, T])
            R = 6
            qh = sb2("qh", [P, R, T])
            OT = sb2("OT", [P, 4, T])
            TBt = T // P
            S = self.steps("gs_pe", self.scan_pe_order())
            V = self.steps("gs_dve", [n for j in range(HD) for n in (f"kv{j}", f"h{j}", f"qh{j}")])
            A = self.steps("gs_act", [f"o{g}" for g in range(4)] + [f"tok{t}" for t in range(TBt)])
            with nc.Block() as block:
                @block.tensor
                def _(e):
                    S.start(e)
                    with e.Fori(0, B) as i:
                        def values(j):
                            if j >= 2:
                                V.wait(e, f"kv{j - 2}", i)
                            for half in range(2):
                                for kt in range(KD):
                                    last = e.matmul(PS[:, 2 * (j % 2) + half, :],
                                                    self.WvB[:, kt, j, :, :].rearrange("p h k -> p (h k)"),
                                                    XT[:, kt, bass.ds(i * T + half * BLK, BLK)], start=kt == 0, stop=kt == KD - 1)
                            S.done(last, f"v{j}")
                        def sums(g):
                            V.wait(e, f"qh{4 * g + 3}", i)
                            if g:
                                A.wait(e, f"o{g - 1}", i)
                            for half in range(2):
                                for r in range(4):
                                    last = e.matmul(PS[32 * r:32 * r + 32, 4 + half, :], self.headsum[:, :],
                                                    qh[:, (4 * g + r) % R, half * BLK:(half + 1) * BLK], start=True, stop=True)
                            S.done(last, f"s{g}")
                        def turn(t):
                            A.wait(e, "o3", i)
                            if t >= 2:
                                A.wait(e, f"tok{t - 2}", i)
                            for g in range(4):
                                last = e.transpose(PS[:, 6 + t % 2, g * P:(g + 1) * P], OT[:, g, t * P:(t + 1) * P], self.ident[:, :])
                            S.done(last, f"t{t}")
                        for name in self.scan_pe_order():
                            {"v": values, "s": sums, "t": turn}[name[0]](int(name[1:]))
                @block.vector
                def _(e):
                    V.start(e)
                    with e.Fori(0, B) as i:
                        cols = bass.ds(i * T, T)
                        for j in range(HD):
                            S.wait(e, f"v{j}", i)
                            if j >= 2:
                                V.wait(e, f"h{j - 2}", i)
                            V.done(e.tensor_tensor(kv[:, j % 2, :], PS[:, 2 * (j % 2):2 * (j % 2) + 2, :].rearrange("p b n -> p (b n)"),
                                                   self.KT[:, cols], ALU.mult), f"kv{j}")
                            V.wait(e, f"kv{j}", i)
                            V.done(e.tensor_tensor_scan(hs[:, j % 2, :], self.decay[:, cols], kv[:, j % 2, :], 0.0,
                                                        ALU.mult, ALU.add), f"h{j}")
                            V.wait(e, f"h{j}", i)
                            if j >= R:
                                S.wait(e, f"s{(j - R) // 4}", i)
                            V.done(e.tensor_tensor(qh[:, j % R, :], hs[:, j % 2, :], self.QT[:, cols], ALU.mult), f"qh{j}")
                @block.scalar
                def _(e):
                    A.start(e)
                    with e.Fori(0, B) as i:
                        for g in range(4):
                            S.wait(e, f"s{g}", i)
                            A.done(e.activation(OT[:, g, :], PS[:, 4:6, :].rearrange("p b n -> p (b n)"), ACT.Copy), f"o{g}")
                        for t in range(TBt):
                            S.wait(e, f"t{t}", i)
                            A.done(e.activation(O[:, i * TBt + t, :].rearrange("p (h j) -> p h j", j=HD),
                                                PS[:, 6 + t % 2, :].rearrange("p (j h) -> p h j", h=32)[:, 0:H, :], ACT.Copy), f"tok{t}")

    def scan_pe_order(self):
        order = ["v0", "v1"]
        for j in range(HD):
            if j % 4 == 3:
                order.append(f"s{j // 4}")
            if j + 2 < HD:
                order.append(f"v{j + 2}")
        return order + [f"t{t}" for t in range(T // P)]

    def gla_out(self, c):
        idxT, cid, win, L = self.idxT, self.cid, self.win, self.L
        nc, PS, X, O, G = self.nc, self.PS, self.X, self.O, self.G
        sb = lambda n, s, dt=F32: self.sb(c, n, s, dt)
        og, ogT, y = sb("og", [P, TB, D]), sb("ogT", [P, KD, BLK]), sb("y", [P, TB, D])
        ms, lm, rs = sb("ms", [P, TB * H]), sb("lm", [P, TB * H]), sb("rs", [P, TB * H])
        st, mv, lv, rstd = sb("st", [P, TB, 6]), sb("mv", [P, TB, 2]), sb("lv", [P, TB]), sb("rstd", [P, TB])
        S = self.steps("go_pe", ["turn", "wo"])
        A = self.steps("go_act", ["sq", "lnms", "rs", "ogT1", "rstd_ln", "rstd"])
        V = self.steps("go_dve", ["ms", "norm", "gate", "ogT0", "y", "stats", "stats_mv", "out"])
        R = 8
        assert NB * 4 * 4 == NCTX
        hot, cntT = sb("c_hot", [P, R, T], BF16), sb("c_cntT", [P, T])
        lc, none = sb("c_lc", [P, T // P, P]), sb("c_none", [P, T // P, P])
        CS = self.steps("cc_pe", [f"c{r}" for r in range(R)], before=["zero"])
        CS2 = self.steps("cc_pe2", ["turn"])
        CV = self.steps("cc_dve", [f"hot{r}" for r in range(R)])
        CV2 = self.steps("cc_dve2", ["cnt", "least", "none", "L"])
        CA2 = self.steps("cc_act2", ["ln"])
        def hots(e, i, g):
            it = i * 2 + g // 2
            CS.wait_before(e, it)
            for r in range(4 * (g % 2), 4 * (g % 2) + 4):
                CV.done(e.tensor_scalar(hot[:, r, :], idxT[:, :], cid[:, bass.ds(it * R + r, 1)], None, ALU.is_equal), f"hot{r}")
        def counts(e, i, g):
            it = i * 2 + g // 2
            for r in range(4 * (g % 2), 4 * (g % 2) + 4):
                CV.wait(e, f"hot{r}", it)
                for b in range(2):
                    last = e.matmul(PS[:, 6 + b, :], win[:, bass.ds(it * R + r + P - NCTX, P)], hot[:, r, b * BLK:(b + 1) * BLK],
                                    start=False, stop=False, skip_group_check=True)
                CS.done(last, f"c{r}")
        with nc.Block() as block:
            @block.tensor
            def _(e):
                S.start(e)
                CS.start(e)
                CS2.start(e)
                for b in range(2):
                    last = e.matmul(PS[:, 6 + b, :], win[:, 2 * P:3 * P], idxT[:, b * BLK:(b + 1) * BLK], start=True, stop=False, skip_group_check=True)
                CS.done(last, "zero")
                with e.Fori(0, NB) as i:
                    counts(e, i, 0)
                    V.wait(e, "gate", i)
                    S.done(self.transposes(e, og, 0, (0, 1)), "turn")
                    counts(e, i, 1)
                    V.wait(e, "ogT0", i)
                    A.wait(e, "ogT1", i)
                    S.done(self.token_major(e, ogT, self.Wo, (2, 3)), "wo")
                    counts(e, i, 2)
                    counts(e, i, 3)
                CV2.wait(e, "cnt")
                for t in range(T // P):
                    last = e.transpose(PS[:, 4 + t // 4, (t % 4) * P:(t % 4 + 1) * P], cntT[:, t * P:(t + 1) * P], self.ident[:, :])
                CS2.done(last, "turn")
            @block.scalar
            def _(e):
                A.start(e)
                CA2.start(e)
                with e.Fori(0, NB) as i:
                    S.wait_before(e, i)
                    A.done(e.activation(og[:, :, :], O[:, bass.ds(i * TB, TB), :], ACT.Square), "sq")
                    V.wait(e, "ms", i)
                    A.done(e.activation(lm[:, :], ms[:, :], ACT.Ln, scale=1.0 / HD, bias=self.eps[:, 0:1]), "lnms")
                    A.wait(e, "lnms", i)
                    A.done(e.activation(rs[:, :], lm[:, :], ACT.Exp, scale=-0.5), "rs")
                    S.wait(e, "turn", i)
                    A.done(e.activation(ogT[:, 1, :], PS[:, 1, :], ACT.Copy), "ogT1")
                    self.norm_rstd(e, A, V, i, mv, lv, rstd)
                CV2.wait(e, "least")
                CV2.wait(e, "none")
                CA2.done(e.activation(lc[:, :, :], lc[:, :, :], ACT.Ln), "ln")
            @block.vector
            def _(e):
                V.start(e)
                CV.start(e)
                CV2.start(e)
                with e.Fori(0, NB) as i:
                    tiles = bass.ds(i * TB, TB)
                    byhead = lambda x: x.rearrange("p t (h j) -> p (t h) j", j=HD)
                    A.wait(e, "sq", i)
                    V.done(e.tensor_reduce(ms[:, :], byhead(og[:, :, :]), AX.X, ALU.add), "ms")
                    hots(e, i, 0)
                    A.wait(e, "rs", i)
                    V.done(e.tensor_tensor(byhead(og[:, :, :]), byhead(O[:, tiles, :]),
                                           rs[:, :].unsqueeze(2).broadcast_to((P, TB * H, HD)), ALU.mult), "norm")
                    V.wait(e, "norm", i)
                    V.done(e.tensor_tensor(og[:, :, :], og[:, :, :], G[:, tiles, :], ALU.mult), "gate")
                    hots(e, i, 1)
                    S.wait(e, "turn", i)
                    V.done(e.tensor_copy(ogT[:, 0, :], PS[:, 0, :]), "ogT0")
                    hots(e, i, 2)
                    S.wait(e, "wo", i)
                    V.done(e.tensor_tensor(y[:, :, :], self.pair_banks(2), X[:, tiles, :], ALU.add), "y")
                    V.wait(e, "y", i)
                    self.norm_stats(e, V, i, y, st, mv)
                    hots(e, i, 3)
                    A.wait(e, "rstd", i)
                    for t in range(TB):
                        last = e.tensor_scalar(X[:, i * TB + t, :], y[:, t, :], mv[:, t, 0:1], rstd[:, t:t + 1],
                                               ALU.subtract, ALU.mult)
                    V.done(last, "out")
                CS.wait(e, f"c{R - 1}", NCTX // R - 1)
                CV2.done(e.tensor_copy(cntT[:, :], PS[:, 6:8, :].rearrange("p b n -> p (b n)")), "cnt")
                CS2.wait(e, "turn")
                cnt = PS[:, 4:6, :].rearrange("p b (t n) -> p (b t) n", n=P)
                CV2.done(e.tensor_scalar(lc[:, :, :], cnt, 1.0, None, ALU.max), "least")
                CV2.done(e.tensor_scalar(none[:, :, :], cnt, 1.0, 1.0, ALU.min, ALU.subtract), "none")
                CA2.wait(e, "ln")
                CV2.wait(e, "none")
                for b in range(B):
                    last = e.scalar_tensor_tensor(out=L[:, b, :, :], in0=none[:, :, b * NCTX:(b + 1) * NCTX], scalar=-MASKED,
                                                  in1=lc[:, :, b * NCTX:(b + 1) * NCTX], op0=ALU.mult, op1=ALU.add)
                CV2.done(last, "L")


    def cross_buffers(self, c, c2):
        sb = lambda n, s, dt=F32: self.sb(c, n, s, dt)
        self.WqT, self.WoutT = sb("c_WqT", [P, KD, D]), sb("c_WoutT", [P, KD, D])
        self.Kblk = sb("c_Kblk", [P, B, KD, HG, NCTX])
        self.Vblk = sb("c_Vblk", [P, B, H // 2, 2, HD])
        self.half = sb("c_half", [P, 2, HD])
        self.selaug = sb("c_selaug", [P, H // 2, 2, NCTX])
        self.L = sb("c_L", [P, B, T // P, NCTX])
        sb2 = lambda n, s, dt=F32: self.sb(c2, n, s, dt)
        self.wq, self.wout, self.up, self.down = sb2("c_wq", [P, KD, D]), sb2("c_wout", [P, KD, D]), sb2("c_up", [P, 4, LAT]), sb2("c_down", [P, 1, D])
        self.ctx, self.upT, self.downT, self.ctxT = sb2("c_ctx", [P, 1, D]), sb2("c_upT", [P, 1, 4 * P]), sb2("c_downT", [P, KD, P]), sb2("c_ctxT", [P, KD, P])
        self.m16 = sb2("c_m16", [P, HG])
        self.idx = sb2("c_idx", [P, T // P, B, NSEL], I32)
        self.idxT = sb2("c_idxT", [P, T], BF16)
        self.cid = sb2("c_cid", [P, NCTX])
        self.win = sb2("c_win", [P, 3 * P], BF16)
        self.s_i, self.s_cw = self.sem("c_i"), self.sem("c_w")
        self.C = self.steps("cs_pool", ["z1", "z2", "z3", "z4", "z5", "cid", "m16a", "half_a", "w1", "sa1", "m16b", "half_b", "w2", "sa2"])

    def load_indices(self, e):
        a, idx, s_i = self.a, self.idx, self.s_i
        for b in range(B):
            e.dma_start(idx[:, :, b, :], a["itok_BxSx64_0_2047"][b].rearrange("(t p) k -> p t k", p=P)).then_inc(s_i, 16)
            e.wait_ge(s_i, 16 * (b + 1))

    def cross_constants(self, e):
        a, C, s_w, m16, half, win, selaug, cid = self.a, self.C, self.s_cw, self.m16, self.half, self.win, self.selaug, self.cid
        C.start(e)
        for t, w in ((self.wq, "L0_xattn_W_q"), (self.wout, "L0_xattn_W_out"), (self.up, "L0_xattn_W_kv_up"), (self.down, "L0_xattn_W_kv_down")):
            e.dma_start(t[:, :, :], a[w].rearrange("(k p) n -> p k n", p=P)).then_inc(s_w, 16)
        e.dma_start(self.ctx[:, 0, :], a["ctx_1024"].rearrange("b c d -> (b c) d")).then_inc(s_w, 16)
        C.done(e.memset(m16[:, :], 1.0), "z1")
        C.done(e.memset(half[:, :, :], 1.0), "z2")
        C.done(e.memset(win[:, :], 0.0), "z3")
        C.done(e.memset(selaug[:, :, :, :], 0.0), "z4")
        C.done(e.memset(cid[:, :], 0.0), "z5")
        C.wait(e, "z5")
        C.done(e.iota(cid[:, :], pattern=[[-1, NCTX]], base=NCTX - 1, channel_multiplier=0, allow_small_or_imprecise_dtypes=True), "cid")
        sel = lambda t, op, fill, base, pattern, cm: e.affine_select(out=t, in_=t, compare_op=op, fill=fill, base=base,
                                                                     pattern=pattern, channel_multiplier=cm)
        C.done(sel(m16[:, :], ALU.is_ge, 0.0, 0, [[-HD, HG]], 1), "m16a")
        C.done(sel(half[:, :, :], ALU.is_ge, 0.0, 0, [[-NCTX, 2], [0, HD]], 1), "half_a")
        C.wait(e, "half_a")
        C.done(sel(win[0:NCTX, :], ALU.not_equal, 1.0, -(P - 1), [[1, 3 * P]], 0), "w1")
        C.wait(e, "w1")
        C.done(sel(selaug[:, :, :, :], ALU.not_equal, 1.0, 0, [[0, H // 2], [0, 2], [-1, NCTX]], 1), "sa1")
        C.wait(e, "sa1")
        C.done(sel(m16[:, :], ALU.is_ge, 0.0, HD - 1, [[HD, HG]], -1), "m16b")
        C.done(sel(half[:, :, :], ALU.is_ge, 0.0, NCTX - 1, [[NCTX, 2], [0, HD]], -1), "half_b")
        C.wait(e, "half_b")
        C.done(sel(win[NCTX:P, :], ALU.not_equal, 1.0, -(P - 1 + NCTX), [[1, 3 * P]], 0), "w2")
        C.wait(e, "w2")
        C.done(sel(selaug[:, :, :, :], ALU.not_equal, 1.0, -NCTX, [[-2, H // 2], [-1, 2], [0, NCTX]], 1), "sa2")

    def cross_setup(self):
        nc, PS = self.nc, self.PS
        WqT, WoutT, Kblk, Vblk, half = self.WqT, self.WoutT, self.Kblk, self.Vblk, self.half
        wq, wout, up, down, ctx, upT, downT, ctxT = self.wq, self.wout, self.up, self.down, self.ctx, self.upT, self.downT, self.ctxT
        m16, idx, idxT, s_i, s_w, C = self.m16, self.idx, self.idxT, self.s_i, self.s_cw, self.C
        with ExitStack() as c3:
            sb = lambda n, s, dt=F32: self.sb(c3, n, s, dt)
            ckv, ckv2 = sb("c_ckv", [P, P]), sb("c_ckv2", [P, B, 2, NCTX])
            f, f2 = sb("c_f", [P, T // P, B * NSEL]), sb("c_f2", [P, T // P, B * NSEL])
            turned = [("wq", wq, WqT, 2, 2), ("wout", wout, WoutT, 2, 2), ("up", up, upT, 4, 1), ("down", down, downT, 1, 2), ("ctx", ctx, ctxT, 1, 2)]
            S = self.steps("cs_pe", [n for n, *_ in turned] + ["ckv", "k", "v0", "v1", "idx"])
            A = self.steps("cs_act", [n for n, *_ in turned] + ["v0", "v1"])
            V = self.steps("cs_dve", ["neg", "wrap", "clamp", "ckv", "ckv2", "k", "idxT", "vb0", "vb1"])
            with nc.Block() as block:
                @block.tensor
                def _(e):
                    S.start(e)
                    e.wait_ge(s_w, 16 * 5)
                    for n, (name, src, dst, rows, cols) in enumerate(turned):
                        if n >= 2:
                            A.wait(e, turned[n - 2][0])
                        for k in range(cols):
                            for r in range(rows):
                                last = e.transpose(PS[:, 2 * (n % 2) + (k * rows + r) // 4, ((k * rows + r) % 4) * P:((k * rows + r) % 4 + 1) * P],
                                                   src[:, r, k * P:(k + 1) * P], self.ident[:, :])
                        S.done(last, name)
                    A.wait(e, "ctx")
                    for kt in range(KD):
                        last = e.matmul(PS[:, 4, 0:P], downT[:, kt, :], ctxT[:, kt, :], start=kt == 0, stop=kt == KD - 1)
                    S.done(last, "ckv")
                    V.wait(e, "ckv")
                    for g in range(KD):
                        last = e.matmul(PS[:, 5, g * P:(g + 1) * P], upT[:, 0, g * P:(g + 1) * P], ckv[:, :], start=True, stop=True)
                    S.done(last, "k")
                    V.wait(e, "ckv2")
                    for b in range(B):
                        S.done(e.matmul(PS[:, 6 + b, 0:D], ckv2[:, b, :, :].rearrange("p a c -> p (a c)"), upT[:, 0, D:2 * D],
                                        start=True, stop=True), f"v{b}")
                    V.wait(e, "clamp")
                    for t in range(T // P):
                        last = e.transpose(PS[:, t // 4, (t % 4) * P:(t % 4 + 1) * P], f[:, t, :], self.ident[:, :])
                    S.done(last, "idx")
                @block.scalar
                def _(e):
                    A.start(e)
                    for n, (name, src, dst, rows, cols) in enumerate(turned):
                        S.wait(e, name)
                        A.done(e.activation(dst[:, :, :].rearrange("p k n -> p (k n)"), PS[:, 2 * (n % 2), 0:rows * cols * P], ACT.Copy), name)
                    for b in range(B):
                        S.wait(e, f"v{b}")
                        C.wait(e, "half_b")
                        A.done(e.activation(Vblk[:, b, :, :, :].rearrange("p a c d -> p (a c d)"), PS[:, 6 + b, 0:D], ACT.Copy), f"v{b}")
                @block.vector
                def _(e):
                    V.start(e)
                    e.wait_ge(s_i, 16 * B)
                    idx_ = idx[:, :, :, :].rearrange("p t b k -> p t (b k)")
                    V.done(e.tensor_scalar(f2[:, :, :], idx_, 0.0, float(NCTX), ALU.is_lt, ALU.mult), "neg")
                    V.wait(e, "neg")
                    V.done(e.tensor_tensor(f[:, :, :], f2[:, :, :], idx_, ALU.add), "wrap")
                    V.wait(e, "wrap")
                    V.done(e.tensor_scalar(f[:, :, :], f[:, :, :], 0.0, float(NCTX - 1), ALU.max, ALU.min), "clamp")
                    C.wait(e, "sa2")
                    S.wait(e, "ckv")
                    V.done(e.tensor_copy(ckv[:, :], PS[:, 4, 0:P]), "ckv")
                    V.wait(e, "ckv")
                    V.done(e.tensor_copy(ckv2[:, :, :, :], ckv[:, :].rearrange("p (b c) -> p b c", b=B).unsqueeze(2).broadcast_to((P, B, 2, NCTX))), "ckv2")
                    S.wait(e, "k")
                    for b in range(B):
                        for g in range(KD):
                            last = e.tensor_tensor(Kblk[:, b, g, :, :],
                                                   PS[:, 5, g * P + b * NCTX:g * P + (b + 1) * NCTX].unsqueeze(1).broadcast_to((P, HG, NCTX)),
                                                   m16[:, :].unsqueeze(2).broadcast_to((P, HG, NCTX)), ALU.mult)
                    V.done(last, "k")
                    S.wait(e, "idx")
                    V.done(e.tensor_copy(idxT[:, :], PS[:, 0:2, :].rearrange("p b n -> p (b n)")), "idxT")
                    for b in range(B):
                        A.wait(e, f"v{b}")
                        V.done(e.tensor_tensor(Vblk[:, b, :, :, :].rearrange("p a c d -> p a (c d)"), Vblk[:, b, :, :, :].rearrange("p a c d -> p a (c d)"),
                                               half[:, :, :].rearrange("p c d -> p (c d)").unsqueeze(1).broadcast_to((P, H // 2, 2 * HD)), ALU.mult), f"vb{b}")

    def cross_blocks(self, c):
        nc, PS, X, L = self.nc, self.PS, self.X, self.L
        sb = lambda n, s, dt=F32: self.sb(c, n, s, dt)
        xs, xT, qT = sb("xs", [P, TB, D]), sb("xT", [P, KD, BLK]), sb("qT", [P, KD, BLK])
        aug, augT = sb("aug", [P, TB, P]), sb("augT", [P, BLK])
        pr = sb("pr", [P, H // 2, BLK])
        rs, oT, y = sb("c_rs", [P, KD, BLK]), sb("c_oT", [P, KD, BLK]), sb("c_y", [P, TB, D])
        st, mv, lv, rstd = sb("c_st", [P, TB, 6]), sb("c_mv", [P, TB, 2]), sb("c_lv", [P, TB]), sb("c_rstd", [P, TB])
        NP_ = H // 2
        for b in range(B):
            s_z = self.sem(f"cb_z{b}")
            S = self.steps(f"cb_pe{b}", ["turn", "q"] + [f"s{t}" for t in range(TB)] + ["aug"] + [f"e{k}" for k in range(4)] + ["pv0"]
                           + [f"e{k}" for k in range(4, 8)] + ["pv1", "wo"])
            A = self.steps(f"cb_act{b}", ["xs", "xT1", "q1", "augT"] + [f"p{k}" for k in range(4)] + ["ls0", "rs0"]
                           + [f"p{k}" for k in range(4, 8)] + ["ls1", "rs1", "rstd_ln", "rstd"])
            V = self.steps(f"cb_dve{b}", ["L", "xT0", "q0"] + [f"m{t}" for t in range(TB)] + ["o0", "o1", "y", "stats", "stats_mv", "out"])
            with nc.Block() as block:
                @block.gpsimd
                def _(e):
                    e.memset(aug[:, :, NCTX + H:P], 0.0).then_inc(s_z, 1)
                @block.tensor
                def _(e):
                    S.start(e)
                    with e.Fori(0, T // BLK) as i:
                        A.wait(e, "xs", i)
                        V.wait_before(e, i)
                        S.done(self.transposes(e, xs, 0, (0, 1)), "turn")
                        V.wait(e, "xT0", i)
                        A.wait(e, "xT1", i)
                        for g in range(KD):
                            for kt in range(KD):
                                last = e.matmul(PS[:, 2 + g, :], self.WqT[:, kt, g * P:(g + 1) * P], xT[:, kt, :], start=kt == 0, stop=kt == KD - 1)
                        S.done(last, "q")
                        V.wait(e, "q0", i)
                        A.wait(e, "q1", i)
                        for t in range(TB):
                            if t >= 2:
                                V.wait(e, f"m{t - 2}", i)
                            for g in range(KD):
                                bank = PS[:, 4 + 2 * (t % 2) + g, :]
                                e.matmul(bank, qT[:, g, t * P:(t + 1) * P], self.Kblk[:, b, g, :, :].rearrange("p h c -> p (h c)"), start=True, stop=False)
                                last = e.matmul(bank, self.ident[:, :], aug[:, t, 0:NCTX].unsqueeze(1).broadcast_to((P, HG, NCTX)), start=False, stop=True)
                            S.done(last, f"s{t}")
                        V.wait(e, f"m{TB - 1}", i)
                        e.wait_ge(s_z, 1)
                        for t in range(TB):
                            last = e.transpose(PS[:, 0, t * P:(t + 1) * P], aug[:, t, :], self.ident[:, :])
                        S.done(last, "aug")
                        A.wait(e, "augT", i)
                        for k in range(NP_):
                            if k >= 4:
                                A.wait(e, f"p{k - 4}", i)
                            g = k // 4
                            e.matmul(PS[:, 4 + k % 4, :], self.Kblk[:, b, g, 2 * (k % 4):2 * (k % 4) + 2, :].rearrange("p h c -> p (h c)"),
                                     qT[:, g, :], start=True, stop=False)
                            S.done(e.matmul(PS[:, 4 + k % 4, :], self.selaug[:, k, :, :].rearrange("p h c -> p (h c)"), augT[:, :],
                                            start=False, stop=True), f"e{k}")
                            if k % 4 == 3:
                                A.wait(e, f"p{k}", i)
                                for r in range(4):
                                    e.matmul(PS[32 * r:32 * r + 32, g, :], self.Vblk[:, b, 4 * g + r, :, :].rearrange("p h d -> p (h d)"),
                                             pr[:, 4 * g + r, :], start=True, stop=True)
                                for r in range(4):
                                    last = e.matmul(PS[32 * r:32 * r + 32, 2 + g, :], self.half[:, :, :].rearrange("p h d -> p (h d)"),
                                                    pr[:, 4 * g + r, :], start=True, stop=True)
                                S.done(last, f"pv{g}")
                        V.wait(e, "o1", i)
                        S.done(self.token_major(e, oT, self.WoutT, (4, 5)), "wo")
                @block.scalar
                def _(e):
                    A.start(e)
                    with e.Fori(0, T // BLK) as i:
                        S.wait_before(e, i)
                        A.done(e.activation(xs[:, :, :], X[:, bass.ds(b * (T // P) + i * TB, TB), :], ACT.Copy), "xs")
                        S.wait(e, "turn", i)
                        A.done(e.activation(xT[:, 1, :], PS[:, 1, :], ACT.Copy), "xT1")
                        S.wait(e, "q", i)
                        A.done(e.activation(qT[:, 1, :], PS[:, 3, :], ACT.Copy, scale=HD ** -0.5), "q1")
                        S.wait(e, "aug", i)
                        A.done(e.activation(augT[:, :], PS[:, 0, :], ACT.Copy), "augT")
                        for k in range(NP_):
                            S.wait(e, f"e{k}", i)
                            A.done(e.activation(pr[:, k, :], PS[:, 4 + k % 4, :], ACT.Exp), f"p{k}")
                            if k % 4 == 3:
                                g = k // 4
                                S.wait(e, f"pv{g}", i)
                                A.done(e.activation(rs[:, g, :], PS[:, 2 + g, :], ACT.Ln), f"ls{g}")
                                A.wait(e, f"ls{g}", i)
                                A.done(e.activation(rs[:, g, :], rs[:, g, :], ACT.Exp, scale=-1.0), f"rs{g}")
                        self.norm_rstd(e, A, V, i, mv, lv, rstd)
                @block.vector
                def _(e):
                    V.start(e)
                    with e.Fori(0, T // BLK) as i:
                        S.wait_before(e, i)
                        V.done(e.tensor_copy(aug[:, :, 0:NCTX], L[:, b, bass.ds(i * TB, TB), :]), "L")
                        S.wait(e, "turn", i)
                        V.done(e.tensor_copy(xT[:, 0, :], PS[:, 0, :]), "xT0")
                        S.wait(e, "q", i)
                        V.done(e.tensor_scalar(qT[:, 0, :], PS[:, 2, :], HD ** -0.5, None, ALU.mult), "q0")
                        for t in range(TB):
                            S.wait(e, f"s{t}", i)
                            V.done(e.tensor_reduce(aug[:, t, NCTX:NCTX + H], PS[:, 4 + 2 * (t % 2):6 + 2 * (t % 2), :].rearrange("p b (h c) -> p (b h) c", c=NCTX),
                                                   AX.X, ALU.max, negate=True), f"m{t}")
                        for g in range(KD):
                            A.wait(e, f"rs{g}", i)
                            V.done(e.tensor_tensor(oT[:, g, :], PS[:, g, :], rs[:, g, :], ALU.mult), f"o{g}")
                        S.wait(e, "wo", i)
                        tile0 = b * (T // P) + i * TB
                        V.done(e.tensor_tensor(y[:, :, :], self.pair_banks(4), X[:, bass.ds(tile0, TB), :], ALU.add), "y")
                        V.wait(e, "y", i)
                        self.norm_stats(e, V, i, y, st, mv)
                        A.wait(e, "rstd", i)
                        for t in range(TB):
                            last = e.tensor_scalar(X[:, tile0 + t, :], y[:, t, :], mv[:, t, 0:1], rstd[:, t:t + 1], ALU.subtract, ALU.mult)
                        V.done(last, "out")


    def row_norm_affine(self, e, V, A, i, src, dst, st, mv, rstd, gain, bias, tag):
        A.wait(e, "rstd", i)
        for t in range(TB):
            last = e.tensor_scalar(dst[:, t, :], src[:, t, :], mv[:, t, 0:1], rstd[:, t:t + 1], ALU.subtract, ALU.mult)
        V.done(last, tag + "_n")
        V.wait(e, tag + "_n", i)
        V.done(e.tensor_tensor(dst[:, :, :], dst[:, :, :], gain[:, :].unsqueeze(1).broadcast_to((P, TB, D)), ALU.mult), tag + "_g")
        V.wait(e, tag + "_g", i)
        V.done(e.tensor_tensor(dst[:, :, :], dst[:, :, :], bias[:, :].unsqueeze(1).broadcast_to((P, TB, D)), ALU.add), tag)

    def self_attention(self, experts=True):
        nc = self.nc
        self.parts = nc.dram_tensor("qk_parts", (4, B * D, T), F32).ap()
        with ExitStack() as c2:
            self.OT = self.sb(c2, "OT_all", [P, B * H // 4, T])
            with ExitStack() as c3:
                self.V = self.sb(c3, "V", [P, NT, H, 2 * HD])
                self.attend_buffers(c3)
                with ExitStack() as c4:
                    self.qkv(c4)
                with ExitStack() as c4:
                    self.attend(c4)
            self.expert_buffers(c2)
            with ExitStack() as c3:
                self.route(c3)
            if experts:
                with ExitStack() as c3:
                    self.experts(c3)

    def qkv(self, c):
        nc, a, PS, X, V_ = self.nc, self.a, self.PS, self.X, self.V
        sb = lambda n, s, dt=F32: self.sb(c, n, s, dt)
        Wq, Wk, Wv = sb("f_Wq", [P, KD, D]), sb("f_Wk", [P, KD, D]), sb("f_Wv", [P, KD, D])
        g1, b1, bv = sb("f_g1", [P, D]), sb("f_b1", [P, D]), sb("f_bv", [P, D])
        bq, bk, bqs = sb("f_bq", [P, KD]), sb("f_bk", [P, KD]), sb("f_bqs", [P, KD])
        h, hT = sb("f_h", [P, TB, D]), sb("f_hT", [P, KD, BLK])
        qf, kf = sb("f_q", [P, KD, BLK]), sb("f_k", [P, KD, BLK])
        part = [sb(n, [P, KD, BLK], F32R) for n in ("f_qhi", "f_qlo", "f_khi", "f_klo")]
        st, mv, lv, rstd = sb("f_st", [P, TB, 6]), sb("f_mv", [P, TB, 2]), sb("f_lv", [P, TB]), sb("f_rstd", [P, TB])
        s_w, s_st, s_z, s_k, s_b = self.sem("f_w"), self.sem("f_store"), self.sem("f_z"), self.sem("f_const"), self.sem("f_b")
        S = self.steps("f_pe", ["turn", "q", "k", "v"])
        A = self.steps("f_act", ["hT1", "q", "k"])
        V = self.steps("f_dve", ["hT0", "qhi", "qlo", "khi", "klo", "v"])
        AN = self.steps("f_nact", ["rstd_ln", "rstd"])
        VN = self.steps("f_ndve", ["stats", "stats_mv", "h_n", "h_g", "h"])
        n_w = 16 * 8
        with nc.Block() as block:
            @block.gpsimd
            def _(e):
                for t, w in ((Wq, "Wq"), (Wk, "Wk"), (Wv, "Wv")):
                    e.dma_start(t[:, :, :], a["L0_ffn_" + w].rearrange("(k p) n -> p k n", p=P)).then_inc(s_w, 16)
                for t, w in ((g1, "ln1_g"), (b1, "ln1_b"), (bv, "bv")):
                    e.dma_start(t[:, :], a["L0_ffn_" + w].partition_broadcast(P)).then_inc(s_w, 16)
                for t, w in ((bq, "bq"), (bk, "bk")):
                    e.dma_start(t[:, :], a["L0_ffn_" + w].rearrange("(k p) -> p k", p=P), allow_slow_non_contiguous=True).then_inc(s_w, 16)
                e.memset(V_[:, :, :, HD:2 * HD], 1.0).then_inc(s_z, 1)
                self.attend_constants(e, s_k)
            @block.tensor
            def _(e):
                S.start(e)
                e.wait_ge(s_w, n_w)
                with e.Fori(0, NB) as i:
                    VN.wait(e, "h", i)
                    V.wait_before(e, i)
                    A.wait_before(e, i)
                    S.done(self.transposes(e, h, 0, (0, 1)), "turn")
                    V.wait(e, "hT0", i)
                    A.wait(e, "hT1", i)
                    for name, w, bank in (("q", Wq, 2), ("k", Wk, 4)):
                        for g in range(KD):
                            for kt in range(KD):
                                last = e.matmul(PS[:, bank + g, :], w[:, kt, g * P:(g + 1) * P], hT[:, kt, :], start=kt == 0, stop=kt == KD - 1)
                        S.done(last, name)
                    S.done(self.token_major(e, hT, Wv, (6, 7)), "v")
            @block.scalar
            def _(e):
                A.start(e)
                e.wait_ge(s_w, n_w)
                e.activation(bqs[:, :], bq[:, :], ACT.Copy, scale=HD ** -0.5).then_inc(s_b, 1)
                e.wait_ge(s_b, 1)
                AN.start(e)
                self.norm_rstd(e, AN, VN, 0, mv, lv, rstd)
                with e.Fori(0, NB) as i:
                    S.wait(e, "turn", i)
                    A.done(e.activation(hT[:, 1, :], PS[:, 1, :], ACT.Copy), "hT1")
                    self.norm_rstd(e, AN, VN, i + 1, mv, lv, rstd)
                    for name, dst, bias, bank, scale in (("q", qf, bqs, 2, HD ** -0.5), ("k", kf, bk, 4, 1.0)):
                        S.wait(e, name, i)
                        for g in range(KD):
                            last = e.activation(dst[:, g, :], PS[:, bank + g, :], ACT.Identity, bias=bias[:, g:g + 1], scale=scale)
                        A.done(last, name)
            @block.vector
            def _(e):
                V.start(e)
                e.wait_ge(s_w, n_w)
                VN.start(e)
                def norm(m):
                    blk = m % NB
                    for t in range(TB):
                        last = e.bn_stats(st[:, t, :], X[:, blk * TB + t, :])
                    VN.done(last, "stats")
                    VN.wait_apart(e, "stats", m, self.apart)
                    for t in range(TB):
                        last = e.bn_aggr(mv[:, t, :], st[:, t, :])
                    VN.done(last, "stats_mv")
                    self.row_norm_affine(e, VN, AN, m, X[:, bass.ds(blk * TB, TB), :], h, st, mv, rstd, g1, b1, "h")
                norm(0)
                with e.Fori(0, NB) as i:
                    S.wait(e, "turn", i)
                    V.done(e.tensor_copy(hT[:, 0, :], PS[:, 0, :]), "hT0")
                    norm(i + 1)
                    for n, (name, src) in enumerate((("q", qf), ("k", kf))):
                        hi, lo = part[2 * n], part[2 * n + 1]
                        A.wait(e, name, i)
                        e.wait_ge(s_st, 16 + 16 * 4 * i)
                        V.done(e.tensor_copy(hi[:, :, :], src[:, :, :]), name + "hi")
                        V.wait(e, name + "hi", i)
                        V.done(e.tensor_tensor(lo[:, :, :], src[:, :, :], hi[:, :, :].bitcast(F32), ALU.subtract), name + "lo")
                    S.wait(e, "v", i)
                    e.wait_ge(s_z, 1)
                    V.done(e.tensor_tensor(V_[:, bass.ds(i * TB, TB), :, 0:HD], self.pair_banks(6).rearrange("p t (h d) -> p t h d", h=H),
                                           bv[:, :].rearrange("p (h d) -> p h d", h=H).unsqueeze(1).broadcast_to((P, TB, H, HD)), ALU.add), "v")
            @block.sync
            def _(e):
                e.sem_inc(s_st, 16)
                dst = self.parts.rearrange("q (b g p) t -> q b p g t", b=B, g=KD)
                with e.Fori(0, B) as b:
                    with e.Fori(0, T // BLK) as cc:
                        for n, name in enumerate(("qhi", "qlo", "khi", "klo")):
                            V.wait(e, name, b * 2 + cc)
                            e.dma_start(dst[n, b, :, :, bass.ds(cc * BLK, BLK)], part[n][:, :, :].bitcast(F32)).then_inc(s_st, 16)
                e.wait_ge(s_st, 16 + 16 * 4 * NB)

    def attend_buffers(self, c):
        sb = lambda n, s, dt=F32: self.sb(c, n, s, dt)
        self.Q = [sb(f"aQ{p}", [P, 2, T], F32R) for p in range(2)]
        self.K = [sb(f"aK{p}", [P, 2, 2, T], F32R) for p in range(2)]
        self.identr, self.maskq, self.maskk = sb("a_idr", [P, P], F32R), sb("a_mq", [P, P], F32R), sb("a_mk", [P, P], F32R)

    def attend_constants(self, e, s):
        for t in (self.identr[:, :], self.maskq[:, :], self.maskk[:, :], self.Q[0][:, :, :], self.Q[1][:, :, :],
                  self.K[0][:, :, :, :], self.K[1][:, :, :, :]):
            e.memset(t.bitcast(F32), 0.0).then_inc(s, 1)
        e.wait_ge(s, 7)
        sel = lambda t, op, fill, pattern, cm: e.affine_select(out=t[:, :], in_=t[:, :], compare_op=op, fill=fill, base=0,
                                                               pattern=pattern, channel_multiplier=cm).then_inc(s, 1)
        sel(self.identr, ALU.not_equal, 1.0, [[-1, P]], 1)
        sel(self.maskq, ALU.is_ge, MASKED, [[-1, P]], 1)
        sel(self.maskk, ALU.is_ge, MASKED, [[1, P]], -1)
        e.wait_ge(s, 10)
        for p in range(2):
            for par in range(2):
                r = self.AUG + P // 2 * par
                e.memset(self.K[p][r:r + 2, :, par, :].bitcast(F32), 1.0).then_inc(s, 1)
        e.wait_ge(s, 14)

    AUG = 2 * HD

    def attend(self, c):
        nc, PS, V_, OT, Q, K = self.nc, self.PS, self.V, self.OT, self.Q, self.K
        sb = lambda n, s, dt=F32: self.sb(c, n, s, dt)
        NG, NK, G4, HALF, AUG = B * H // 4, T // P, 4, P // 2, self.AUG
        NQ = T // BLK
        Vs = [sb(f"aV{p}", [P, NK, G4, 2 * HD]) for p in range(2)]
        R = 2
        Pb = [sb(f"aP{r}", [P, G4, BLK]) for r in range(R)]
        nm = sb("a_nm", [P, 2, 2, NK])
        nm2 = sb("a_nm2", [P, 2, 2, NK // 2])
        nmp = sb("a_nmp", [P, 2, NK, 2, HALF], F32R)
        part_cols = lambda pair, part: nmp[:, pair, :, :, AUG + part].rearrange("p t r -> p r t")
        parts = self.parts.rearrange("q (n s r2 r) t -> q n r2 s r t", s=2, r2=2, r=HD)
        steps = [(qb, kt) for qb in range(NQ) for kt in range(TB * (qb + 1))]
        last_step = len(steps) - 1
        head = [(4, 0), (0, 0), (3, 0), (4, 1), (5, 0), (1, 0), (7, 1), (5, 1), (6, 0), (2, 0), (7, 0), (6, 1)]
        chunks = [(j, qt, cb) for j in range(G4) for qt, cb in head]
        half = len(chunks) // 2
        FIRST = 3
        per = 2
        users, feed = [], []
        for n in range(len(chunks)):
            users.append(f"c{n}")
            feed.append(f"c{n}")
            if n == half + 2:
                users += ["T0", "T0"]
                feed.append("T0")
                assert (len(users) - 2) % 3 == 0
                users.append("-")
        while len(users) % 3:
            users.append("-")
        users += ["T1", "T1"]
        bank = {u: 5 + users.index(u) % 3 for u in users if u != "-"}
        def freed_by(u):
            at = users.index(u)
            n = 2 if u[0] == "T" else 1
            return [next((users[k] for k in range(at + m - 3, -1, -3) if users[k] != "-"), None) for m in range(n)]
        order = []
        for s in range(len(steps)):
            for item in (f"e{s}a", f"e{s}b", f"pv{s - 1}"):
                if item == f"pv{last_step - 1}":
                    order.append("T1")
                if item != "pv-1":
                    order.append(item)
                if s >= FIRST:
                    k = 0
                    while feed and k < per:
                        u = feed.pop(0)
                        order.append(u)
                        k += u[0] == "c"
        order.append(f"pv{last_step}")
        ahead = [u for u in order if u[0] in "cT"]
        split = lambda u: {f"c{half - 1}": [u, "min0", "hi0", "lo0"], f"c{2 * half - 1}": [u, "min1", "hi1", "lo1"]}.get(u, [u])
        v_of = lambda seq: [n for u in seq for n in (split(u) if u[0] == "c" else [f"r{u[1]}"] if u[0] == "T" else
                                                     ["o1"] if u == f"pv{last_step}" else [])]
        a_of = lambda seq: [n for u in seq for n in ((["o0"] if u == f"e{TB + 1}a" else []) + ["p" + u[1:]] if u[0] == "e" else
                                                     [f"r{u[1]}"] if u[0] == "T" else [])]
        two = lambda names: [f"{n}.{p}" for p in range(2) for n in names]
        first = lambda names: [f"{n}.-" for n in names]
        S = self.steps("a_pe", two(order), first(ahead))
        V = self.steps("a_dve", two(v_of(order)), first(v_of(ahead) + ["o1"]))
        a_steps = a_of(order)
        r0, r1 = a_steps.index("r0"), a_steps.index("r1")
        A = self.steps("a_act", two(a_of(order)), first(a_steps[r0:]))
        C = self.steps("a_pool", two(["z0", "z1", "vs"]), ["zero", "vs.-"])
        s_ld = [[self.sem(f"a_ld{p}{q}") for q in range(2)] for p in range(2)]
        n_ld = 16 * 12

        def prev(steps_, eng, name, p, i):
            steps_.wait(eng, f"{name}.{1 - p}", i if p else i - 1)

        def span(j, qt, cb):
            return min(BLK, (qt + 1) * P - cb * BLK), (qt + 1) * P <= (cb + 1) * BLK

        with nc.Block() as block:
            @block.gpsimd
            def _(e):
                C.start(e)
                C.done(e.memset(nmp[:, :, :, :, :].bitcast(F32), 0.0), "zero")
                C.wait(e, "zero")
                C.done(e.tensor_copy(Vs[0][:, :, :, :], V_[:, 0:NK, 0:G4, :]), "vs.-")
                with e.Fori(0, NG // 2) as i:
                    for p in range(2):
                        n = (i * 2 + p + 1) % NG
                        prev(S, e, f"e{last_step}b", p, i)
                        prev(C, e, "vs", p, i)
                        e.sem_inc(self.apart, 1)
                        for q in range(2):
                            e.memset(Q[1 - p][AUG:AUG + 2, q, :].bitcast(F32), 0.0)
                            C.done(e.memset(Q[1 - p][AUG + HALF:AUG + HALF + 2, q, :].bitcast(F32), 0.0), f"z{q}.{p}")
                        prev(S, e, f"pv{last_step}", p, i)
                        C.wait(e, f"z1.{p}", i)
                        e.sem_inc(self.apart, 1)
                        C.done(e.tensor_copy(Vs[1 - p][:, :, :, :], V_[:, bass.ds((n // 4) * NK, NK), bass.ds((n % 4) * G4, G4), :]), f"vs.{p}")
            def loads(e, p, n):
                for q in range(2):
                    for par in range(2):
                        for dst, slots in ((Q[p][:, q, :], ((0, 0), (1, 0), (3, 1))), (K[p][:, q, par, :], ((0, 2), (1, 3), (3, 2)))):
                            for slot, part in slots:
                                r = HALF * par + HD * slot
                                e.dma_start(dst[r:r + HD, :].bitcast(F32), parts[part, n, par, q, :, :]).then_inc(s_ld[p][q], 16)
            @block.sync
            def _(e):
                loads(e, 0, 0)
                with e.Fori(0, NG // 2) as i:
                    for p in range(2):
                        prev(S, e, f"e{last_step}b", p, i)
                        loads(e, 1 - p, (i * 2 + p + 1) % NG)

            @block.tensor
            def _(e):
                S.start(e)
                def take(u, p, tag, i):
                    for f in freed_by(u):
                        if f is None:
                            if p is not None:
                                prev(V, e, "r1", p, i)
                                prev(A, e, "r1", p, i)
                        elif f[0] == "c":
                            V.wait(e, f + tag, i)
                        else:
                            V.wait(e, "r" + f[1] + tag, i)
                            A.wait(e, "r" + f[1] + tag, i)
                def chunk(u, p, q, tag, i):
                    n = int(u[1:])
                    j, qt, cb = chunks[n]
                    if n % half == 0:
                        pair = n // half
                        if p is None:
                            e.wait_ge(s_ld[q][pair], n_ld)
                        else:
                            e.wait_ge(s_ld[q][pair], n_ld * (i + 1 + (p == 1)))
                            C.wait(e, f"z{pair}" + tag, i)
                    take(u, p, tag, i)
                    w, diag = span(j, qt, cb)
                    last = e.matmul(PS[:, bank[u], 0:w], Q[q][:, j // 2, qt * P:(qt + 1) * P], K[q][:, j // 2, j % 2, cb * BLK:cb * BLK + w],
                                    start=True, stop=not diag)
                    if diag:
                        last = e.matmul(PS[:, bank[u], w - P:w], self.identr[:, :], self.maskq[:, :], start=False, stop=True)
                    S.done(last, u + tag)
                def turn(u, p, tag, i):
                    pair = int(u[1])
                    take(u, p, tag, i)
                    V.wait(e, f"lo{pair}" + tag, i)
                    for qt in range(NK):
                        last = e.matmul(PS[:, bank[u] + qt // TB, (qt % TB) * P:(qt % TB + 1) * P],
                                        nmp[:, pair, qt, :, :].rearrange("p r c -> p (r c)"), self.identr[:, :], start=True, stop=True)
                    S.done(last, u + tag)
                for u in ahead:
                    (chunk(u, None, 0, ".-", 0) if u[0] == "c" else turn(u, None, ".-", 0))
                with e.Fori(0, NG // 2) as i:
                    for p in range(2):
                        tag = f".{p}"
                        def scores(s, x):
                            qb, kt = steps[s]
                            c0, diag = max(0, kt - TB * qb) * P, kt >= TB * qb
                            if s:
                                A.wait(e, f"p{s - 1}{x}" + tag, i)
                            else:
                                prev(A, e, f"p{last_step}{x}", p, i)
                                prev(V, e, f"r{'ab'.index(x)}", p, i)
                                prev(A, e, f"r{'ab'.index(x)}", p, i)
                            for j in ((0, 1), (2, 3))["ab".index(x)]:
                                last = e.matmul(PS[:, j, c0:BLK], K[p][:, j // 2, j % 2, kt * P:(kt + 1) * P],
                                                Q[p][:, j // 2, qb * BLK + c0:(qb + 1) * BLK], start=True, stop=not diag)
                                if diag:
                                    last = e.matmul(PS[:, j, c0:c0 + P], self.identr[:, :], self.maskk[:, :], start=False, stop=True)
                            S.done(last, f"e{s}{x}" + tag)
                        def pv(s):
                            qb, kt = steps[s]
                            c0 = max(0, kt - TB * qb) * P
                            A.wait(e, f"p{s}b" + tag, i)
                            if s == 0:
                                prev(C, e, "vs", p, i)
                                prev(V, e, "o1", p, i)
                            elif kt == 0:
                                A.wait(e, "o0" + tag, i)
                            for j in range(G4):
                                last = e.matmul(PS[32 * j:32 * j + 32, 4, c0:BLK], Vs[p][:, kt, j, :], Pb[s % R][:, j, c0:BLK],
                                                start=kt == 0, stop=kt == TB * (qb + 1) - 1, skip_group_check=True)
                            S.done(last, f"pv{s}" + tag)
                        for u in order:
                            if u[0] == "e":
                                scores(int(u[1:-1]), u[-1])
                            elif u[0] == "p":
                                pv(int(u[2:]))
                            elif u[0] == "c":
                                chunk(u, p, 1 - p, tag, i)
                            else:
                                turn(u, p, tag, i)

            def rows(pair, par, q, tag):
                r, b0 = AUG + HALF * par, bank[f"T{pair}"]
                return Q[q][r:r + 2, pair, :], PS[r:r + 2, b0:b0 + 2, :].rearrange("p b n -> p (b n)")

            @block.scalar
            def _(e):
                A.start(e)
                for pair, between in ((0, r1 - r0 - 1), (1, len(a_steps) - 1 - r1)):
                    S.wait(e, f"T{pair}.-")
                    A.done(e.activation(*rows(pair, 0, 0, ".-"), ACT.Copy), f"r{pair}.-")
                    A.wait(e, f"r{pair}.-")
                    if between:
                        e.sem_inc(A.sem, between)
                with e.Fori(0, NG // 2) as i:
                    for p in range(2):
                        tag = f".{p}"
                        for u in a_steps:
                            if u == "o0":
                                S.wait(e, f"pv{TB - 1}" + tag, i)
                                A.done(e.activation(OT[:, i * 2 + p, 0:BLK], PS[:, 4, :], ACT.Copy), u + tag)
                            elif u[0] == "r":
                                S.wait(e, f"T{u[1]}" + tag, i)
                                A.done(e.activation(*rows(int(u[1]), 0, 1 - p, tag), ACT.Copy), u + tag)
                            else:
                                s, x = int(u[1:-1]), u[-1]
                                c0, j0 = max(0, steps[s][1] - TB * steps[s][0]) * P, 2 * "ab".index(x)
                                if s >= R:
                                    S.wait(e, f"pv{s - R}" + tag, i)
                                else:
                                    prev(S, e, f"pv{last_step + 1 - R + s}", p, i)
                                S.wait(e, f"e{s}{x}" + tag, i)
                                A.done(e.activation(Pb[s % R][:, j0:j0 + 2, c0:BLK], PS[:, j0:j0 + 2, c0:BLK], ACT.Exp), u + tag)

            @block.vector
            def _(e):
                V.start(e)
                C.wait(e, "zero")
                def work(names, q, tag, i):
                    for u in names:
                        pair = int(u[-1])
                        if u[0] == "c":
                            j, qt, cb = chunks[int(u[1:])]
                            dst = nm2[:, j // 2, j % 2, qt - TB:qt - TB + 1] if cb else nm[:, j // 2, j % 2, qt:qt + 1]
                            S.wait(e, u + tag, i)
                            V.done(e.tensor_reduce(dst, PS[:, bank[u], 0:span(j, qt, cb)[0]], AX.X, ALU.max, negate=True), u + tag)
                        elif u[:3] == "min":
                            V.wait(e, f"c{half * (pair + 1) - 1}" + tag, i)
                            late = nm[:, pair, :, TB:NK]
                            V.done(e.tensor_tensor(late, late, nm2[:, pair, :, :], ALU.min), u + tag)
                        elif u[:2] == "hi":
                            V.wait(e, f"min{pair}" + tag, i)
                            V.done(e.tensor_copy(part_cols(pair, 0), nm[:, pair, :, :]), u + tag)
                        elif u[:2] == "lo":
                            V.wait(e, f"hi{pair}" + tag, i)
                            V.done(e.tensor_tensor(part_cols(pair, 1), nm[:, pair, :, :], part_cols(pair, 0).bitcast(F32),
                                                   ALU.subtract), u + tag)
                        elif u[0] == "r":
                            S.wait(e, f"T{pair}" + tag, i)
                            V.done(e.tensor_copy(*rows(pair, 1, q, tag)), u + tag)
                work(v_of(ahead), 0, ".-", 0)
                V.wait(e, "r1.-")
                e.sem_inc(V.sem, 1)
                with e.Fori(0, NG // 2) as i:
                    for p in range(2):
                        tag = f".{p}"
                        work(v_of(order)[:-1], 1 - p, tag, i)
                        S.wait(e, f"pv{last_step}" + tag, i)
                        V.done(e.tensor_copy(OT[:, i * 2 + p, BLK:2 * BLK], PS[:, 4, :]), "o1" + tag)


    def route(self, c):
        nc, a, PS, X, OT = self.nc, self.a, self.PS, self.X, self.OT
        sb = lambda n, s, dt=F32: self.sb(c, n, s, dt)
        NG4 = H // 4
        Wo, bo, g2, b2 = sb("r_Wo", [P, KD, D]), sb("r_bo", [P, D]), sb("r_g2", [P, D]), sb("r_b2", [P, D])
        Wr, br, eb2 = sb("r_Wr", [P, KD, E]), sb("r_br", [P, E]), sb("r_eb2", [E, D])
        os_, rec, on, onT = sb("r_os", [P, NG4, BLK]), sb("r_rec", [P, TB, H]), sb("r_on", [P, TB, D]), sb("r_onT", [P, KD, BLK])
        ya, h2, h2T = sb("r_a", [P, TB, D]), sb("r_h2", [P, TB, D]), sb("r_h2T", [P, KD, BLK])
        lg, best, keep, ex, ws, wT = (sb("r_lg", [P, TB, E]), sb("r_best", [P, TB, 8]), sb("r_keep", [P, TB, E]), sb("r_ex", [P, TB, E]),
                                      sb("r_ws", [P, TB]), sb("r_wT", [E, BLK]))
        st, mv, lv, rstd = sb("r_st", [P, TB, 6]), sb("r_mv", [P, TB, 2]), sb("r_lv", [P, TB]), sb("r_rstd", [P, TB])
        s_w = self.sem("r_w")
        n_w = 16 * 7
        SA = self.steps("r_pe", [f"ot{t}" for t in range(TB)] + ["onT", "wo"])
        SB = self.steps("r_pe2", ["h2T", "lg", "wT", "b2"])
        AA = self.steps("r_act", ["os", "onT1", "rstd_ln", "rstd"])
        AB = self.steps("r_act2", ["h2T1", "ex", "wT"])
        VA = self.steps("r_dve", [n for t in range(TB) for n in (f"rec{t}", f"on{t}")]
                        + ["onT0", "xb", "a", "xa", "stats", "stats_mv", "h2_n", "h2_g", "h2"])
        VB = self.steps("r_dve2", ["h2T0", "hi", "lo", "lg", "best", "keep", "sh", "w_", "ws", "wr", "w", "x"])
        with nc.Block() as block:
            @block.gpsimd
            def _(e):
                e.dma_start(Wo[:, :, :], a["L0_ffn_Wo"].rearrange("(k p) n -> p k n", p=P)).then_inc(s_w, 16)
                e.dma_start(Wr[:, :, :], a["L0_ffn_Wr"].rearrange("(k p) n -> p k n", p=P)).then_inc(s_w, 16)
                for t, w in ((bo, "bo"), (g2, "ln2_g"), (b2, "ln2_b"), (br, "br")):
                    e.dma_start(t[:, :], a["L0_ffn_" + w].partition_broadcast(P)).then_inc(s_w, 16)
                e.dma_start(eb2[:, :], a["L0_ffn_e_b2"]).then_inc(s_w, 16)
                self.W.start(e)
                for p in range(2):
                    self.split_weights(e, p, "-", 0, p)
            @block.sync
            def _(e):
                self.load_weights(e, 0)
                for p, (name, load) in ((1, x) for x in (("w1lo", self.load_w1), ("w2lo", self.load_w2))):
                    self.W.wait(e, f"{name}0-")
                    load(e, p)
            @block.tensor
            def _(e):
                SA.start(e)
                SB.start(e)
                e.wait_ge(s_w, n_w)
                def ot(i):
                    AA.wait(e, "os", i)
                    for t in range(TB):
                        if t >= 2:
                            VA.wait(e, f"on{t - 2}", i)
                        for g in range(NG4):
                            last = e.transpose(PS[:, t % 2, g * P:(g + 1) * P], os_[:, g, t * P:(t + 1) * P], self.ident[:, :])
                        SA.done(last, f"ot{t}")
                def onT_(i):
                    VA.wait(e, f"on{TB - 1}", i)
                    SA.done(self.transposes(e, on, 0, (2, 3)), "onT")
                def wo(i):
                    VA.wait(e, "onT0", i)
                    AA.wait(e, "onT1", i)
                    SA.done(self.token_major(e, onT, Wo, (0, 1)), "wo")
                def h2T_(i):
                    VA.wait(e, "h2", i)
                    SB.done(self.transposes(e, h2, 0, (4, 5)), "h2T")
                def logits(i):
                    VB.wait(e, "h2T0", i)
                    AB.wait(e, "h2T1", i)
                    for t in range(TB):
                        for kt in range(KD):
                            last = e.matmul(PS[:, 6, t * E:(t + 1) * E], h2T[:, kt, t * P:(t + 1) * P], Wr[:, kt, :], start=kt == 0, stop=kt == KD - 1)
                    SB.done(last, "lg")
                def biases(i):
                    VB.wait(e, "w", i)
                    for t in range(TB):
                        last = e.transpose(PS[0:E, 7, t * P:(t + 1) * P], ex[:, t, :], self.ident[:, :])
                    SB.done(last, "wT")
                    AB.wait(e, "wT", i)
                    for t in range(TB):
                        last = e.matmul(PS[:, 4 + t // 2, (t % 2) * D:(t % 2 + 1) * D], wT[:, t * P:(t + 1) * P], eb2[:, :], start=True, stop=True)
                    SB.done(last, "b2")
                ot(0)
                onT_(0)
                wo(0)
                with e.Fori(0, NB - 1) as i:
                    VB.wait_before(e, i)
                    h2T_(i)
                    ot(i + 1)
                    logits(i)
                    onT_(i + 1)
                    wo(i + 1)
                    biases(i)
                VB.wait_before(e, NB - 1)
                h2T_(NB - 1)
                logits(NB - 1)
                biases(NB - 1)
            @block.scalar
            def _(e):
                AA.start(e)
                AB.start(e)
                def first_sums(i):
                    SA.wait_before(e, i)
                    AA.done(e.activation(os_[:, :, :], OT[:, bass.ds((i // 2) * NG4, NG4), bass.ds((i % 2) * BLK, BLK)], ACT.Copy), "os")
                def onT1(i):
                    SA.wait(e, "onT", i)
                    AA.done(e.activation(onT[:, 1, :], PS[:, 3, :], ACT.Copy), "onT1")
                def h2T1(i):
                    SB.wait(e, "h2T", i)
                    AB.done(e.activation(h2T[:, 1, :], PS[:, 5, :], ACT.Copy), "h2T1")
                def exps(i):
                    VB.wait(e, "sh", i)
                    AB.done(e.activation(ex[:, :, :], lg[:, :, :], ACT.Exp), "ex")
                def wT_(i):
                    SB.wait(e, "wT", i)
                    AB.done(e.activation(wT[:, :], PS[0:E, 7, :], ACT.Copy), "wT")
                first_sums(0)
                onT1(0)
                self.norm_rstd(e, AA, VA, 0, mv, lv, rstd)
                with e.Fori(0, NB - 1) as i:
                    first_sums(i + 1)
                    h2T1(i)
                    exps(i)
                    onT1(i + 1)
                    wT_(i)
                    self.norm_rstd(e, AA, VA, i + 1, mv, lv, rstd)
                h2T1(NB - 1)
                exps(NB - 1)
                wT_(NB - 1)
            @block.vector
            def _(e):
                VA.start(e)
                VB.start(e)
                e.wait_ge(s_w, n_w)
                bc = lambda v, n: v.unsqueeze(2).broadcast_to((P, TB, n))
                def divide(i):
                    for t in range(TB):
                        SA.wait(e, f"ot{t}", i)
                        o = PS[:, t % 2, :].rearrange("p (h c) -> p h c", c=2 * HD)
                        VA.done(e.reciprocal(rec[:, t, :], o[:, :, HD]), f"rec{t}")
                        VA.wait(e, f"rec{t}", i)
                        VA.done(e.tensor_tensor(on[:, t, :].rearrange("p (h d) -> p h d", h=H), o[:, :, 0:HD],
                                                rec[:, t, :].unsqueeze(2).broadcast_to((P, H, HD)), ALU.mult), f"on{t}")
                def onT0(i):
                    SA.wait(e, "onT", i)
                    VA.done(e.tensor_copy(onT[:, 0, :], PS[:, 2, :]), "onT0")
                    VA.done(e.tensor_tensor(ya[:, :, :], X[:, bass.ds(i * TB, TB), :], bo[:, :].unsqueeze(1).broadcast_to((P, TB, D)), ALU.add), "xb")
                def residual(i):
                    xt = X[:, bass.ds(i * TB, TB), :]
                    VA.wait(e, "xb", i)
                    SA.wait(e, "wo", i)
                    VA.done(e.tensor_tensor(ya[:, :, :], self.pair_banks(0), ya[:, :, :], ALU.add), "a")
                    VA.wait(e, "a", i)
                    VA.done(e.tensor_tensor(xt, xt, ya[:, :, :], ALU.add), "xa")
                    self.norm_stats(e, VA, i, ya, st, mv)
                def norm(i):
                    self.row_norm_affine(e, VA, AA, i, ya, h2, st, mv, rstd, g2, b2, "h2")
                def h2_parts(i):
                    SB.wait(e, "h2T", i)
                    VB.done(e.tensor_copy(h2T[:, 0, :], PS[:, 4, :]), "h2T0")
                    AB.wait(e, "h2T1", i)
                    VB.wait(e, "h2T0", i)
                    hi, lo = (t[:, :, bass.ds(i * BLK, BLK)] for t in self.h2)
                    VB.done(e.tensor_copy(hi, h2T[:, :, :]), "hi")
                    VB.wait(e, "hi", i)
                    VB.done(e.tensor_tensor(lo, h2T[:, :, :], hi.bitcast(F32), ALU.subtract), "lo")
                def best_two(i):
                    SB.wait(e, "lg", i)
                    VB.done(e.tensor_tensor(lg[:, :, :], PS[:, 6, 0:TB * E].rearrange("p (t n) -> p t n", n=E),
                                            br[:, :].unsqueeze(1).broadcast_to((P, TB, E)), ALU.add), "lg")
                    VB.wait_apart(e, "lg", i, self.apart)
                    for t in range(TB):
                        last = e.max(best[:, t, :], lg[:, t, :])
                    VB.done(last, "best")
                    VB.wait(e, "best", i)
                    VB.done(e.tensor_tensor(keep[:, :, :], lg[:, :, :], bc(best[:, :, 1], E), ALU.is_ge), "keep")
                    VB.wait(e, "keep", i)
                    VB.done(e.tensor_tensor(lg[:, :, :], lg[:, :, :], bc(best[:, :, 0], E), ALU.subtract), "sh")
                def weights(i):
                    AB.wait(e, "ex", i)
                    VB.done(e.tensor_tensor(ex[:, :, :], ex[:, :, :], keep[:, :, :], ALU.mult), "w_")
                    VB.wait(e, "w_", i)
                    VB.done(e.tensor_reduce(ws[:, :], ex[:, :, :], AX.X, ALU.add), "ws")
                    VB.wait(e, "ws", i)
                    VB.done(e.reciprocal(ws[:, :], ws[:, :]), "wr")
                    VB.wait(e, "wr", i)
                    e.tensor_tensor(self.w_all[:, bass.ds(i * TB, TB), :], ex[:, :, :], bc(ws[:, :], E), ALU.mult)
                    VB.done(e.tensor_tensor(ex[:, :, :], ex[:, :, :], bc(ws[:, :], E), ALU.mult), "w")
                def add_biases(i):
                    xt = X[:, bass.ds(i * TB, TB), :]
                    SB.wait(e, "b2", i)
                    VB.done(e.tensor_tensor(xt, self.pair_banks(4), xt, ALU.add), "x")
                divide(0)
                onT0(0)
                residual(0)
                norm(0)
                with e.Fori(0, NB - 1) as i:
                    h2_parts(i)
                    divide(i + 1)
                    best_two(i)
                    onT0(i + 1)
                    weights(i)
                    residual(i + 1)
                    add_biases(i)
                    norm(i + 1)
                h2_parts(NB - 1)
                best_two(NB - 1)
                weights(NB - 1)
                add_biases(NB - 1)

    def expert_buffers(self, c):
        sb = lambda n, s, dt=F32: self.sb(c, n, s, dt)
        self.h2 = [sb(f"x_h2{n}", [P, KD, N], F32R) for n in range(2)]
        self.w1 = [[sb(f"x_w1{p}{n}", [P, KD, FF], F32R) for n in range(2)] for p in range(2)]
        self.w2 = [[sb(f"x_w2{p}{n}", [P, NF, D], F32R) for n in range(2)] for p in range(2)]
        self.raw1, self.raw2 = sb("x_raw1", [P, KD, FF]), sb("x_raw2", [P, NF, D])
        self.s_w1, self.s_w2 = self.sem("x_w1"), self.sem("x_w2")
        names = [f"{w}{part}{p}" for p in range(2) for w in ("w1", "w2") for part in ("hi", "lo")]
        self.W = self.steps("x_pool", names, [n + "-" for n in names])

    def load_w1(self, e, n):
        e.dma_start(self.raw1[:, :, :], self.a["L0_ffn_e_w1"].rearrange("e (k p) n -> e p k n", p=P)[n]).then_inc(self.s_w1, 16)

    def load_w2(self, e, n):
        e.dma_start(self.raw2[:, :, :], self.a["L0_ffn_e_w2"].rearrange("e (k p) n -> e p k n", p=P)[n]).then_inc(self.s_w2, 16)

    def load_weights(self, e, n):
        self.load_w1(e, n)
        self.load_w2(e, n)

    def split_weights(self, e, p, tag, i, n):
        for raw, w, name, s in ((self.raw1, self.w1, "w1", self.s_w1), (self.raw2, self.w2, "w2", self.s_w2)):
            e.wait_ge(s, 16 * (n + 1))
            e.sem_inc(self.apart, 1)
            self.W.done(e.tensor_copy(w[p][0][:, :, :], raw[:, :, :]), f"{name}hi{p}{tag}")
            self.W.wait(e, f"{name}hi{p}{tag}", i)
            self.W.done(e.tensor_tensor(w[p][1][:, :, :], raw[:, :, :], w[p][0][:, :, :].bitcast(F32), ALU.subtract), f"{name}lo{p}{tag}")

    def experts(self, c):
        nc, a, PS, X = self.nc, self.a, self.PS, self.X
        sb = lambda n, s, dt=F32: self.sb(c, n, s, dt)
        h2, w1, w2, W = self.h2, self.w1, self.w2, self.W
        b1r, b1 = sb("x_b1r", [E * NF, P]), sb("x_b1", [P, E, NF])
        g = [sb(f"x_g{r}", [P, BLK]) for r in range(2)]
        mid = [sb(f"x_mid{n}", [P, NF, BLK], F32R) for n in range(2)]
        st, mv, lv, rstd = sb("x_st", [P, NT, 6]), sb("x_mv", [P, NT, 2]), sb("x_lv", [P, NT]), sb("x_rstd", [P, NT])
        PASSES = ((0, 0), (0, 1), (1, 0))
        s_b, s_out = self.sem("x_b"), self.sem("x_out")
        fs = range(NF)
        S = self.steps("x_pe", [f"m{f}" for f in fs] + ["out"], ["b1"])
        A = self.steps("x_act", [f"g{f}" for f in fs], ["b1"])
        A2 = self.steps("x_act2", ["ln", "rstd"])
        V = self.steps("x_dve", [n for f in fs for n in (f"hi{f}", f"lo{f}")] + [f"x{t}" for t in range(TB)])
        V2 = self.steps("x_dve2", [f"stats{k}" for k in range(NB)] + ["mv"] + [f"out{k}" for k in range(NB)])
        s_free = [self.sem(f"x_free{p}") for p in range(2)]
        with nc.Block() as block:
            @block.sync
            def _(e):
                e.dma_start(b1r[:, :], a["L0_ffn_e_b1"].rearrange("e (f p) -> (e f) p", p=P)).then_inc(s_b, 16)
                with e.Fori(0, E // 2 - 1) as i:
                    for p in range(2):
                        for name, load in (("w1lo", self.load_w1), ("w2lo", self.load_w2)):
                            W.wait(e, f"{name}{1 - p}", i if p else i - 1)
                            load(e, i * 2 + p + 2)
                dst = self.out.rearrange("b (t p) d -> p (b t) d", p=P)
                for k in range(NB):
                    V2.wait(e, f"out{k}")
                    e.dma_start(dst[:, k * TB:(k + 1) * TB, :], X[:, k * TB:(k + 1) * TB, :]).then_inc(s_out, 16)
                e.wait_ge(s_out, 16 * NB)
            @block.gpsimd
            def _(e):
                with e.Fori(0, E // 2 - 1) as i:
                    for p in range(2):
                        e.wait_ge(s_free[p], i + 1)
                        self.split_weights(e, p, "", i, i * 2 + p + 2)
            @block.tensor
            def _(e):
                S.start(e)
                e.wait_ge(s_b, 16)
                S.done(e.transpose(PS[:, 0, 0:E * NF], b1r[:, :], self.ident[0:E * NF, 0:E * NF]), "b1")
                A.wait(e, "b1")
                with e.Fori(0, E // 2) as i:
                    for p in range(2):
                        with e.Fori(0, NB) as k:
                            it = (i * 2 + p) * NB + k
                            W.wait(e, f"w1lo{p}", i - 1)
                            for f in fs:
                                if f >= 4:
                                    A.wait(e, f"g{f - 4}", it)
                                else:
                                    A.wait_before(e, it)
                                for n, (u, v) in enumerate(PASSES):
                                    for kt in range(KD):
                                        last = e.matmul(PS[:, f % 4, :], w1[p][u][:, kt, f * P:(f + 1) * P], h2[v][:, kt, bass.ds(k * BLK, BLK)],
                                                        start=n == 0 and kt == 0, stop=n == 2 and kt == KD - 1)
                                S.done(last, f"m{f}")
                            W.wait(e, f"w2lo{p}", i - 1)
                            V.wait_before(e, it)
                            for f in fs:
                                V.wait(e, f"lo{f}", it)
                                for t in range(TB):
                                    for n, (u, v) in enumerate(PASSES):
                                        last = e.matmul(PS[:, 4 + t, 0:D], mid[u][:, f, t * P:(t + 1) * P], w2[p][v][:, f, :],
                                                        start=f == 0 and n == 0, stop=f == NF - 1 and n == 2)
                            S.done(last, "out")
                        S.wait_before(e, (i * 2 + p + 1) * NB)
                        e.sem_inc(s_free[p], 1)
            @block.scalar
            def _(e):
                A.start(e)
                A2.start(e)
                S.wait(e, "b1")
                A.done(e.activation(b1[:, :, :].rearrange("p e f -> p (e f)"), PS[:, 0, 0:E * NF], ACT.Copy), "b1")
                A.wait(e, "b1")
                with e.Fori(0, E) as n:
                    with e.Fori(0, NB) as k:
                        it = n * NB + k
                        for f in fs:
                            S.wait(e, f"m{f}", it)
                            if f >= 2:
                                V.wait(e, f"lo{f - 2}", it)
                            else:
                                V.wait_before(e, it)
                            A.done(e.activation(g[f % 2][:, :], PS[:, f % 4, :], ACT.Gelu, bias=b1[:, n, f:f + 1]), f"g{f}")
                V2.wait(e, "mv")
                A2.done(e.activation(lv[:, :], mv[:, :, 1], ACT.Ln, bias=self.eps[:, 0:1]), "ln")
                A2.wait(e, "ln")
                A2.done(e.activation(rstd[:, :], lv[:, :], ACT.Exp, scale=-0.5), "rstd")
            @block.vector
            def _(e):
                V.start(e)
                V2.start(e)
                with e.Fori(0, E) as n:
                    with e.Fori(0, NB) as k:
                        it = n * NB + k
                        for f in fs:
                            A.wait(e, f"g{f}", it)
                            if f == 0:
                                S.wait_before(e, it)
                            V.done(e.tensor_copy(mid[0][:, f, :], g[f % 2][:, :]), f"hi{f}")
                            V.wait(e, f"hi{f}", it)
                            V.done(e.tensor_tensor(mid[1][:, f, :], g[f % 2][:, :], mid[0][:, f, :].bitcast(F32), ALU.subtract), f"lo{f}")
                        S.wait(e, "out", it)
                        for t in range(TB):
                            xt = X[:, k * TB + t, :]
                            V.done(e.scalar_tensor_tensor(out=xt, in0=PS[:, 4 + t, 0:D], scalar=self.w_all[:, k * TB + t, bass.ds(n, 1)],
                                                          in1=xt, op0=ALU.mult, op1=ALU.add), f"x{t}")
                V.wait_before(e, E * NB)
                for k in range(NB):
                    tiles = range(k * TB, (k + 1) * TB)
                    for t in tiles:
                        last = e.bn_stats(st[:, t, :], X[:, t, :])
                    V2.done(last, f"stats{k}")
                for k in range(NB):
                    V2.wait(e, f"stats{k}")
                    for t in range(k * TB, (k + 1) * TB):
                        last = e.bn_aggr(mv[:, t, :], st[:, t, :])
                V2.done(last, "mv")
                A2.wait(e, "rstd")
                for k in range(NB):
                    for t in range(k * TB, (k + 1) * TB):
                        last = e.tensor_scalar(X[:, t, :], X[:, t, :], mv[:, t, 0:1], rstd[:, t:t + 1], ALU.subtract, ALU.mult)
                    V2.done(last, f"out{k}")


def kernel(**inputs):
    import concourse.bacc as bacc
    import numpy as np
    from concourse.bass_utils import run_bass_kernel_spmd

    nc = bacc.Bacc("TRN2", target_bir_lowering=False, num_devices=1)
    arrays, aps = {}, {}
    for name, value in inputs.items():
        array = np.ascontiguousarray(value)
        arrays[name] = array
        aps[name] = nc.dram_tensor(name, array.shape, mybir.dt.from_np(array.dtype), kind="ExternalInput").ap()
    out = nc.dram_tensor("out", (B, T, D), F32, kind="ExternalOutput").ap()
    Kernel(nc, aps, out).build()
    results = run_bass_kernel_spmd(nc, [arrays], core_ids=[0])
    return results.results[0]["out"]
```

```python
from contextlib import ExitStack

import concourse.bass as bass
from concourse import mybir

F32 = mybir.dt.float32
F32R = mybir.dt.float32r
BF16 = mybir.dt.bfloat16
I32 = mybir.dt.int32
ALU = mybir.AluOpType
ACT = mybir.ActivationFunctionType
AX = mybir.AxisListType

P = 128
B = 2
T = 1024
N = B * T
D = 256
KD = D // P
H = 16
HD = D // H
DK = 8
LOW = 16
NT = N // P
BLK = 512
NB = N // BLK
TB = BLK // P
NCTX = 64
NSEL = 64
LAT = 128
E = 8
FF = 4 * D
NF = FF // P
EPS = 1e-5
MASKED = -1e30
HG = P // HD


class Steps:

    def __init__(self, sem, names, before=()):
        self.sem, self.names, self.before = sem, list(names), ["start", *before]
        assert len(set(self.names)) == len(self.names)

    def value(self, name, i=0):
        if name in self.before:
            return self.before.index(name) + 1
        return len(self.before) + i * len(self.names) + self.names.index(name) + 1

    def start(self, eng):
        eng.sem_inc(self.sem, 1)

    def done(self, instruction, name):
        instruction.then_inc(self.sem, 1)

    def wait_apart(self, eng, name, i, apart):
        self.wait(eng, name, i)
        eng.sem_inc(apart, 1)

    def wait(self, eng, name, i=0):
        eng.wait_ge(self.sem, self.value(name, i))

    def wait_before(self, eng, i):
        eng.wait_ge(self.sem, len(self.before) + i * len(self.names))


class Kernel:
    def __init__(self, nc, a, out):
        self.nc, self.a, self.out = nc, a, out
        self.top = ExitStack()
        self.n_sem = 0

    def sb(self, ctx, name, shape, dt=F32):
        return ctx.enter_context(self.nc.sbuf_tensor(name, shape, dt))

    def sem(self, name):
        return self.top.enter_context(self.nc.semaphore(name))

    def steps(self, name, names, before=()):
        return Steps(self.sem(name), names, before)

    def build(self, upto=99):
        nc = self.nc
        with self.top:
            self.PS = self.top.enter_context(nc.psum_tensor("PS", [P, 8, BLK], F32))
            self.X = self.sb(self.top, "X", [P, NT, D])
            self.ident = self.sb(self.top, "ident", [P, P])
            self.eps = self.sb(self.top, "eps", [P, 1])
            self.w_all = self.sb(self.top, "w_all", [P, NT, E])
            self.apart = self.sem("apart")
            with ExitStack() as c:
                with ExitStack() as c2:
                    self.cross_buffers(c, c2)
                    self.gla_buffers(c2)
                    with ExitStack() as c3:
                        self.gla_setup(c3)
                        self.gla_gates(c3)
                    self.gla_scan(c2)
                    self.cross_setup()
                    self.gla_out(c2)
                if upto >= 2:
                    self.cross_blocks(c)
            if upto >= 3:
                self.self_attention(upto >= 4)
            if upto < 4:
                self.store()

    def store(self):
        s_out = self.sem("s_out")
        with self.nc.Block() as block:
            @block.sync
            def _(e):
                e.dma_start(self.out.rearrange("b (t p) d -> p (b t) d", p=P), self.X[:, :, :]).then_inc(s_out, 16)
                e.wait_ge(s_out, 16)


    def transposes(self, pe, src, blk, banks):
        for kt in range(KD):
            for t in range(TB):
                last = pe.transpose(self.PS[:, banks[kt], t * P:(t + 1) * P],
                                    src[:, TB * blk + t, kt * P:(kt + 1) * P], self.ident[:, :])
        return last

    def token_major(self, pe, srcT, w, banks, start=True, stop=True):
        for t in range(TB):
            for kt in range(KD):
                last = pe.matmul(self.PS[:, banks[t // 2], (t % 2) * D:(t % 2 + 1) * D],
                                 srcT[:, kt, t * P:(t + 1) * P], w[:, kt, :], start=kt == 0, stop=kt == KD - 1)
        return last

    def pair_banks(self, b0):
        return self.PS[:, b0:b0 + 2, :].rearrange("p b (t d) -> p (b t) d", t=2)

    NORM = ["stats", "stats_mv", "rstd"]

    def norm_stats(self, dve, V, i, y, st, mv):
        for t in range(TB):
            last = dve.bn_stats(st[:, t, :], y(t))
        V.done(last, "stats")
        V.wait_apart(dve, "stats", i, self.apart)
        for t in range(TB):
            last = dve.bn_aggr(mv[:, t, :], st[:, t, :])
        V.done(last, "stats_mv")

    def norm_sd(self, act, A, V, i, mv, sd):
        V.wait(act, "stats_mv", i)
        A.done(act.activation(sd[:, :], mv[:, :, 1], ACT.Sqrt, bias=self.eps[:, 0:1]), "sd")

    def norm_rstd(self, dve, V, A, i, sd, rstd):
        A.wait(dve, "sd", i)
        V.done(dve.reciprocal(rstd[:, :], sd[:, :]), "rstd")
        V.wait(dve, "rstd", i)


    def gla_buffers(self, c):
        sb = lambda n, s, dt=F32: self.sb(c, n, s, dt)
        self.XTp = [sb(f"XTp{n}", [P, KD, N], F32R) for n in range(2)]
        self.Wvp = sb("Wvp", [P, 2, KD, D], F32R)
        self.Wo = sb("Wo", [P, KD, D])
        self.G = sb("G", [P, NT, D])
        self.headsum = sb("headsum", [P, 32])
        self.QT, self.KT, self.decay = sb("QT", [P, N]), sb("KT", [P, N]), sb("decay", [P, N])

    def gla_setup(self, c):
        nc, a, PS, X, ident, G, R, Wvp = self.nc, self.a, self.PS, self.X, self.ident, self.G, self.headsum, self.Wvp
        sb = lambda n, s, dt=F32: self.sb(c, n, s, dt)
        self.XT = XT = sb("XT", [P, KD, N])
        self.Wq, self.Wk = sb("Wq", [P, KD, P]), sb("Wk", [P, KD, P])
        self.Wgk1, self.Wgk2 = sb("Wgk1", [P, KD, LOW]), sb("Wgk2", [LOW, P])
        self.bgk2 = sb("bgk2", [P, 1])
        Wv, Wg, gnw = sb("Wv", [P, KD, D]), sb("Wg", [P, KD, D]), sb("gnw", [P, HD])
        s_x, s_w = self.sem("g_x"), self.sem("g_w")
        loads = [(self.Wq, "L0_attn_Wq"), (self.Wk, "L0_attn_Wk"), (self.Wgk1, "L0_attn_Wgk1"), (Wv, "L0_attn_Wv"),
                 (Wg, "L0_attn_Wg"), (self.Wo, "L0_attn_Wo")]
        n_w = 16 * (len(loads) + 3)
        C = self.steps("g_c", ["zero", "zeror", "eps", "ident", "r1", "r2"])
        S = self.steps("g_pe", [n for k in range(NB) for n in (f"t{k}", f"g{k}")])
        V = self.steps("g_dve", [n for k in range(NB) for n in (f"x0{k}",)] + ["wv0", "wv1"] + [f"gn{k}" for k in range(NB)])
        A = self.steps("g_act", [n for k in range(NB) for n in (f"x1{k}", f"silu{k}")])
        with nc.Block() as block:
            @block.sync
            def _(e):
                for k in range(NB):
                    e.dma_start(X[:, k * TB:(k + 1) * TB, :],
                                a["x"].rearrange("b (t p) d -> p (b t) d", p=P)[:, k * TB:(k + 1) * TB, :]).then_inc(s_x, 16)
                    e.wait_ge(s_x, 16 * (k + 1))
            @block.gpsimd
            def _(e):
                for t, w in loads:
                    e.dma_start(t[:, :, :], a[w].rearrange("(k p) n -> p k n", p=P)).then_inc(s_w, 16)
                e.dma_start(self.Wgk2[:, :], a["L0_attn_Wgk2"]).then_inc(s_w, 16)
                e.dma_start(self.bgk2[:, :], a["L0_attn_bgk2"].rearrange("(p o) -> p o", o=1)).then_inc(s_w, 16)
                e.dma_start(gnw[:, :], a["L0_attn_gnw"].partition_broadcast(P)).then_inc(s_w, 16)
                C.start(e)
                C.done(e.memset(ident[:, :], 0.0), "zero")
                C.done(e.memset(R[:, :], 1.0), "zeror")
                C.done(e.memset(self.eps[:, :], EPS), "eps")
                C.wait(e, "zeror")
                C.done(e.affine_select(out=ident[:, :], in_=ident[:, :], compare_op=ALU.not_equal, fill=1.0, base=0,
                                       pattern=[[-1, P]], channel_multiplier=1), "ident")
                C.done(e.affine_select(out=R[:, :], in_=R[:, :], compare_op=ALU.is_ge, fill=0.0, base=0,
                                       pattern=[[-DK, 32]], channel_multiplier=1), "r1")
                C.wait(e, "r1")
                C.done(e.affine_select(out=R[:, :], in_=R[:, :], compare_op=ALU.is_ge, fill=0.0, base=DK - 1,
                                       pattern=[[DK, 32]], channel_multiplier=-1), "r2")
            @block.tensor
            def _(e):
                S.start(e)
                C.wait(e, "ident")
                for k in range(NB):
                    e.wait_ge(s_x, 16 * (k + 1))
                    if k >= 2:
                        V.wait(e, f"x0{k - 2}")
                        A.wait(e, f"x1{k - 2}")
                    S.done(self.transposes(e, X, k, (2 * (k % 2), 2 * (k % 2) + 1)), f"t{k}")
                    e.wait_ge(s_w, n_w)
                    V.wait(e, f"x0{k}")
                    A.wait(e, f"x1{k}")
                    if k >= 2:
                        A.wait(e, f"silu{k - 2}")
                    S.done(self.token_major(e, XT[:, :, k * BLK:(k + 1) * BLK], Wg, (4 + 2 * (k % 2), 5 + 2 * (k % 2))), f"g{k}")
            @block.vector
            def _(e):
                V.start(e)
                for k in range(NB):
                    S.wait(e, f"t{k}")
                    V.done(e.tensor_copy(XT[:, 0, k * BLK:(k + 1) * BLK], PS[:, 2 * (k % 2), :]), f"x0{k}")
                e.wait_ge(s_w, n_w)
                V.done(e.tensor_copy(Wvp[:, 0, :, :], Wv[:, :, :]), "wv0")
                V.wait(e, "wv0")
                V.done(e.tensor_tensor(Wvp[:, 1, :, :], Wv[:, :, :], Wvp[:, 0, :, :].bitcast(F32), ALU.subtract), "wv1")
                for k in range(NB):
                    A.wait(e, f"silu{k}")
                    g = G[:, k * TB:(k + 1) * TB, :].rearrange("p t (h j) -> p (t h) j", j=HD)
                    V.done(e.tensor_tensor(g, g, gnw[:, :].unsqueeze(1).broadcast_to((P, TB * H, HD)), ALU.mult), f"gn{k}")
            @block.scalar
            def _(e):
                A.start(e)
                for k in range(NB):
                    S.wait(e, f"t{k}")
                    A.done(e.activation(XT[:, 1, k * BLK:(k + 1) * BLK], PS[:, 2 * (k % 2) + 1, :], ACT.Copy), f"x1{k}")
                    S.wait(e, f"g{k}")
                    A.done(e.activation(G[:, k * TB:(k + 1) * TB, :], self.pair_banks(4 + 2 * (k % 2)), ACT.Silu), f"silu{k}")

    def gla_gates(self, c):
        nc, PS, XT = self.nc, self.PS, self.XT
        sb = lambda n, s, dt=F32: self.sb(c, n, s, dt)
        lowT, z, az = sb("lowT", [LOW, BLK]), sb("z", [P, N]), sb("az", [P, N])
        S = self.steps("gg_pe", ["low", "q", "k", "z"])
        A = self.steps("gg_act", ["low", "z", "abs", "q", "exp"])
        V = self.steps("gg_dve", ["k", "xhi", "xlo"])
        A2 = self.steps("gg_act2", [f"ln{k}" for k in range(NB)] + [f"decay{k}" for k in range(NB)])
        V2 = self.steps("gg_dve2", [f"u{k}" for k in range(NB)])
        with nc.Block() as block:
            @block.sync
            def _(e):
                self.load_indices(e)
            @block.gpsimd
            def _(e):
                self.cross_constants(e)
            @block.tensor
            def _(e):
                S.start(e)
                with e.Fori(0, NB) as i:
                    x = lambda kt: XT[:, kt, bass.ds(i * BLK, BLK)]
                    A.wait_before(e, i)
                    V.wait_before(e, i)
                    for name, w, bank, m in (("low", self.Wgk1, 0, LOW), ("q", self.Wq, 1, P), ("k", self.Wk, 2, P)):
                        for kt in range(KD):
                            last = e.matmul(PS[0:m, bank, :], w[:, kt, :], x(kt), start=kt == 0, stop=kt == KD - 1)
                        S.done(last, name)
                    A.wait(e, "low", i)
                    S.done(e.matmul(PS[:, 3, :], self.Wgk2[:, :], lowT[:, :], start=True, stop=True), "z")
            @block.scalar
            def _(e):
                A.start(e)
                with e.Fori(0, NB) as i:
                    cols = bass.ds(i * BLK, BLK)
                    S.wait(e, "low", i)
                    A.done(e.activation(lowT[:, :], PS[0:LOW, 0, :], ACT.Copy), "low")
                    S.wait_apart(e, "z", i, self.apart)
                    A.done(e.activation(z[:, cols], PS[:, 3, :], ACT.Identity, bias=self.bgk2[:, 0:1]), "z")
                    A.wait_apart(e, "z", i, self.apart)
                    A.done(e.activation(az[:, cols], z[:, cols], ACT.Abs), "abs")
                    A.done(e.activation(self.QT[:, cols], PS[:, 1, :], ACT.Copy, scale=DK ** -0.5), "q")
                    A.wait_apart(e, "abs", i, self.apart)
                    A.done(e.activation(az[:, cols], az[:, cols], ACT.Exp, scale=-1.0), "exp")
                A2.start(e)
                A.wait_before(e, NB)
                for k in range(NB):
                    cols = slice(k * BLK, (k + 1) * BLK)
                    A2.done(e.activation(az[:, cols], az[:, cols], ACT.Ln, bias=1.0), f"ln{k}")
                for k in range(NB):
                    cols = slice(k * BLK, (k + 1) * BLK)
                    V2.wait(e, f"u{k}")
                    A2.done(e.activation(self.decay[:, cols], z[:, cols], ACT.Exp, scale=1.0 / 16.0), f"decay{k}")
            @block.vector
            def _(e):
                V.start(e)
                with e.Fori(0, NB) as i:
                    S.wait(e, "k", i)
                    V.done(e.tensor_copy(self.KT[:, bass.ds(i * BLK, BLK)], PS[:, 2, :]), "k")
                    x, (hi, lo) = XT[:, :, bass.ds(i * BLK, BLK)], (t[:, :, bass.ds(i * BLK, BLK)] for t in self.XTp)
                    V.done(e.tensor_copy(hi, x), "xhi")
                    V.wait(e, "xhi", i)
                    V.done(e.tensor_tensor(lo, x, hi.bitcast(F32), ALU.subtract), "xlo")
                V2.start(e)
                for k in range(NB):
                    cols = slice(k * BLK, (k + 1) * BLK)
                    A2.wait(e, f"ln{k}")
                    V2.done(e.scalar_tensor_tensor(out=z[:, cols], in0=z[:, cols], scalar=0.0, in1=az[:, cols], op0=ALU.min,
                                                   op1=ALU.subtract), f"u{k}")

    def gla_scan(self, c):
        nc, PS, XTp, Wvp = self.nc, self.PS, self.XTp, self.Wvp
        sb = lambda n, s, dt=F32: self.sb(c, n, s, dt)
        self.O = O = sb("O", [P, NT, D])
        with ExitStack() as c2:
            sb2 = lambda n, s, dt=F32: self.sb(c2, n, s, dt)
            kv, hs = sb2("kv", [P, 2, T]), sb2("hs", [P, 2, T])
            R, RW = 5, 3
            wcol = sb2("wcol", [P, RW, 2 * KD, P], F32R)
            qh = sb2("qh", [P, R, T])
            OT = sb2("OT", [P, 4, T])
            TBt = T // P
            S = self.steps("gs_pe", self.scan_pe_order())
            on_pool = lambda j: j % 2 == 0
            V = self.steps("gs_dve", [n for j in range(HD) for n in (f"kv{j}", f"h{j}") + (() if on_pool(j) else (f"qh{j}",))])
            C = self.steps("gs_pool", [f"qh{j}" for j in range(HD) if on_pool(j)])
            def qh_(e, steps_, i, j):
                V.wait(e, f"h{j}", i)
                if j >= R:
                    S.wait(e, f"s{(j - R) // 4}", i)
                if on_pool(j):
                    e.sem_inc(self.apart, 1)
                steps_.done(e.tensor_tensor(qh[:, j % R, :], hs[:, j % 2, :], self.QT[:, bass.ds(i * T, T)], ALU.mult), f"qh{j}")
            act_order = [f"w{j}" for j in range(RW)]
            for name in self.scan_pe_order():
                if name[0] == "v" and int(name[1:]) + RW < HD:
                    act_order.append(f"w{int(name[1:]) + RW}")
                elif name[0] == "s":
                    act_order.append("o" + name[1:])
            act_order += [f"tok{t}" for t in range(TBt)]
            A = self.steps("gs_act", act_order)
            with nc.Block() as block:
                @block.tensor
                def _(e):
                    S.start(e)
                    with e.Fori(0, B) as i:
                        def values(j):
                            if j >= 2:
                                V.wait(e, f"kv{j - 2}", i)
                            A.wait(e, f"w{j}", i)
                            for half in range(2):
                                for n, (u, v) in enumerate(((0, 0), (1, 0), (0, 1))):
                                    for kt in range(KD):
                                        last = e.matmul(PS[:, 2 * (j % 2) + half, :], wcol[:, j % RW, u * KD + kt, :], XTp[v][:, kt, bass.ds(i * T + half * BLK, BLK)],
                                                        start=n == 0 and kt == 0, stop=n == 2 and kt == KD - 1)
                            S.done(last, f"v{j}")
                        def sums(g):
                            for r in range(4):
                                (C if on_pool(4 * g + r) else V).wait(e, f"qh{4 * g + r}", i)
                            if g:
                                A.wait(e, f"o{g - 1}", i)
                            for half in range(2):
                                for r in range(4):
                                    last = e.matmul(PS[32 * r:32 * r + 32, 4 + half, :], self.headsum[:, :],
                                                    qh[:, (4 * g + r) % R, half * BLK:(half + 1) * BLK], start=True, stop=True)
                            S.done(last, f"s{g}")
                        def turn(t):
                            A.wait(e, "o3", i)
                            if t >= 2:
                                A.wait(e, f"tok{t - 2}", i)
                            for g in range(4):
                                last = e.transpose(PS[:, 6 + t % 2, g * P:(g + 1) * P], OT[:, g, t * P:(t + 1) * P], self.ident[:, :])
                            S.done(last, f"t{t}")
                        for name in self.scan_pe_order():
                            {"v": values, "s": sums, "t": turn}[name[0]](int(name[1:]))
                @block.vector
                def _(e):
                    V.start(e)
                    with e.Fori(0, B) as i:
                        cols = bass.ds(i * T, T)
                        for j in range(HD):
                            S.wait(e, f"v{j}", i)
                            if j >= 2:
                                V.wait(e, f"h{j - 2}", i)
                            V.done(e.tensor_tensor(kv[:, j % 2, :], PS[:, 2 * (j % 2):2 * (j % 2) + 2, :].rearrange("p b n -> p (b n)"),
                                                   self.KT[:, cols], ALU.mult), f"kv{j}")
                            V.wait(e, f"kv{j}", i)
                            if j >= 2:
                                (C if on_pool(j - 2) else V).wait(e, f"qh{j - 2}", i)
                            V.done(e.tensor_tensor_scan(hs[:, j % 2, :], self.decay[:, cols], kv[:, j % 2, :], 0.0,
                                                        ALU.mult, ALU.add), f"h{j}")
                            if not on_pool(j):
                                qh_(e, V, i, j)
                @block.gpsimd
                def _(e):
                    C.start(e)
                    with e.Fori(0, B) as i:
                        for j in range(HD):
                            if on_pool(j):
                                qh_(e, C, i, j)
                @block.scalar
                def _(e):
                    A.start(e)
                    with e.Fori(0, B) as i:
                        for name in act_order:
                            n = int(name.lstrip("wotk"))
                            if name[0] == "w":
                                S.wait(e, f"v{n - RW}", i) if n >= RW else S.wait_before(e, i)
                                A.done(e.activation(wcol[:, n % RW, :, :].rearrange("p k (h c) -> p k h c", c=DK),
                                                    Wvp[:, :, :, :].rearrange("p u k (h j) -> p j (u k) h", j=HD)[:, n, :, :]
                                                    .unsqueeze(3).broadcast_to((P, 2 * KD, H, DK)), ACT.Copy), name)
                            elif name[0] == "o":
                                S.wait(e, f"s{n}", i)
                                A.done(e.activation(OT[:, n, :], PS[:, 4:6, :].rearrange("p b n -> p (b n)"), ACT.Copy), name)
                            else:
                                S.wait(e, f"t{n}", i)
                                A.done(e.activation(O[:, i * TBt + n, :].rearrange("p (h j) -> p h j", j=HD),
                                                    PS[:, 6 + n % 2, :].rearrange("p (j h) -> p h j", h=32)[:, 0:H, :], ACT.Copy), name)

    def scan_pe_order(self):
        order = ["v0", "v1"]
        for j in range(HD):
            if j + 2 < HD:
                order.append(f"v{j + 2}")
            if j % 4 == 0 and j >= 4:
                order.append(f"s{(j - 3) // 4}")
        order.append(f"s{HD // 4 - 1}")
        return order + [f"t{t}" for t in range(T // P)]

    def gla_out(self, c):
        idxT, cid, win, L = self.idxT, self.cid, self.win, self.L
        nc, PS, X, O, G = self.nc, self.PS, self.X, self.O, self.G
        sb = lambda n, s, dt=F32: self.sb(c, n, s, dt)
        og, ogT, y = sb("og", [P, TB, D]), sb("ogT", [P, KD, BLK]), sb("y", [P, TB, D])
        ms, rs = sb("ms", [P, TB * H]), sb("rs", [P, TB * H])
        st, mv, sd, rstd = sb("st", [P, TB, 6]), sb("mv", [P, TB, 2]), sb("sd", [P, TB]), sb("rstd", [P, TB])
        S = self.steps("go_pe", ["turn", "wo"])
        A = self.steps("go_act", ["ogT1", "sd"])
        V = self.steps("go_dve", ["ogT0", "y", *self.NORM, "out"])
        AF = self.steps("go_act2", ["sq", "sqrt"])
        VF = self.steps("go_dve2", ["ms", "rs", "norm", "gate"])
        R = 8
        assert NB * 4 * 4 == NCTX
        hot, cntT = sb("c_hot", [P, R, T], BF16), sb("c_cntT", [P, T])
        lc, none = sb("c_lc", [P, T // P, P]), sb("c_none", [P, T // P, P])
        CS = self.steps("cc_pe", [f"c{r}" for r in range(R)], before=["zero"])
        CS2 = self.steps("cc_pe2", ["turn"])
        CV = self.steps("cc_dve", [f"hot{r}" for r in range(R)])
        CV2 = self.steps("cc_dve2", ["cnt", "least", "none", "L"])
        CA2 = self.steps("cc_act2", ["ln"])
        def hots(e, i, g):
            it = i * 2 + g // 2
            CS.wait_before(e, it)
            for r in range(4 * (g % 2), 4 * (g % 2) + 4):
                CV.done(e.tensor_scalar(hot[:, r, :], idxT[:, :], cid[:, bass.ds(it * R + r, 1)], None, ALU.is_equal), f"hot{r}")
        def counts(e, i, g):
            it = i * 2 + g // 2
            for r in range(4 * (g % 2), 4 * (g % 2) + 4):
                CV.wait(e, f"hot{r}", it)
                for b in range(2):
                    last = e.matmul(PS[:, 6 + b, :], win[:, bass.ds(it * R + r + P - NCTX, P)], hot[:, r, b * BLK:(b + 1) * BLK],
                                    start=False, stop=False, skip_group_check=True)
                CS.done(last, f"c{r}")
        with nc.Block() as block:
            @block.tensor
            def _(e):
                S.start(e)
                CS.start(e)
                CS2.start(e)
                for b in range(2):
                    last = e.matmul(PS[:, 6 + b, :], win[:, 2 * P:3 * P], idxT[:, b * BLK:(b + 1) * BLK], start=True, stop=False, skip_group_check=True)
                CS.done(last, "zero")
                with e.Fori(0, NB) as i:
                    VF.wait(e, "gate", i)
                    S.done(self.transposes(e, og, 0, (0, 1)), "turn")
                    V.wait(e, "ogT0", i)
                    A.wait(e, "ogT1", i)
                    S.done(self.token_major(e, ogT, self.Wo, (2, 3)), "wo")
                    counts(e, i, 0)
                    counts(e, i, 1)
                    counts(e, i, 2)
                    counts(e, i, 3)
                CV2.wait(e, "cnt")
                for t in range(T // P):
                    last = e.transpose(PS[:, 4 + t // 4, (t % 4) * P:(t % 4 + 1) * P], cntT[:, t * P:(t + 1) * P], self.ident[:, :])
                CS2.done(last, "turn")
            @block.scalar
            def _(e):
                A.start(e)
                CA2.start(e)
                AF.start(e)
                def square(m):
                    AF.done(e.activation(og[:, :, :], O[:, bass.ds((m % NB) * TB, TB), :], ACT.Square, scale=HD ** -0.5), "sq")
                def root(m):
                    VF.wait(e, "ms", m)
                    AF.done(e.activation(rs[:, :], ms[:, :], ACT.Sqrt, bias=self.eps[:, 0:1]), "sqrt")
                square(0)
                root(0)
                with e.Fori(0, NB) as i:
                    S.wait(e, "turn", i)
                    A.done(e.activation(ogT[:, 1, :], PS[:, 1, :], ACT.Copy), "ogT1")
                    square(i + 1)
                    root(i + 1)
                    self.norm_sd(e, A, V, i, mv, sd)
                CV2.wait(e, "least")
                CV2.wait(e, "none")
                CA2.done(e.activation(lc[:, :, :], lc[:, :, :], ACT.Ln), "ln")
            @block.vector
            def _(e):
                V.start(e)
                CV.start(e)
                CV2.start(e)
                VF.start(e)
                byhead = lambda x: x.rearrange("p t (h j) -> p (t h) j", j=HD)
                def mean_squares(m):
                    AF.wait(e, "sq", m)
                    VF.done(e.tensor_reduce(ms[:, :], byhead(og[:, :, :]), AX.X, ALU.add), "ms")
                def gated(m):
                    tiles = bass.ds((m % NB) * TB, TB)
                    AF.wait(e, "sqrt", m)
                    VF.done(e.reciprocal(rs[:, :], rs[:, :]), "rs")
                    VF.wait(e, "rs", m)
                    VF.done(e.tensor_tensor(byhead(og[:, :, :]), byhead(O[:, tiles, :]),
                                            rs[:, :].unsqueeze(2).broadcast_to((P, TB * H, HD)), ALU.mult), "norm")
                    VF.wait(e, "norm", m)
                    VF.done(e.tensor_tensor(og[:, :, :], og[:, :, :], G[:, tiles, :], ALU.mult), "gate")
                mean_squares(0)
                gated(0)
                with e.Fori(0, NB) as i:
                    S.wait(e, "turn", i)
                    V.done(e.tensor_copy(ogT[:, 0, :], PS[:, 0, :]), "ogT0")
                    hots(e, i, 0)
                    mean_squares(i + 1)
                    hots(e, i, 1)
                    gated(i + 1)
                    S.wait(e, "wo", i)
                    V.done(e.tensor_tensor(y[:, :, :], self.pair_banks(2), X[:, bass.ds(i * TB, TB), :], ALU.add), "y")
                    V.wait(e, "y", i)
                    self.norm_stats(e, V, i, lambda t: y[:, t, :], st, mv)
                    hots(e, i, 2)
                    self.norm_rstd(e, V, A, i, sd, rstd)
                    for t in range(TB):
                        last = e.tensor_scalar(X[:, i * TB + t, :], y[:, t, :], mv[:, t, 0:1], rstd[:, t:t + 1],
                                               ALU.subtract, ALU.mult)
                    V.done(last, "out")
                    hots(e, i, 3)
                CS.wait(e, f"c{R - 1}", NCTX // R - 1)
                CV2.done(e.tensor_copy(cntT[:, :], PS[:, 6:8, :].rearrange("p b n -> p (b n)")), "cnt")
                CS2.wait(e, "turn")
                cnt = PS[:, 4:6, :].rearrange("p b (t n) -> p (b t) n", n=P)
                CV2.done(e.tensor_scalar(lc[:, :, :], cnt, 1.0, None, ALU.max), "least")
                CV2.done(e.tensor_scalar(none[:, :, :], cnt, 1.0, 1.0, ALU.min, ALU.subtract), "none")
                CA2.wait(e, "ln")
                CV2.wait(e, "none")
                for b in range(B):
                    last = e.scalar_tensor_tensor(out=L[:, b, :, :], in0=none[:, :, b * NCTX:(b + 1) * NCTX], scalar=-MASKED,
                                                  in1=lc[:, :, b * NCTX:(b + 1) * NCTX], op0=ALU.mult, op1=ALU.add)
                CV2.done(last, "L")


    def cross_buffers(self, c, c2):
        sb = lambda n, s, dt=F32: self.sb(c, n, s, dt)
        self.WqT, self.WoutT = sb("c_WqT", [P, KD, D]), sb("c_WoutT", [P, KD, D])
        self.Kblk = sb("c_Kblk", [P, B, KD, HG, NCTX])
        self.Vblk = sb("c_Vblk", [P, B, H // 2, 2, HD])
        self.half = sb("c_half", [P, 2, HD])
        self.selaug = sb("c_selaug", [P, H // 2, 2, NCTX], F32R)
        self.L = sb("c_L", [P, B, T // P, NCTX])
        sb2 = lambda n, s, dt=F32: self.sb(c2, n, s, dt)
        self.wq, self.wout, self.up, self.down = sb2("c_wq", [P, KD, D]), sb2("c_wout", [P, KD, D]), sb2("c_up", [P, 4, LAT]), sb2("c_down", [P, 1, D])
        self.ctx = sb2("c_ctx", [P, 1, D])
        self.m16 = sb2("c_m16", [P, HG])
        self.idx = sb2("c_idx", [P, T // P, B, NSEL], I32)
        self.idxT = sb2("c_idxT", [P, T], BF16)
        self.cid = sb2("c_cid", [P, NCTX])
        self.win = sb2("c_win", [P, 3 * P], BF16)
        self.s_i, self.s_cw = self.sem("c_i"), self.sem("c_w")
        self.C = self.steps("cs_pool", ["z1", "z2", "z3", "z4", "z5", "cid", "m16a", "half_a", "w1", "sa1", "m16b", "half_b", "w2", "sa2"])

    def load_indices(self, e):
        a, idx, s_i = self.a, self.idx, self.s_i
        for b in range(B):
            e.dma_start(idx[:, :, b, :], a["itok_BxSx64_0_2047"][b].rearrange("(t p) k -> p t k", p=P)).then_inc(s_i, 16)
            e.wait_ge(s_i, 16 * (b + 1))

    def cross_constants(self, e):
        a, C, s_w, m16, half, win, selaug, cid = self.a, self.C, self.s_cw, self.m16, self.half, self.win, self.selaug, self.cid
        C.start(e)
        for t, w in ((self.wq, "L0_xattn_W_q"), (self.wout, "L0_xattn_W_out"), (self.up, "L0_xattn_W_kv_up"), (self.down, "L0_xattn_W_kv_down")):
            e.dma_start(t[:, :, :], a[w].rearrange("(k p) n -> p k n", p=P)).then_inc(s_w, 16)
        e.dma_start(self.ctx[:, 0, :], a["ctx_1024"].rearrange("b c d -> (b c) d")).then_inc(s_w, 16)
        C.done(e.memset(m16[:, :], 1.0), "z1")
        C.done(e.memset(half[:, :, :], 1.0), "z2")
        C.done(e.memset(win[:, :], 0.0), "z3")
        C.done(e.memset(selaug[:, :, :, :].bitcast(F32), 0.0), "z4")
        C.done(e.memset(cid[:, :], 0.0), "z5")
        C.wait(e, "z5")
        C.done(e.iota(cid[:, :], pattern=[[-1, NCTX]], base=NCTX - 1, channel_multiplier=0, allow_small_or_imprecise_dtypes=True), "cid")
        sel = lambda t, op, fill, base, pattern, cm: e.affine_select(out=t, in_=t, compare_op=op, fill=fill, base=base,
                                                                     pattern=pattern, channel_multiplier=cm)
        C.done(sel(m16[:, :], ALU.is_ge, 0.0, 0, [[-HD, HG]], 1), "m16a")
        C.done(sel(half[:, :, :], ALU.is_ge, 0.0, 0, [[-NCTX, 2], [0, HD]], 1), "half_a")
        C.wait(e, "half_a")
        C.done(sel(win[0:NCTX, :], ALU.not_equal, 1.0, -(P - 1), [[1, 3 * P]], 0), "w1")
        C.wait(e, "w1")
        C.done(sel(selaug[:, :, :, :], ALU.not_equal, 1.0, 0, [[0, H // 2], [0, 2], [-1, NCTX]], 1), "sa1")
        C.wait(e, "sa1")
        C.done(sel(m16[:, :], ALU.is_ge, 0.0, HD - 1, [[HD, HG]], -1), "m16b")
        C.done(sel(half[:, :, :], ALU.is_ge, 0.0, NCTX - 1, [[NCTX, 2], [0, HD]], -1), "half_b")
        C.wait(e, "half_b")
        C.done(sel(win[NCTX:P, :], ALU.not_equal, 1.0, -(P - 1 + NCTX), [[1, 3 * P]], 0), "w2")
        C.wait(e, "w2")
        C.done(sel(selaug[:, :, :, :], ALU.not_equal, 1.0, -NCTX, [[-2, H // 2], [-1, 2], [0, NCTX]], 1), "sa2")

    def cross_setup(self):
        nc, PS = self.nc, self.PS
        WqT, WoutT, Kblk, Vblk, half = self.WqT, self.WoutT, self.Kblk, self.Vblk, self.half
        wq, wout, up, down, ctx = self.wq, self.wout, self.up, self.down, self.ctx
        m16, idx, idxT, s_i, s_w, C = self.m16, self.idx, self.idxT, self.s_i, self.s_cw, self.C
        with ExitStack() as c3:
            sb = lambda n, s, dt=F32: self.sb(c3, n, s, dt)
            upT, downT, ctxT = sb("c_upT", [P, 1, 4 * P]), sb("c_downT", [P, KD, P]), sb("c_ctxT", [P, KD, P])
            ckv, ckv2 = sb("c_ckv", [P, P]), sb("c_ckv2", [P, B, 2, NCTX])
            f, f2 = sb("c_f", [P, T // P, B * NSEL]), sb("c_f2", [P, T // P, B * NSEL])
            turned = [("wq", wq, WqT, 2, 2), ("wout", wout, WoutT, 2, 2), ("up", up, upT, 4, 1), ("down", down, downT, 1, 2), ("ctx", ctx, ctxT, 1, 2)]
            S = self.steps("cs_pe", [n for n, *_ in turned] + ["ckv", "k", "v0", "v1", "idx"])
            A = self.steps("cs_act", [n for n, *_ in turned] + ["v0", "v1"])
            V = self.steps("cs_dve", ["neg", "wrap", "clamp", "ckv", "ckv2", "k", "idxT", "vb0", "vb1"])
            with nc.Block() as block:
                @block.tensor
                def _(e):
                    S.start(e)
                    e.wait_ge(s_w, 16 * 5)
                    for n, (name, src, dst, rows, cols) in enumerate(turned):
                        if n >= 2:
                            A.wait(e, turned[n - 2][0])
                        for k in range(cols):
                            for r in range(rows):
                                last = e.transpose(PS[:, 2 * (n % 2) + (k * rows + r) // 4, ((k * rows + r) % 4) * P:((k * rows + r) % 4 + 1) * P],
                                                   src[:, r, k * P:(k + 1) * P], self.ident[:, :])
                        S.done(last, name)
                    A.wait(e, "ctx")
                    for kt in range(KD):
                        last = e.matmul(PS[:, 4, 0:P], downT[:, kt, :], ctxT[:, kt, :], start=kt == 0, stop=kt == KD - 1)
                    S.done(last, "ckv")
                    V.wait(e, "ckv")
                    for g in range(KD):
                        last = e.matmul(PS[:, 5, g * P:(g + 1) * P], upT[:, 0, g * P:(g + 1) * P], ckv[:, :], start=True, stop=True)
                    S.done(last, "k")
                    V.wait(e, "ckv2")
                    for b in range(B):
                        S.done(e.matmul(PS[:, 6 + b, 0:D], ckv2[:, b, :, :].rearrange("p a c -> p (a c)"), upT[:, 0, D:2 * D],
                                        start=True, stop=True), f"v{b}")
                    V.wait(e, "clamp")
                    for t in range(T // P):
                        last = e.transpose(PS[:, t // 4, (t % 4) * P:(t % 4 + 1) * P], f[:, t, :], self.ident[:, :])
                    S.done(last, "idx")
                @block.scalar
                def _(e):
                    A.start(e)
                    for n, (name, src, dst, rows, cols) in enumerate(turned):
                        S.wait(e, name)
                        A.done(e.activation(dst[:, :, :].rearrange("p k n -> p (k n)"), PS[:, 2 * (n % 2), 0:rows * cols * P], ACT.Copy), name)
                    for b in range(B):
                        S.wait(e, f"v{b}")
                        C.wait(e, "half_b")
                        A.done(e.activation(Vblk[:, b, :, :, :].rearrange("p a c d -> p (a c d)"), PS[:, 6 + b, 0:D], ACT.Copy), f"v{b}")
                @block.vector
                def _(e):
                    V.start(e)
                    e.wait_ge(s_i, 16 * B)
                    idx_ = idx[:, :, :, :].rearrange("p t b k -> p t (b k)")
                    V.done(e.tensor_scalar(f2[:, :, :], idx_, 0.0, float(NCTX), ALU.is_lt, ALU.mult), "neg")
                    V.wait(e, "neg")
                    V.done(e.tensor_tensor(f[:, :, :], f2[:, :, :], idx_, ALU.add), "wrap")
                    V.wait(e, "wrap")
                    V.done(e.tensor_scalar(f[:, :, :], f[:, :, :], 0.0, float(NCTX - 1), ALU.max, ALU.min), "clamp")
                    C.wait(e, "sa2")
                    S.wait(e, "ckv")
                    V.done(e.tensor_copy(ckv[:, :], PS[:, 4, 0:P]), "ckv")
                    V.wait(e, "ckv")
                    V.done(e.tensor_copy(ckv2[:, :, :, :], ckv[:, :].rearrange("p (b c) -> p b c", b=B).unsqueeze(2).broadcast_to((P, B, 2, NCTX))), "ckv2")
                    S.wait(e, "k")
                    for b in range(B):
                        for g in range(KD):
                            last = e.tensor_tensor(Kblk[:, b, g, :, :],
                                                   PS[:, 5, g * P + b * NCTX:g * P + (b + 1) * NCTX].unsqueeze(1).broadcast_to((P, HG, NCTX)),
                                                   m16[:, :].unsqueeze(2).broadcast_to((P, HG, NCTX)), ALU.mult)
                    V.done(last, "k")
                    S.wait(e, "idx")
                    V.done(e.tensor_copy(idxT[:, :], PS[:, 0:2, :].rearrange("p b n -> p (b n)")), "idxT")
                    for b in range(B):
                        A.wait(e, f"v{b}")
                        V.done(e.tensor_tensor(Vblk[:, b, :, :, :].rearrange("p a c d -> p a (c d)"), Vblk[:, b, :, :, :].rearrange("p a c d -> p a (c d)"),
                                               half[:, :, :].rearrange("p c d -> p (c d)").unsqueeze(1).broadcast_to((P, H // 2, 2 * HD)), ALU.mult), f"vb{b}")

    def cross_blocks(self, c):
        nc, PS, X, L, ident = self.nc, self.PS, self.X, self.L, self.ident
        sb = lambda n, s, dt=F32: self.sb(c, n, s, dt)
        parts = lambda name, shape: [sb(name + n, shape, F32R) for n in ("_hi", "_lo")]
        xs, xT = sb("xs", [P, TB, D]), parts("xT", [P, KD, BLK])
        aug = sb("aug", [P, TB, P])
        qT, augT = [parts(f"qT{b}", [P, KD, BLK]) for b in range(B)], [parts(f"augT{b}", [P, BLK]) for b in range(B)]
        Wq, K = parts("c_Wqp", [P, KD, D]), parts("c_Kp", [P, B, KD, HG, NCTX])
        Lr, identr = sb("c_Lr", [P, B, T // P, NCTX], F32R), sb("c_idr", [P, P], F32R)
        pr = sb("pr", [P, H // 2, BLK])
        rs, oT, y = sb("c_rs", [P, KD, BLK]), sb("c_oT", [P, KD, BLK]), sb("c_y", [P, TB, D])
        st, mv, sd, rstd = sb("c_st", [P, TB, 6]), sb("c_mv", [P, TB, 2]), sb("c_sd", [P, TB]), sb("c_rstd", [P, TB])
        PASSES = ((0, 0), (1, 0), (0, 1))
        NP_ = H // 2
        s_z = self.sem("cb_z")
        VC = self.steps("cb_const", ["Whi", "Khi", "Wlo", "Klo", "L", "ident"])
        S1 = self.steps("cb_pe1", ["turn", "q"] + [f"s{t}" for t in range(TB)] + ["aug"])
        S2 = self.steps("cb_pe2", [f"e{k}" for k in range(4)] + ["pv0"] + [f"e{k}" for k in range(4, 8)] + ["pv1", "wo"])
        A1 = self.steps("cb_act1", ["xs", "xT1", "q1", "augThi"])
        A2 = self.steps("cb_act2", [f"p{k}" for k in range(NP_)] + ["sd"])
        V1 = self.steps("cb_dve1", ["xT0", "xTlo0", "xTlo1", "q0", "qlo0", "qlo1", "L"] + [f"m{t}" for t in range(TB)] + ["augTlo"])
        V2 = self.steps("cb_dve2", ["rs0", "o0", "rs1", "o1", *self.NORM, "out"])
        VY = self.steps("cb_y", ["y"])
        s_banks = lambda t: PS[:, 2 * (t % 2):2 * (t % 2) + 2, :]
        def blocks(e, body):
            with e.Fori(0, T // BLK) as i:
                for b in range(B):
                    body(i * B + b, b, i, 1 - b, i if b == 0 else (i + 1) % (T // BLK))
        with nc.Block() as block:
            @block.gpsimd
            def _(e):
                e.memset(aug[:, :, NCTX + H:P], 0.0).then_inc(s_z, 1)
            @block.tensor
            def _(e):
                S1.start(e)
                S2.start(e)
                def turn(m):
                    A1.wait(e, "xs", m)
                    S1.done(self.transposes(e, xs, 0, (0, 1)), "turn")
                def q(m):
                    V1.wait_before(e, m)
                    A1.wait_before(e, m)
                    A1.wait(e, "xT1", m)
                    V1.wait(e, "xTlo1", m)
                    for g in range(KD):
                        for n, (u, v) in enumerate(PASSES):
                            for kt in range(KD):
                                last = e.matmul(PS[:, 2 + g, :], Wq[u][:, kt, g * P:(g + 1) * P], xT[v][:, kt, :],
                                                start=n == 0 and kt == 0, stop=n == 2 and kt == KD - 1)
                    S1.done(last, "q")
                def scores(m, b, i, t):
                    V1.wait(e, f"m{t - 2}" if t >= 2 else "qlo1", m)
                    A1.wait(e, "q1", m)
                    for g in range(KD):
                        bank = PS[:, 2 * (t % 2) + g, :]
                        for n, (u, v) in enumerate(PASSES):
                            e.matmul(bank, qT[b][u][:, g, t * P:(t + 1) * P], K[v][:, b, g, :, :].rearrange("p h c -> p (h c)"),
                                     start=n == 0, stop=False)
                        last = e.matmul(bank, identr[:, :], Lr[:, b, i * TB + t, :].unsqueeze(1).broadcast_to((P, HG, NCTX)),
                                        start=False, stop=True)
                    S1.done(last, f"s{t}")
                def turn_aug(m):
                    V1.wait(e, f"m{TB - 1}", m)
                    for t in range(TB):
                        last = e.transpose(PS[:, 2, t * P:(t + 1) * P], aug[:, t, :], ident[:, :])
                    S1.done(last, "aug")
                def exps(m, b, ks):
                    for k in ks:
                        if k == 0:
                            A1.wait(e, "augThi", m)
                            V1.wait(e, "augTlo", m)
                            VY.wait_before(e, m)
                        if k >= 2:
                            A2.wait(e, f"p{k - 2}", m)
                        g, bank = k // 4, PS[:, 4 + k % 2, :]
                        for n, (u, v) in enumerate(PASSES):
                            e.matmul(bank, K[u][:, b, g, 2 * (k % 4):2 * (k % 4) + 2, :].rearrange("p h c -> p (h c)"), qT[b][v][:, g, :],
                                     start=n == 0, stop=False)
                        for v in range(2):
                            last = e.matmul(bank, self.selaug[:, k, :, :].rearrange("p h c -> p (h c)"), augT[b][v][:, :],
                                            start=False, stop=v == 1)
                        S2.done(last, f"e{k}")
                def values(m, b, g):
                    A2.wait(e, f"p{4 * g + 3}", m)
                    if g:
                        V2.wait(e, "o0", m)
                    for r in range(4):
                        e.matmul(PS[32 * r:32 * r + 32, 6, :], self.Vblk[:, b, 4 * g + r, :, :].rearrange("p h d -> p (h d)"),
                                 pr[:, 4 * g + r, :], start=True, stop=True)
                    for r in range(4):
                        last = e.matmul(PS[32 * r:32 * r + 32, 7, :], self.half[:, :, :].rearrange("p h d -> p (h d)"),
                                        pr[:, 4 * g + r, :], start=True, stop=True)
                    S2.done(last, f"pv{g}")
                def wout(m):
                    V2.wait(e, "o1", m)
                    S2.done(self.token_major(e, oT, self.WoutT, (4, 5)), "wo")
                turn(0)
                VC.wait(e, "ident")
                q(0)
                for t in range(TB):
                    scores(0, 0, 0, t)
                e.wait_ge(s_z, 1)
                turn_aug(0)
                def body(m, b, i, nb, ni):
                    turn(m + 1)
                    exps(m, b, (0, 1))
                    q(m + 1)
                    exps(m, b, (2, 3))
                    scores(m + 1, nb, ni, 0)
                    values(m, b, 0)
                    exps(m, b, (4, 5))
                    scores(m + 1, nb, ni, 1)
                    exps(m, b, (6, 7))
                    values(m, b, 1)
                    scores(m + 1, nb, ni, 2)
                    scores(m + 1, nb, ni, 3)
                    wout(m)
                    turn_aug(m + 1)
                blocks(e, body)
            @block.scalar
            def _(e):
                A1.start(e)
                A2.start(e)
                def copy_x(m, b, i):
                    A1.done(e.activation(xs[:, :, :], X[:, bass.ds(b * (T // P) + i * TB, TB), :], ACT.Copy), "xs")
                def xT1(m):
                    S1.wait(e, "turn", m)
                    A1.done(e.activation(xT[0][:, 1, :], PS[:, 1, :], ACT.Copy), "xT1")
                def q1(m, b):
                    S1.wait(e, "q", m)
                    A1.done(e.activation(qT[b][0][:, 1, :], PS[:, 3, :], ACT.Copy, scale=HD ** -0.5), "q1")
                def augThi(m, b):
                    S1.wait(e, "aug", m)
                    A1.done(e.activation(augT[b][0][:, :], PS[:, 2, :], ACT.Copy), "augThi")
                def exps(m, ks):
                    for k in ks:
                        S2.wait(e, f"e{k}", m)
                        A2.done(e.activation(pr[:, k, :], PS[:, 4 + k % 2, :], ACT.Exp), f"p{k}")
                copy_x(0, 0, 0)
                xT1(0)
                q1(0, 0)
                augThi(0, 0)
                def body(m, b, i, nb, ni):
                    copy_x(m + 1, nb, ni)
                    xT1(m + 1)
                    exps(m, (0, 1))
                    q1(m + 1, nb)
                    exps(m, range(2, NP_))
                    augThi(m + 1, nb)
                    self.norm_sd(e, A2, V2, m, mv, sd)
                blocks(e, body)
            @block.vector
            def _(e):
                V1.start(e)
                V2.start(e)
                VY.start(e)
                VC.start(e)
                VC.done(e.tensor_copy(Wq[0][:, :, :], self.WqT[:, :, :]), "Whi")
                VC.done(e.tensor_copy(K[0][:, :, :, :, :], self.Kblk[:, :, :, :, :]), "Khi")
                VC.wait(e, "Khi")
                VC.done(e.tensor_tensor(Wq[1][:, :, :], self.WqT[:, :, :], Wq[0][:, :, :].bitcast(F32), ALU.subtract), "Wlo")
                VC.done(e.tensor_tensor(K[1][:, :, :, :, :], self.Kblk[:, :, :, :, :], K[0][:, :, :, :, :].bitcast(F32), ALU.subtract), "Klo")
                VC.done(e.tensor_copy(Lr[:, :, :, :], L[:, :, :, :]), "L")
                VC.done(e.tensor_copy(identr[:, :], ident[:, :]), "ident")
                def x_parts(m):
                    S1.wait(e, "turn", m)
                    V1.done(e.tensor_copy(xT[0][:, 0, :], PS[:, 0, :]), "xT0")
                    V1.wait(e, "xT0", m)
                    for kt in range(KD):
                        if kt:
                            A1.wait(e, "xT1", m)
                        V1.done(e.tensor_tensor(xT[1][:, kt, :], PS[:, kt, :], xT[0][:, kt, :].bitcast(F32), ALU.subtract), f"xTlo{kt}")
                def q_parts(m, b, i):
                    S1.wait(e, "q", m)
                    V1.done(e.tensor_scalar(qT[b][0][:, 0, :], PS[:, 2, :], HD ** -0.5, None, ALU.mult), "q0")
                    V1.wait(e, "q0", m)
                    for g in range(KD):
                        if g:
                            A1.wait(e, "q1", m)
                        V1.done(e.scalar_tensor_tensor(out=qT[b][1][:, g, :], in0=PS[:, 2 + g, :], scalar=HD ** -0.5,
                                                       in1=qT[b][0][:, g, :].bitcast(F32), op0=ALU.mult, op1=ALU.subtract), f"qlo{g}")
                    V1.done(e.tensor_copy(aug[:, :, 0:NCTX], L[:, b, bass.ds(i * TB, TB), :]), "L")
                def maximum(m, t):
                    S1.wait(e, f"s{t}", m)
                    V1.done(e.tensor_reduce(aug[:, t, NCTX:NCTX + H], s_banks(t).rearrange("p b (h c) -> p (b h) c", c=NCTX),
                                            AX.X, ALU.max, negate=True), f"m{t}")
                def augTlo(m, b):
                    A1.wait(e, "augThi", m)
                    V1.done(e.tensor_tensor(augT[b][1][:, :], PS[:, 2, :], augT[b][0][:, :].bitcast(F32), ALU.subtract), "augTlo")
                def divide(m, g):
                    S2.wait(e, f"pv{g}", m)
                    V2.done(e.reciprocal(rs[:, g, :], PS[:, 7, :]), f"rs{g}")
                    V2.wait(e, f"rs{g}", m)
                    V2.done(e.tensor_tensor(oT[:, g, :], PS[:, 6, :], rs[:, g, :], ALU.mult), f"o{g}")
                x_parts(0)
                q_parts(0, 0, 0)
                for t in range(TB):
                    maximum(0, t)
                augTlo(0, 0)
                def body(m, b, i, nb, ni):
                    tile0 = b * (T // P) + i * TB
                    x_parts(m + 1)
                    q_parts(m + 1, nb, ni)
                    maximum(m + 1, 0)
                    divide(m, 0)
                    maximum(m + 1, 1)
                    divide(m, 1)
                    maximum(m + 1, 2)
                    maximum(m + 1, 3)
                    S2.wait(e, "wo", m)
                    VY.done(e.tensor_tensor(y[:, :, :], self.pair_banks(4), X[:, bass.ds(tile0, TB), :], ALU.add), "y")
                    augTlo(m + 1, nb)
                    VY.wait(e, "y", m)
                    self.norm_stats(e, V2, m, lambda t: y[:, t, :], st, mv)
                    self.norm_rstd(e, V2, A2, m, sd, rstd)
                    for t in range(TB):
                        last = e.tensor_scalar(X[:, tile0 + t, :], y[:, t, :], mv[:, t, 0:1], rstd[:, t:t + 1], ALU.subtract, ALU.mult)
                    V2.done(last, "out")
                blocks(e, body)


    def row_norm_affine(self, e, V, A, i, src, dst, mv, sd, rstd, gain, bias, tag):
        self.norm_rstd(e, V, A, i, sd, rstd)
        for t in range(TB):
            last = e.tensor_scalar(dst[:, t, :], src[:, t, :], mv[:, t, 0:1], rstd[:, t:t + 1], ALU.subtract, ALU.mult)
        V.done(last, tag + "_n")
        V.wait(e, tag + "_n", i)
        V.done(e.tensor_tensor(dst[:, :, :], dst[:, :, :], gain[:, :].unsqueeze(1).broadcast_to((P, TB, D)), ALU.mult), tag + "_g")
        V.wait(e, tag + "_g", i)
        V.done(e.tensor_tensor(dst[:, :, :], dst[:, :, :], bias[:, :].unsqueeze(1).broadcast_to((P, TB, D)), ALU.add), tag)

    def self_attention(self, experts=True):
        nc = self.nc
        self.parts = nc.dram_tensor("qk_parts", (4, B * D, T), F32).ap()
        with ExitStack() as c2:
            self.OT = self.sb(c2, "OT_all", [P, B * H // 4, T])
            with ExitStack() as c3:
                self.V = self.sb(c3, "V", [P, NT, H, 2 * HD])
                self.attend_buffers(c3)
                with ExitStack() as c4:
                    self.qkv(c4)
                with ExitStack() as c4:
                    self.attend(c4)
            self.expert_buffers(c2)
            with ExitStack() as c3:
                self.route(c3)
            if experts:
                with ExitStack() as c3:
                    self.experts(c3)

    def qkv(self, c):
        nc, a, PS, X, V_ = self.nc, self.a, self.PS, self.X, self.V
        sb = lambda n, s, dt=F32: self.sb(c, n, s, dt)
        Wq, Wk, Wv = sb("f_Wq", [P, KD, D]), sb("f_Wk", [P, KD, D]), sb("f_Wv", [P, KD, D])
        g1, b1, bv = sb("f_g1", [P, D]), sb("f_b1", [P, D]), sb("f_bv", [P, D])
        bq, bk, bqs = sb("f_bq", [P, KD]), sb("f_bk", [P, KD]), sb("f_bqs", [P, KD])
        h, hT = sb("f_h", [P, TB, D]), sb("f_hT", [P, KD, BLK])
        qf, kf = sb("f_q", [P, KD, BLK]), sb("f_k", [P, KD, BLK])
        part = [sb(n, [P, KD, BLK], F32R) for n in ("f_qhi", "f_qlo", "f_khi", "f_klo")]
        st, mv, sd, rstd = sb("f_st", [P, TB, 6]), sb("f_mv", [P, TB, 2]), sb("f_sd", [P, TB]), sb("f_rstd", [P, TB])
        s_w, s_st, s_z, s_k, s_b = self.sem("f_w"), self.sem("f_store"), self.sem("f_z"), self.sem("f_const"), self.sem("f_b")
        S = self.steps("f_pe", ["turn", "q", "k", "v"])
        A = self.steps("f_act", ["hT1", "q", "k"])
        V = self.steps("f_dve", ["hT0", "qhi", "qlo", "khi", "klo", "v"])
        AN = self.steps("f_nact", ["sd"])
        VN = self.steps("f_ndve", [*self.NORM, "h_n", "h_g", "h"])
        n_w = 16 * 8
        with nc.Block() as block:
            @block.gpsimd
            def _(e):
                for t, w in ((Wq, "Wq"), (Wk, "Wk"), (Wv, "Wv")):
                    e.dma_start(t[:, :, :], a["L0_ffn_" + w].rearrange("(k p) n -> p k n", p=P)).then_inc(s_w, 16)
                for t, w in ((g1, "ln1_g"), (b1, "ln1_b"), (bv, "bv")):
                    e.dma_start(t[:, :], a["L0_ffn_" + w].partition_broadcast(P)).then_inc(s_w, 16)
                for t, w in ((bq, "bq"), (bk, "bk")):
                    e.dma_start(t[:, :], a["L0_ffn_" + w].rearrange("(k p) -> p k", p=P), allow_slow_non_contiguous=True).then_inc(s_w, 16)
                e.memset(V_[:, :, :, HD:2 * HD], 1.0).then_inc(s_z, 1)
                self.attend_constants(e, s_k)
            @block.tensor
            def _(e):
                S.start(e)
                e.wait_ge(s_w, n_w)
                with e.Fori(0, NB) as i:
                    VN.wait(e, "h", i)
                    V.wait_before(e, i)
                    A.wait_before(e, i)
                    S.done(self.transposes(e, h, 0, (0, 1)), "turn")
                    V.wait(e, "hT0", i)
                    A.wait(e, "hT1", i)
                    for name, w, bank in (("q", Wq, 2), ("k", Wk, 4)):
                        for g in range(KD):
                            for kt in range(KD):
                                last = e.matmul(PS[:, bank + g, :], w[:, kt, g * P:(g + 1) * P], hT[:, kt, :], start=kt == 0, stop=kt == KD - 1)
                        S.done(last, name)
                    S.done(self.token_major(e, hT, Wv, (6, 7)), "v")
            @block.scalar
            def _(e):
                A.start(e)
                e.wait_ge(s_w, n_w)
                e.activation(bqs[:, :], bq[:, :], ACT.Copy, scale=HD ** -0.5).then_inc(s_b, 1)
                e.wait_ge(s_b, 1)
                AN.start(e)
                self.norm_sd(e, AN, VN, 0, mv, sd)
                with e.Fori(0, NB) as i:
                    S.wait(e, "turn", i)
                    A.done(e.activation(hT[:, 1, :], PS[:, 1, :], ACT.Copy), "hT1")
                    self.norm_sd(e, AN, VN, i + 1, mv, sd)
                    for name, dst, bias, bank, scale in (("q", qf, bqs, 2, HD ** -0.5), ("k", kf, bk, 4, 1.0)):
                        S.wait(e, name, i)
                        for g in range(KD):
                            last = e.activation(dst[:, g, :], PS[:, bank + g, :], ACT.Identity, bias=bias[:, g:g + 1], scale=scale)
                        A.done(last, name)
            @block.vector
            def _(e):
                V.start(e)
                e.wait_ge(s_w, n_w)
                VN.start(e)
                def norm(m):
                    blk = m % NB
                    self.norm_stats(e, VN, m, lambda t: X[:, blk * TB + t, :], st, mv)
                    self.row_norm_affine(e, VN, AN, m, X[:, bass.ds(blk * TB, TB), :], h, mv, sd, rstd, g1, b1, "h")
                norm(0)
                with e.Fori(0, NB) as i:
                    S.wait(e, "turn", i)
                    V.done(e.tensor_copy(hT[:, 0, :], PS[:, 0, :]), "hT0")
                    norm(i + 1)
                    for n, (name, src) in enumerate((("q", qf), ("k", kf))):
                        hi, lo = part[2 * n], part[2 * n + 1]
                        A.wait(e, name, i)
                        e.wait_ge(s_st, 16 + 16 * 4 * i)
                        V.done(e.tensor_copy(hi[:, :, :], src[:, :, :]), name + "hi")
                        V.wait(e, name + "hi", i)
                        V.done(e.tensor_tensor(lo[:, :, :], src[:, :, :], hi[:, :, :].bitcast(F32), ALU.subtract), name + "lo")
                    S.wait(e, "v", i)
                    e.wait_ge(s_z, 1)
                    V.done(e.tensor_tensor(V_[:, bass.ds(i * TB, TB), :, 0:HD], self.pair_banks(6).rearrange("p t (h d) -> p t h d", h=H),
                                           bv[:, :].rearrange("p (h d) -> p h d", h=H).unsqueeze(1).broadcast_to((P, TB, H, HD)), ALU.add), "v")
            @block.sync
            def _(e):
                e.sem_inc(s_st, 16)
                dst = self.parts.rearrange("q (b g p) t -> q b p g t", b=B, g=KD)
                with e.Fori(0, B) as b:
                    with e.Fori(0, T // BLK) as cc:
                        for n, name in enumerate(("qhi", "qlo", "khi", "klo")):
                            V.wait(e, name, b * 2 + cc)
                            e.dma_start(dst[n, b, :, :, bass.ds(cc * BLK, BLK)], part[n][:, :, :].bitcast(F32)).then_inc(s_st, 16)
                e.wait_ge(s_st, 16 + 16 * 4 * NB)

    def attend_buffers(self, c):
        sb = lambda n, s, dt=F32: self.sb(c, n, s, dt)
        self.Q = [sb(f"aQ{p}", [P, 2, T], F32R) for p in range(2)]
        self.K = [sb(f"aK{p}", [P, 2, 2, T], F32R) for p in range(2)]
        self.identr, self.maskq, self.maskk = sb("a_idr", [P, P], F32R), sb("a_mq", [P, P], F32R), sb("a_mk", [P, P], F32R)

    def attend_constants(self, e, s):
        for t in (self.identr[:, :], self.maskq[:, :], self.maskk[:, :], self.Q[0][:, :, :], self.Q[1][:, :, :],
                  self.K[0][:, :, :, :], self.K[1][:, :, :, :]):
            e.memset(t.bitcast(F32), 0.0).then_inc(s, 1)
        e.wait_ge(s, 7)
        sel = lambda t, op, fill, pattern, cm: e.affine_select(out=t[:, :], in_=t[:, :], compare_op=op, fill=fill, base=0,
                                                               pattern=pattern, channel_multiplier=cm).then_inc(s, 1)
        sel(self.identr, ALU.not_equal, 1.0, [[-1, P]], 1)
        sel(self.maskq, ALU.is_ge, MASKED, [[-1, P]], 1)
        sel(self.maskk, ALU.is_ge, MASKED, [[1, P]], -1)
        e.wait_ge(s, 10)
        for p in range(2):
            for par in range(2):
                r = self.AUG + P // 2 * par
                e.memset(self.K[p][r:r + 2, :, par, :].bitcast(F32), 1.0).then_inc(s, 1)
        e.wait_ge(s, 14)

    AUG = 2 * HD

    def attend(self, c):
        nc, PS, V_, OT, Q, K = self.nc, self.PS, self.V, self.OT, self.Q, self.K
        sb = lambda n, s, dt=F32: self.sb(c, n, s, dt)
        NG, NK, G4, HALF, AUG = B * H // 4, T // P, 4, P // 2, self.AUG
        NQ = T // BLK
        Vs = [sb(f"aV{p}", [P, NK, G4, 2 * HD]) for p in range(2)]
        R = 2
        Pb = [sb(f"aP{r}", [P, G4, BLK]) for r in range(R)]
        nm = sb("a_nm", [P, 2, 2, NK])
        nm2 = sb("a_nm2", [P, 2, 2, NK // 2])
        nmp = sb("a_nmp", [P, 2, NK, 2, HALF], F32R)
        part_cols = lambda pair, part: nmp[:, pair, :, :, AUG + part].rearrange("p t r -> p r t")
        parts = self.parts.rearrange("q (n s r2 r) t -> q n r2 s r t", s=2, r2=2, r=HD)
        steps = [(qb, kt) for qb in range(NQ) for kt in range(TB * (qb + 1))]
        last_step = len(steps) - 1
        head = [(4, 0), (0, 0), (3, 0), (4, 1), (5, 0), (1, 0), (7, 1), (5, 1), (6, 0), (2, 0), (7, 0), (6, 1)]
        chunks = [(j, qt, cb) for j in range(G4) for qt, cb in head]
        half = len(chunks) // 2
        FIRST = 3
        per = 2
        users, feed = [], []
        for n in range(len(chunks)):
            users.append(f"c{n}")
            feed.append(f"c{n}")
            if n == half + 2:
                users += ["T0", "T0"]
                feed.append("T0")
                assert (len(users) - 2) % 3 == 0
                users.append("-")
        while len(users) % 3:
            users.append("-")
        users += ["T1", "T1"]
        bank = {u: 5 + users.index(u) % 3 for u in users if u != "-"}
        def freed_by(u):
            at = users.index(u)
            n = 2 if u[0] == "T" else 1
            return [next((users[k] for k in range(at + m - 3, -1, -3) if users[k] != "-"), None) for m in range(n)]
        order = []
        for s in range(len(steps)):
            for item in (f"e{s}a", f"e{s}b", f"pv{s - 1}"):
                if item == f"pv{last_step - 1}":
                    order.append("T1")
                if item != "pv-1":
                    order.append(item)
                if s >= FIRST:
                    k = 0
                    while feed and k < per:
                        u = feed.pop(0)
                        order.append(u)
                        k += u[0] == "c"
        order.append(f"pv{last_step}")
        ahead = [u for u in order if u[0] in "cT"]
        split = lambda u: {f"c{half - 1}": [u, "min0", "hi0", "lo0"], f"c{2 * half - 1}": [u, "min1", "hi1", "lo1"]}.get(u, [u])
        v_of = lambda seq: [n for u in seq for n in (split(u) if u[0] == "c" else [f"r{u[1]}"] if u[0] == "T" else
                                                     ["o1"] if u == f"pv{last_step}" else [])]
        a_of = lambda seq: [n for u in seq for n in ((["o0"] if u == f"e{TB + 1}a" else []) + ["p" + u[1:]] if u[0] == "e" else
                                                     [f"r{u[1]}"] if u[0] == "T" else [])]
        two = lambda names: [f"{n}.{p}" for p in range(2) for n in names]
        first = lambda names: [f"{n}.-" for n in names]
        S = self.steps("a_pe", two(order), first(ahead))
        V = self.steps("a_dve", two(v_of(order)), first(v_of(ahead) + ["o1"]))
        a_steps = a_of(order)
        r0, r1 = a_steps.index("r0"), a_steps.index("r1")
        A = self.steps("a_act", two(a_of(order)), first(a_steps[r0:]))
        C = self.steps("a_pool", two(["z0", "z1", "vs"]), ["zero", "vs.-"])
        s_ld = [[self.sem(f"a_ld{p}{q}") for q in range(2)] for p in range(2)]
        n_ld = 16 * 12

        def prev(steps_, eng, name, p, i):
            steps_.wait(eng, f"{name}.{1 - p}", i if p else i - 1)

        def span(j, qt, cb):
            return min(BLK, (qt + 1) * P - cb * BLK), (qt + 1) * P <= (cb + 1) * BLK

        with nc.Block() as block:
            @block.gpsimd
            def _(e):
                C.start(e)
                C.done(e.memset(nmp[:, :, :, :, :].bitcast(F32), 0.0), "zero")
                C.wait(e, "zero")
                C.done(e.tensor_copy(Vs[0][:, :, :, :], V_[:, 0:NK, 0:G4, :]), "vs.-")
                with e.Fori(0, NG // 2) as i:
                    for p in range(2):
                        n = (i * 2 + p + 1) % NG
                        prev(S, e, f"e{last_step}b", p, i)
                        prev(C, e, "vs", p, i)
                        e.sem_inc(self.apart, 1)
                        for q in range(2):
                            e.memset(Q[1 - p][AUG:AUG + 2, q, :].bitcast(F32), 0.0)
                            C.done(e.memset(Q[1 - p][AUG + HALF:AUG + HALF + 2, q, :].bitcast(F32), 0.0), f"z{q}.{p}")
                        prev(S, e, f"pv{last_step}", p, i)
                        C.wait(e, f"z1.{p}", i)
                        e.sem_inc(self.apart, 1)
                        C.done(e.tensor_copy(Vs[1 - p][:, :, :, :], V_[:, bass.ds((n // 4) * NK, NK), bass.ds((n % 4) * G4, G4), :]), f"vs.{p}")
            def loads(e, p, n):
                for q in range(2):
                    for par in range(2):
                        for dst, slots in ((Q[p][:, q, :], ((0, 0), (1, 0), (3, 1))), (K[p][:, q, par, :], ((0, 2), (1, 3), (3, 2)))):
                            for slot, part in slots:
                                r = HALF * par + HD * slot
                                e.dma_start(dst[r:r + HD, :].bitcast(F32), parts[part, n, par, q, :, :]).then_inc(s_ld[p][q], 16)
            @block.sync
            def _(e):
                loads(e, 0, 0)
                with e.Fori(0, NG // 2) as i:
                    for p in range(2):
                        prev(S, e, f"e{last_step}b", p, i)
                        loads(e, 1 - p, (i * 2 + p + 1) % NG)

            @block.tensor
            def _(e):
                S.start(e)
                def take(u, p, tag, i):
                    for f in freed_by(u):
                        if f is None:
                            if p is not None:
                                prev(V, e, "r1", p, i)
                                prev(A, e, "r1", p, i)
                        elif f[0] == "c":
                            V.wait(e, f + tag, i)
                        else:
                            V.wait(e, "r" + f[1] + tag, i)
                            A.wait(e, "r" + f[1] + tag, i)
                def chunk(u, p, q, tag, i):
                    n = int(u[1:])
                    j, qt, cb = chunks[n]
                    if n % half == 0:
                        pair = n // half
                        if p is None:
                            e.wait_ge(s_ld[q][pair], n_ld)
                        else:
                            e.wait_ge(s_ld[q][pair], n_ld * (i + 1 + (p == 1)))
                            C.wait(e, f"z{pair}" + tag, i)
                    take(u, p, tag, i)
                    w, diag = span(j, qt, cb)
                    last = e.matmul(PS[:, bank[u], 0:w], Q[q][:, j // 2, qt * P:(qt + 1) * P], K[q][:, j // 2, j % 2, cb * BLK:cb * BLK + w],
                                    start=True, stop=not diag)
                    if diag:
                        last = e.matmul(PS[:, bank[u], w - P:w], self.identr[:, :], self.maskq[:, :], start=False, stop=True)
                    S.done(last, u + tag)
                def turn(u, p, tag, i):
                    pair = int(u[1])
                    take(u, p, tag, i)
                    V.wait(e, f"lo{pair}" + tag, i)
                    for qt in range(NK):
                        last = e.matmul(PS[:, bank[u] + qt // TB, (qt % TB) * P:(qt % TB + 1) * P],
                                        nmp[:, pair, qt, :, :].rearrange("p r c -> p (r c)"), self.identr[:, :], start=True, stop=True)
                    S.done(last, u + tag)
                for u in ahead:
                    (chunk(u, None, 0, ".-", 0) if u[0] == "c" else turn(u, None, ".-", 0))
                with e.Fori(0, NG // 2) as i:
                    for p in range(2):
                        tag = f".{p}"
                        def scores(s, x):
                            qb, kt = steps[s]
                            c0, diag = max(0, kt - TB * qb) * P, kt >= TB * qb
                            if s:
                                A.wait(e, f"p{s - 1}{x}" + tag, i)
                            else:
                                prev(A, e, f"p{last_step}{x}", p, i)
                                prev(V, e, f"r{'ab'.index(x)}", p, i)
                                prev(A, e, f"r{'ab'.index(x)}", p, i)
                            for j in ((0, 1), (2, 3))["ab".index(x)]:
                                last = e.matmul(PS[:, j, c0:BLK], K[p][:, j // 2, j % 2, kt * P:(kt + 1) * P],
                                                Q[p][:, j // 2, qb * BLK + c0:(qb + 1) * BLK], start=True, stop=not diag)
                                if diag:
                                    last = e.matmul(PS[:, j, c0:c0 + P], self.identr[:, :], self.maskk[:, :], start=False, stop=True)
                            S.done(last, f"e{s}{x}" + tag)
                        def pv(s):
                            qb, kt = steps[s]
                            c0 = max(0, kt - TB * qb) * P
                            A.wait(e, f"p{s}b" + tag, i)
                            if s == 0:
                                prev(C, e, "vs", p, i)
                                prev(V, e, "o1", p, i)
                            elif kt == 0:
                                A.wait(e, "o0" + tag, i)
                            for j in range(G4):
                                last = e.matmul(PS[32 * j:32 * j + 32, 4, c0:BLK], Vs[p][:, kt, j, :], Pb[s % R][:, j, c0:BLK],
                                                start=kt == 0, stop=kt == TB * (qb + 1) - 1, skip_group_check=True)
                            S.done(last, f"pv{s}" + tag)
                        for u in order:
                            if u[0] == "e":
                                scores(int(u[1:-1]), u[-1])
                            elif u[0] == "p":
                                pv(int(u[2:]))
                            elif u[0] == "c":
                                chunk(u, p, 1 - p, tag, i)
                            else:
                                turn(u, p, tag, i)

            def rows(pair, par, q, tag):
                r, b0 = AUG + HALF * par, bank[f"T{pair}"]
                return Q[q][r:r + 2, pair, :], PS[r:r + 2, b0:b0 + 2, :].rearrange("p b n -> p (b n)")

            @block.scalar
            def _(e):
                A.start(e)
                for pair, between in ((0, r1 - r0 - 1), (1, len(a_steps) - 1 - r1)):
                    S.wait(e, f"T{pair}.-")
                    A.done(e.activation(*rows(pair, 0, 0, ".-"), ACT.Copy), f"r{pair}.-")
                    A.wait(e, f"r{pair}.-")
                    if between:
                        e.sem_inc(A.sem, between)
                with e.Fori(0, NG // 2) as i:
                    for p in range(2):
                        tag = f".{p}"
                        for u in a_steps:
                            if u == "o0":
                                S.wait(e, f"pv{TB - 1}" + tag, i)
                                A.done(e.activation(OT[:, i * 2 + p, 0:BLK], PS[:, 4, :], ACT.Copy), u + tag)
                            elif u[0] == "r":
                                S.wait(e, f"T{u[1]}" + tag, i)
                                A.done(e.activation(*rows(int(u[1]), 0, 1 - p, tag), ACT.Copy), u + tag)
                            else:
                                s, x = int(u[1:-1]), u[-1]
                                c0, j0 = max(0, steps[s][1] - TB * steps[s][0]) * P, 2 * "ab".index(x)
                                if s >= R:
                                    S.wait(e, f"pv{s - R}" + tag, i)
                                else:
                                    prev(S, e, f"pv{last_step + 1 - R + s}", p, i)
                                S.wait(e, f"e{s}{x}" + tag, i)
                                A.done(e.activation(Pb[s % R][:, j0:j0 + 2, c0:BLK], PS[:, j0:j0 + 2, c0:BLK], ACT.Exp), u + tag)

            @block.vector
            def _(e):
                V.start(e)
                C.wait(e, "zero")
                def work(names, q, tag, i):
                    for u in names:
                        pair = int(u[-1])
                        if u[0] == "c":
                            j, qt, cb = chunks[int(u[1:])]
                            dst = nm2[:, j // 2, j % 2, qt - TB:qt - TB + 1] if cb else nm[:, j // 2, j % 2, qt:qt + 1]
                            S.wait(e, u + tag, i)
                            V.done(e.tensor_reduce(dst, PS[:, bank[u], 0:span(j, qt, cb)[0]], AX.X, ALU.max, negate=True), u + tag)
                        elif u[:3] == "min":
                            V.wait(e, f"c{half * (pair + 1) - 1}" + tag, i)
                            late = nm[:, pair, :, TB:NK]
                            V.done(e.tensor_tensor(late, late, nm2[:, pair, :, :], ALU.min), u + tag)
                        elif u[:2] == "hi":
                            V.wait(e, f"min{pair}" + tag, i)
                            V.done(e.tensor_copy(part_cols(pair, 0), nm[:, pair, :, :]), u + tag)
                        elif u[:2] == "lo":
                            V.wait(e, f"hi{pair}" + tag, i)
                            V.done(e.tensor_tensor(part_cols(pair, 1), nm[:, pair, :, :], part_cols(pair, 0).bitcast(F32),
                                                   ALU.subtract), u + tag)
                        elif u[0] == "r":
                            S.wait(e, f"T{pair}" + tag, i)
                            V.done(e.tensor_copy(*rows(pair, 1, q, tag)), u + tag)
                work(v_of(ahead), 0, ".-", 0)
                V.wait(e, "r1.-")
                e.sem_inc(V.sem, 1)
                with e.Fori(0, NG // 2) as i:
                    for p in range(2):
                        tag = f".{p}"
                        work(v_of(order)[:-1], 1 - p, tag, i)
                        S.wait(e, f"pv{last_step}" + tag, i)
                        V.done(e.tensor_copy(OT[:, i * 2 + p, BLK:2 * BLK], PS[:, 4, :]), "o1" + tag)


    def route(self, c):
        nc, a, PS, X, OT = self.nc, self.a, self.PS, self.X, self.OT
        sb = lambda n, s, dt=F32: self.sb(c, n, s, dt)
        NG4 = H // 4
        Wo, bo, g2, b2 = sb("r_Wo", [P, KD, D]), sb("r_bo", [P, D]), sb("r_g2", [P, D]), sb("r_b2", [P, D])
        Wr, br, eb2 = sb("r_Wr", [P, KD, E]), sb("r_br", [P, E]), sb("r_eb2", [E, D])
        os_, rec, on, onT = sb("r_os", [P, NG4, BLK]), sb("r_rec", [P, TB, H]), sb("r_on", [P, TB, D]), sb("r_onT", [P, KD, BLK])
        ya, h2, h2T = sb("r_a", [P, TB, D]), sb("r_h2", [P, TB, D]), sb("r_h2T", [P, KD, BLK])
        lg, best, keep, ex, ws, wT = (sb("r_lg", [P, TB, E]), sb("r_best", [P, TB, 8]), sb("r_keep", [P, TB, E]), sb("r_ex", [P, TB, E]),
                                      sb("r_ws", [P, TB]), sb("r_wT", [E, BLK]))
        st, mv, sd, rstd = sb("r_st", [P, TB, 6]), sb("r_mv", [P, TB, 2]), sb("r_sd", [P, TB]), sb("r_rstd", [P, TB])
        s_w = self.sem("r_w")
        n_w = 16 * 7
        SA = self.steps("r_pe", [f"ot{t}" for t in range(TB)] + ["onT", "wo"])
        SB = self.steps("r_pe2", ["h2T", "lg", "wT", "b2"])
        AA = self.steps("r_act", ["os", "onT1", "sd"])
        AB = self.steps("r_act2", ["h2T1", "ex", "wT"])
        VA = self.steps("r_dve", [n for t in range(TB) for n in (f"rec{t}", f"on{t}")]
                        + ["onT0", "xb", "a", "xa", *self.NORM, "h2_n", "h2_g", "h2"])
        VB = self.steps("r_dve2", ["h2T0", "hi", "lo", "lg", "best", "keep", "sh", "w_", "ws", "wr", "w", "x"])
        with nc.Block() as block:
            @block.gpsimd
            def _(e):
                e.dma_start(Wo[:, :, :], a["L0_ffn_Wo"].rearrange("(k p) n -> p k n", p=P)).then_inc(s_w, 16)
                e.dma_start(Wr[:, :, :], a["L0_ffn_Wr"].rearrange("(k p) n -> p k n", p=P)).then_inc(s_w, 16)
                for t, w in ((bo, "bo"), (g2, "ln2_g"), (b2, "ln2_b"), (br, "br")):
                    e.dma_start(t[:, :], a["L0_ffn_" + w].partition_broadcast(P)).then_inc(s_w, 16)
                e.dma_start(eb2[:, :], a["L0_ffn_e_b2"]).then_inc(s_w, 16)
                self.W.start(e)
                for p in range(2):
                    self.split_weights(e, p, "-", 0, p)
            @block.sync
            def _(e):
                self.load_weights(e, 0)
                for p, (name, load) in ((1, x) for x in (("w1lo", self.load_w1), ("w2lo", self.load_w2))):
                    self.W.wait(e, f"{name}0-")
                    load(e, p)
            @block.tensor
            def _(e):
                SA.start(e)
                SB.start(e)
                e.wait_ge(s_w, n_w)
                def ot(i):
                    AA.wait(e, "os", i)
                    for t in range(TB):
                        if t >= 2:
                            VA.wait(e, f"on{t - 2}", i)
                        for g in range(NG4):
                            last = e.transpose(PS[:, t % 2, g * P:(g + 1) * P], os_[:, g, t * P:(t + 1) * P], self.ident[:, :])
                        SA.done(last, f"ot{t}")
                def onT_(i):
                    VA.wait(e, f"on{TB - 1}", i)
                    SA.done(self.transposes(e, on, 0, (2, 3)), "onT")
                def wo(i):
                    VA.wait(e, "onT0", i)
                    AA.wait(e, "onT1", i)
                    SA.done(self.token_major(e, onT, Wo, (0, 1)), "wo")
                def h2T_(i):
                    VA.wait(e, "h2", i)
                    SB.done(self.transposes(e, h2, 0, (4, 5)), "h2T")
                def logits(i):
                    VB.wait(e, "h2T0", i)
                    AB.wait(e, "h2T1", i)
                    for t in range(TB):
                        for kt in range(KD):
                            last = e.matmul(PS[:, 6, t * E:(t + 1) * E], h2T[:, kt, t * P:(t + 1) * P], Wr[:, kt, :], start=kt == 0, stop=kt == KD - 1)
                    SB.done(last, "lg")
                def biases(i):
                    VB.wait(e, "w", i)
                    for t in range(TB):
                        last = e.transpose(PS[0:E, 7, t * P:(t + 1) * P], ex[:, t, :], self.ident[:, :])
                    SB.done(last, "wT")
                    AB.wait(e, "wT", i)
                    for t in range(TB):
                        last = e.matmul(PS[:, 4 + t // 2, (t % 2) * D:(t % 2 + 1) * D], wT[:, t * P:(t + 1) * P], eb2[:, :], start=True, stop=True)
                    SB.done(last, "b2")
                ot(0)
                onT_(0)
                wo(0)
                with e.Fori(0, NB - 1) as i:
                    VB.wait_before(e, i)
                    h2T_(i)
                    ot(i + 1)
                    logits(i)
                    onT_(i + 1)
                    wo(i + 1)
                    biases(i)
                VB.wait_before(e, NB - 1)
                h2T_(NB - 1)
                logits(NB - 1)
                biases(NB - 1)
            @block.scalar
            def _(e):
                AA.start(e)
                AB.start(e)
                def first_sums(i):
                    SA.wait_before(e, i)
                    AA.done(e.activation(os_[:, :, :], OT[:, bass.ds((i // 2) * NG4, NG4), bass.ds((i % 2) * BLK, BLK)], ACT.Copy), "os")
                def onT1(i):
                    SA.wait(e, "onT", i)
                    AA.done(e.activation(onT[:, 1, :], PS[:, 3, :], ACT.Copy), "onT1")
                def h2T1(i):
                    SB.wait(e, "h2T", i)
                    AB.done(e.activation(h2T[:, 1, :], PS[:, 5, :], ACT.Copy), "h2T1")
                def exps(i):
                    VB.wait(e, "sh", i)
                    AB.done(e.activation(ex[:, :, :], lg[:, :, :], ACT.Exp), "ex")
                def wT_(i):
                    SB.wait(e, "wT", i)
                    AB.done(e.activation(wT[:, :], PS[0:E, 7, :], ACT.Copy), "wT")
                first_sums(0)
                onT1(0)
                self.norm_sd(e, AA, VA, 0, mv, sd)
                with e.Fori(0, NB - 1) as i:
                    first_sums(i + 1)
                    h2T1(i)
                    exps(i)
                    onT1(i + 1)
                    wT_(i)
                    self.norm_sd(e, AA, VA, i + 1, mv, sd)
                h2T1(NB - 1)
                exps(NB - 1)
                wT_(NB - 1)
            @block.vector
            def _(e):
                VA.start(e)
                VB.start(e)
                e.wait_ge(s_w, n_w)
                bc = lambda v, n: v.unsqueeze(2).broadcast_to((P, TB, n))
                def divide(i):
                    for t in range(TB):
                        SA.wait(e, f"ot{t}", i)
                        o = PS[:, t % 2, :].rearrange("p (h c) -> p h c", c=2 * HD)
                        VA.done(e.reciprocal(rec[:, t, :], o[:, :, HD]), f"rec{t}")
                        VA.wait(e, f"rec{t}", i)
                        VA.done(e.tensor_tensor(on[:, t, :].rearrange("p (h d) -> p h d", h=H), o[:, :, 0:HD],
                                                rec[:, t, :].unsqueeze(2).broadcast_to((P, H, HD)), ALU.mult), f"on{t}")
                def onT0(i):
                    SA.wait(e, "onT", i)
                    VA.done(e.tensor_copy(onT[:, 0, :], PS[:, 2, :]), "onT0")
                    VA.done(e.tensor_tensor(ya[:, :, :], X[:, bass.ds(i * TB, TB), :], bo[:, :].unsqueeze(1).broadcast_to((P, TB, D)), ALU.add), "xb")
                def residual(i):
                    xt = X[:, bass.ds(i * TB, TB), :]
                    VA.wait(e, "xb", i)
                    SA.wait(e, "wo", i)
                    VA.done(e.tensor_tensor(ya[:, :, :], self.pair_banks(0), ya[:, :, :], ALU.add), "a")
                    VA.wait(e, "a", i)
                    VA.done(e.tensor_tensor(xt, xt, ya[:, :, :], ALU.add), "xa")
                    self.norm_stats(e, VA, i, lambda t: ya[:, t, :], st, mv)
                def norm(i):
                    self.row_norm_affine(e, VA, AA, i, ya, h2, mv, sd, rstd, g2, b2, "h2")
                def h2_parts(i):
                    SB.wait(e, "h2T", i)
                    VB.done(e.tensor_copy(h2T[:, 0, :], PS[:, 4, :]), "h2T0")
                    AB.wait(e, "h2T1", i)
                    VB.wait(e, "h2T0", i)
                    hi, lo = (t[:, :, bass.ds(i * BLK, BLK)] for t in self.h2)
                    VB.done(e.tensor_copy(hi, h2T[:, :, :]), "hi")
                    VB.wait(e, "hi", i)
                    VB.done(e.tensor_tensor(lo, h2T[:, :, :], hi.bitcast(F32), ALU.subtract), "lo")
                def best_two(i):
                    SB.wait(e, "lg", i)
                    VB.done(e.tensor_tensor(lg[:, :, :], PS[:, 6, 0:TB * E].rearrange("p (t n) -> p t n", n=E),
                                            br[:, :].unsqueeze(1).broadcast_to((P, TB, E)), ALU.add), "lg")
                    VB.wait_apart(e, "lg", i, self.apart)
                    for t in range(TB):
                        last = e.max(best[:, t, :], lg[:, t, :])
                    VB.done(last, "best")
                    VB.wait(e, "best", i)
                    VB.done(e.tensor_tensor(keep[:, :, :], lg[:, :, :], bc(best[:, :, 1], E), ALU.is_ge), "keep")
                    VB.wait(e, "keep", i)
                    VB.done(e.tensor_tensor(lg[:, :, :], lg[:, :, :], bc(best[:, :, 0], E), ALU.subtract), "sh")
                def weights(i):
                    AB.wait(e, "ex", i)
                    VB.done(e.tensor_tensor(ex[:, :, :], ex[:, :, :], keep[:, :, :], ALU.mult), "w_")
                    VB.wait(e, "w_", i)
                    VB.done(e.tensor_reduce(ws[:, :], ex[:, :, :], AX.X, ALU.add), "ws")
                    VB.wait(e, "ws", i)
                    VB.done(e.reciprocal(ws[:, :], ws[:, :]), "wr")
                    VB.wait(e, "wr", i)
                    e.tensor_tensor(self.w_all[:, bass.ds(i * TB, TB), :], ex[:, :, :], bc(ws[:, :], E), ALU.mult)
                    VB.done(e.tensor_tensor(ex[:, :, :], ex[:, :, :], bc(ws[:, :], E), ALU.mult), "w")
                def add_biases(i):
                    xt = X[:, bass.ds(i * TB, TB), :]
                    SB.wait(e, "b2", i)
                    VB.done(e.tensor_tensor(xt, self.pair_banks(4), xt, ALU.add), "x")
                divide(0)
                onT0(0)
                residual(0)
                norm(0)
                with e.Fori(0, NB - 1) as i:
                    h2_parts(i)
                    divide(i + 1)
                    best_two(i)
                    onT0(i + 1)
                    weights(i)
                    residual(i + 1)
                    add_biases(i)
                    norm(i + 1)
                h2_parts(NB - 1)
                best_two(NB - 1)
                weights(NB - 1)
                add_biases(NB - 1)

    def expert_buffers(self, c):
        sb = lambda n, s, dt=F32: self.sb(c, n, s, dt)
        self.h2 = [sb(f"x_h2{n}", [P, KD, N], F32R) for n in range(2)]
        self.w1 = [[sb(f"x_w1{p}{n}", [P, KD, FF], F32R) for n in range(2)] for p in range(2)]
        self.w2 = [[sb(f"x_w2{p}{n}", [P, NF, D], F32R) for n in range(2)] for p in range(2)]
        self.raw1, self.raw2 = sb("x_raw1", [P, KD, FF]), sb("x_raw2", [P, NF, D])
        self.s_w1, self.s_w2 = self.sem("x_w1"), self.sem("x_w2")
        names = [f"{w}{part}{p}" for p in range(2) for w in ("w1", "w2") for part in ("hi", "lo")]
        self.W = self.steps("x_pool", names, [n + "-" for n in names])

    def load_w1(self, e, n):
        e.dma_start(self.raw1[:, :, :], self.a["L0_ffn_e_w1"].rearrange("e (k p) n -> e p k n", p=P)[n]).then_inc(self.s_w1, 16)

    def load_w2(self, e, n):
        e.dma_start(self.raw2[:, :, :], self.a["L0_ffn_e_w2"].rearrange("e (k p) n -> e p k n", p=P)[n]).then_inc(self.s_w2, 16)

    def load_weights(self, e, n):
        self.load_w1(e, n)
        self.load_w2(e, n)

    def split_weights(self, e, p, tag, i, n):
        for raw, w, name, s in ((self.raw1, self.w1, "w1", self.s_w1), (self.raw2, self.w2, "w2", self.s_w2)):
            e.wait_ge(s, 16 * (n + 1))
            e.sem_inc(self.apart, 1)
            self.W.done(e.tensor_copy(w[p][0][:, :, :], raw[:, :, :]), f"{name}hi{p}{tag}")
            self.W.wait(e, f"{name}hi{p}{tag}", i)
            self.W.done(e.tensor_tensor(w[p][1][:, :, :], raw[:, :, :], w[p][0][:, :, :].bitcast(F32), ALU.subtract), f"{name}lo{p}{tag}")

    def experts(self, c):
        nc, a, PS, X = self.nc, self.a, self.PS, self.X
        sb = lambda n, s, dt=F32: self.sb(c, n, s, dt)
        h2, w1, w2, W = self.h2, self.w1, self.w2, self.W
        b1r, b1 = sb("x_b1r", [E * NF, P]), sb("x_b1", [P, E, NF])
        g = [sb(f"x_g{r}", [P, BLK]) for r in range(2)]
        mid = [sb(f"x_mid{n}", [P, NF, BLK], F32R) for n in range(2)]
        st, mv, sd, rstd = sb("x_st", [P, NT, 6]), sb("x_mv", [P, NT, 2]), sb("x_sd", [P, NT]), sb("x_rstd", [P, NT])
        PASSES = ((0, 0), (0, 1), (1, 0))
        s_b, s_out = self.sem("x_b"), self.sem("x_out")
        fs = range(NF)
        S = self.steps("x_pe", [f"m{f}" for f in fs] + ["out"], ["b1"])
        A = self.steps("x_act", [f"g{f}" for f in fs], ["b1"])
        A2 = self.steps("x_act2", ["sd"])
        V = self.steps("x_dve", [n for f in fs for n in (f"hi{f}", f"lo{f}")] + [f"x{t}" for t in range(TB)])
        V2 = self.steps("x_dve2", [f"stats{k}" for k in range(NB)] + ["mv", "rstd"] + [f"out{k}" for k in range(NB)])
        s_free = [self.sem(f"x_free{p}") for p in range(2)]
        with nc.Block() as block:
            @block.sync
            def _(e):
                e.dma_start(b1r[:, :], a["L0_ffn_e_b1"].rearrange("e (f p) -> (e f) p", p=P)).then_inc(s_b, 16)
                with e.Fori(0, E // 2 - 1) as i:
                    for p in range(2):
                        for name, load in (("w1lo", self.load_w1), ("w2lo", self.load_w2)):
                            W.wait(e, f"{name}{1 - p}", i if p else i - 1)
                            load(e, i * 2 + p + 2)
                dst = self.out.rearrange("b (t p) d -> p (b t) d", p=P)
                for k in range(NB):
                    V2.wait(e, f"out{k}")
                    e.dma_start(dst[:, k * TB:(k + 1) * TB, :], X[:, k * TB:(k + 1) * TB, :]).then_inc(s_out, 16)
                e.wait_ge(s_out, 16 * NB)
            @block.gpsimd
            def _(e):
                with e.Fori(0, E // 2 - 1) as i:
                    for p in range(2):
                        e.wait_ge(s_free[p], i + 1)
                        self.split_weights(e, p, "", i, i * 2 + p + 2)
            @block.tensor
            def _(e):
                S.start(e)
                e.wait_ge(s_b, 16)
                S.done(e.transpose(PS[:, 0, 0:E * NF], b1r[:, :], self.ident[0:E * NF, 0:E * NF]), "b1")
                A.wait(e, "b1")
                with e.Fori(0, E // 2) as i:
                    for p in range(2):
                        with e.Fori(0, NB) as k:
                            it = (i * 2 + p) * NB + k
                            W.wait(e, f"w1lo{p}", i - 1)
                            for f in fs:
                                if f >= 4:
                                    A.wait(e, f"g{f - 4}", it)
                                else:
                                    A.wait_before(e, it)
                                for n, (u, v) in enumerate(PASSES):
                                    for kt in range(KD):
                                        last = e.matmul(PS[:, f % 4, :], w1[p][u][:, kt, f * P:(f + 1) * P], h2[v][:, kt, bass.ds(k * BLK, BLK)],
                                                        start=n == 0 and kt == 0, stop=n == 2 and kt == KD - 1)
                                S.done(last, f"m{f}")
                            W.wait(e, f"w2lo{p}", i - 1)
                            V.wait_before(e, it)
                            for f in fs:
                                V.wait(e, f"lo{f}", it)
                                for t in range(TB):
                                    for n, (u, v) in enumerate(PASSES):
                                        last = e.matmul(PS[:, 4 + t, 0:D], mid[u][:, f, t * P:(t + 1) * P], w2[p][v][:, f, :],
                                                        start=f == 0 and n == 0, stop=f == NF - 1 and n == 2)
                            S.done(last, "out")
                        S.wait_before(e, (i * 2 + p + 1) * NB)
                        e.sem_inc(s_free[p], 1)
            @block.scalar
            def _(e):
                A.start(e)
                A2.start(e)
                S.wait(e, "b1")
                A.done(e.activation(b1[:, :, :].rearrange("p e f -> p (e f)"), PS[:, 0, 0:E * NF], ACT.Copy), "b1")
                A.wait(e, "b1")
                with e.Fori(0, E) as n:
                    with e.Fori(0, NB) as k:
                        it = n * NB + k
                        for f in fs:
                            S.wait(e, f"m{f}", it)
                            if f >= 2:
                                V.wait(e, f"lo{f - 2}", it)
                            else:
                                V.wait_before(e, it)
                            A.done(e.activation(g[f % 2][:, :], PS[:, f % 4, :], ACT.Gelu, bias=b1[:, n, f:f + 1]), f"g{f}")
                V2.wait(e, "mv")
                A2.done(e.activation(sd[:, :], mv[:, :, 1], ACT.Sqrt, bias=self.eps[:, 0:1]), "sd")
            @block.vector
            def _(e):
                V.start(e)
                V2.start(e)
                with e.Fori(0, E) as n:
                    with e.Fori(0, NB) as k:
                        it = n * NB + k
                        for f in fs:
                            A.wait(e, f"g{f}", it)
                            if f == 0:
                                S.wait_before(e, it)
                            V.done(e.tensor_copy(mid[0][:, f, :], g[f % 2][:, :]), f"hi{f}")
                            V.wait(e, f"hi{f}", it)
                            V.done(e.tensor_tensor(mid[1][:, f, :], g[f % 2][:, :], mid[0][:, f, :].bitcast(F32), ALU.subtract), f"lo{f}")
                        S.wait(e, "out", it)
                        for t in range(TB):
                            xt = X[:, k * TB + t, :]
                            V.done(e.scalar_tensor_tensor(out=xt, in0=PS[:, 4 + t, 0:D], scalar=self.w_all[:, k * TB + t, bass.ds(n, 1)],
                                                          in1=xt, op0=ALU.mult, op1=ALU.add), f"x{t}")
                V.wait_before(e, E * NB)
                for k in range(NB):
                    tiles = range(k * TB, (k + 1) * TB)
                    for t in tiles:
                        last = e.bn_stats(st[:, t, :], X[:, t, :])
                    V2.done(last, f"stats{k}")
                for k in range(NB):
                    V2.wait(e, f"stats{k}")
                    for t in range(k * TB, (k + 1) * TB):
                        last = e.bn_aggr(mv[:, t, :], st[:, t, :])
                V2.done(last, "mv")
                self.norm_rstd(e, V2, A2, 0, sd, rstd)
                for k in range(NB):
                    for t in range(k * TB, (k + 1) * TB):
                        last = e.tensor_scalar(X[:, t, :], X[:, t, :], mv[:, t, 0:1], rstd[:, t:t + 1], ALU.subtract, ALU.mult)
                    V2.done(last, f"out{k}")


def kernel(**inputs):
    import concourse.bacc as bacc
    import numpy as np
    from concourse.bass_utils import run_bass_kernel_spmd

    nc = bacc.Bacc("TRN2", target_bir_lowering=False, num_devices=1)
    arrays, aps = {}, {}
    for name, value in inputs.items():
        array = np.ascontiguousarray(value)
        arrays[name] = array
        aps[name] = nc.dram_tensor(name, array.shape, mybir.dt.from_np(array.dtype), kind="ExternalInput").ap()
    out = nc.dram_tensor("out", (B, T, D), F32, kind="ExternalOutput").ap()
    Kernel(nc, aps, out).build()
    results = run_bass_kernel_spmd(nc, [arrays], core_ids=[0])
    return results.results[0]["out"]
```
